# Optimizing a Trainium2 kernel written in Bass

```python
import numpy as np
import jax
import jax.numpy as jnp

def _softmax(x, axis=-1):
    return jax.nn.softmax(x, axis=axis)

def _gelu(x):
    return jax.nn.gelu(x, approximate=True)

def _silu(x):
    return jax.nn.silu(x)

def _sigmoid(x):
    return jax.nn.sigmoid(x)

def _layernorm(x, axis=-1, eps=1e-05):
    m = jnp.mean(x, axis=axis, keepdims=True)
    v = jnp.var(x, axis=axis, keepdims=True)
    return (x - m) / jnp.sqrt(v + eps)

def _scatter_add(tgt, idx, src, axis=0):
    return tgt.at[idx].add(src)

def _segment_sum(src, seg, n):
    return jax.ops.segment_sum(src, seg, n)
kernel_name = 'mk_lm_tower_d1_tok_ids1024_r4_ae4df2'

def setup_inputs(seed: int=0):
    np.random.seed(seed)
    _w = jnp.asarray

    def _rec_inputs():
        import jax
        import jax.numpy as jnp
        _rk = jax.random.key(seed)
        x = jax.random.randint(jax.random.fold_in(_rk, 1), (8, 256), 0, 50257, jnp.int32)
        return x
    x = _rec_inputs()

    def _L0_tok_setup():
        import jax, jax.numpy as jnp
        import numpy as np
        TIER_BITS = [16, 8, 6, 4]

        def quantize_ste(x, bits):
            if bits >= 16:
                return x
            max_val = float(2 ** (bits - 1) - 1)
            scale = jnp.maximum(jnp.max(jnp.abs(x)), 1e-08) / max_val
            x_q = jnp.clip(jnp.round(x / scale), -max_val, max_val) * scale
            return x + jax.lax.stop_gradient(x_q - x)
        key = jax.random.key(seed)
        ks = jax.random.split(key, 6)
        dim = 256
        sizes = [64, 512 - 64, 4096 - 512, 50257 - 4096]
        tws = [jax.random.normal(ks[i], (sizes[i], dim), dtype=jnp.float32) * 0.02 for i in range(4)]
        input_ids = jax.random.randint(ks[4], (8, 512), 0, 50257, dtype=jnp.int64)
        return {'input_ids': input_ids, 'tw0': tws[0], 'tw1': tws[1], 'tw2': tws[2], 'tw3': tws[3], 'ts0': jnp.ones((1, dim), jnp.float32) * 0.1, 'ts1': jnp.ones((1, dim), jnp.float32) * 0.1, 'ts2': jnp.ones((1, dim), jnp.float32) * 0.1, 'ts3': jnp.ones((1, dim), jnp.float32) * 0.1}
    _L0_tok_all = _L0_tok_setup()
    _L0_tok_in = {k: v for k, v in _L0_tok_all.items() if k in ('tw0', 'tw1', 'tw2', 'tw3', 'ts0', 'ts1', 'ts2', 'ts3')}
    del _L0_tok_all

    def _L0_attn_setup():
        import jax, jax.numpy as jnp
        import numpy as np
        import math
        B, S, HID, H = (2, 512, 256, 16)
        D = HID // H

        def _get_slopes(n):
            start = 2 ** (-2 ** (-(math.log2(n) - 3)))
            return np.array([start * 2 ** (-i) for i in range(n)], dtype=np.float32)
        key = jax.random.key(seed)
        ks = jax.random.split(key, 9)
        sc = 1.0 / math.sqrt(HID)
        return {'x': jax.random.normal(ks[0], (B, S, HID), dtype=jnp.float32), 'Wq': jax.random.normal(ks[1], (HID, HID), dtype=jnp.float32) * sc, 'bq': jnp.zeros((HID,), dtype=jnp.float32), 'Wk': jax.random.normal(ks[2], (HID, HID), dtype=jnp.float32) * sc, 'bk': jnp.zeros((HID,), dtype=jnp.float32), 'Wv': jax.random.normal(ks[3], (HID, HID), dtype=jnp.float32) * sc, 'bv': jnp.zeros((HID,), dtype=jnp.float32), 'Wo': jax.random.normal(ks[4], (HID, HID), dtype=jnp.float32) * sc, 'bo': jnp.zeros((HID,), dtype=jnp.float32), 'slopes': jnp.asarray(_get_slopes(H))}
    _L0_attn_all = _L0_attn_setup()
    _L0_attn_in = {k: v for k, v in _L0_attn_all.items() if k in ('Wq', 'bq', 'Wk', 'bk', 'Wv', 'bv', 'Wo', 'bo', 'slopes')}
    del _L0_attn_all

    def _L0_ffn_setup():
        import jax, jax.numpy as jnp
        import numpy as np
        from jax import lax
        HIDDEN = 256
        INTER = 128
        E = 64
        K = 6
        G = 8
        TG = 4
        NSH = 2
        ISH = INTER * NSH

        def _moe_forward(hidden_states, gate_w, gate_bias, eg_w, eu_w, ed_w, sg_w, su_w, sd_w):
            B, S, H = hidden_states.shape
            x = hidden_states.reshape(-1, H)
            T = x.shape[0]
            shared = jax.nn.silu(x @ sg_w.T) * (x @ su_w.T) @ sd_w.T
            logits = x @ gate_w.T
            scores = jax.nn.sigmoid(logits) + gate_bias
            group_scores = scores.reshape(T, G, E // G).max(axis=-1)
            _, sel_groups = lax.top_k(group_scores, TG)
            group_mask = jnp.zeros((T, G), scores.dtype).at[jnp.arange(T)[:, None], sel_groups].set(1.0)
            mask = jnp.repeat(group_mask, E // G, axis=1)
            masked_scores = scores * mask
            topk_w, topk_i = lax.top_k(masked_scores, K)
            topk_w = topk_w / (topk_w.sum(axis=-1, keepdims=True) + 1e-08)
            comb = jnp.zeros((T, E), x.dtype).at[jnp.arange(T)[:, None], topk_i].add(topk_w)
            h = jax.nn.silu(jnp.einsum('th,eih->eti', x, eg_w)) * jnp.einsum('th,eih->eti', x, eu_w)
            routed = jnp.einsum('eti,ehi,te->th', h, ed_w, comb)
            return (shared + routed).reshape(B, S, H)
        key = jax.random.key(seed)
        ks = jax.random.split(key, 9)
        s = 0.02
        return {'hidden_states': jax.random.normal(ks[0], (1, 256, HIDDEN), jnp.float32), 'gate_w': jax.random.normal(ks[1], (E, HIDDEN), jnp.float32) * s, 'gate_bias': jnp.zeros((E,), jnp.float32), 'eg_w': jax.random.normal(ks[2], (E, INTER, HIDDEN), jnp.float32) * s, 'eu_w': jax.random.normal(ks[3], (E, INTER, HIDDEN), jnp.float32) * s, 'ed_w': jax.random.normal(ks[4], (E, HIDDEN, INTER), jnp.float32) * s, 'sg_w': jax.random.normal(ks[5], (ISH, HIDDEN), jnp.float32) * s, 'su_w': jax.random.normal(ks[6], (ISH, HIDDEN), jnp.float32) * s, 'sd_w': jax.random.normal(ks[7], (HIDDEN, ISH), jnp.float32) * s}
    _L0_ffn_all = _L0_ffn_setup()
    _L0_ffn_in = {k: v for k, v in _L0_ffn_all.items() if k in ('gate_w', 'gate_bias', 'eg_w', 'eu_w', 'ed_w', 'sg_w', 'su_w', 'sd_w')}
    del _L0_ffn_all
    return {'x': x, 'L0_tok_tw0': _L0_tok_in['tw0'], 'L0_tok_tw1': _L0_tok_in['tw1'], 'L0_tok_tw2': _L0_tok_in['tw2'], 'L0_tok_tw3': _L0_tok_in['tw3'], 'L0_tok_ts0': _L0_tok_in['ts0'], 'L0_tok_ts1': _L0_tok_in['ts1'], 'L0_tok_ts2': _L0_tok_in['ts2'], 'L0_tok_ts3': _L0_tok_in['ts3'], 'L0_attn_Wq': _L0_attn_in['Wq'], 'L0_attn_bq': _L0_attn_in['bq'], 'L0_attn_Wk': _L0_attn_in['Wk'], 'L0_attn_bk': _L0_attn_in['bk'], 'L0_attn_Wv': _L0_attn_in['Wv'], 'L0_attn_bv': _L0_attn_in['bv'], 'L0_attn_Wo': _L0_attn_in['Wo'], 'L0_attn_bo': _L0_attn_in['bo'], 'L0_attn_slopes': _L0_attn_in['slopes'], 'L0_ffn_gate_w': _L0_ffn_in['gate_w'], 'L0_ffn_gate_bias': _L0_ffn_in['gate_bias'], 'L0_ffn_eg_w': _L0_ffn_in['eg_w'], 'L0_ffn_eu_w': _L0_ffn_in['eu_w'], 'L0_ffn_ed_w': _L0_ffn_in['ed_w'], 'L0_ffn_sg_w': _L0_ffn_in['sg_w'], 'L0_ffn_su_w': _L0_ffn_in['su_w'], 'L0_ffn_sd_w': _L0_ffn_in['sd_w']}

def reference(x, L0_tok_tw0, L0_tok_tw1, L0_tok_tw2, L0_tok_tw3, L0_tok_ts0, L0_tok_ts1, L0_tok_ts2, L0_tok_ts3, L0_attn_Wq, L0_attn_bq, L0_attn_Wk, L0_attn_bk, L0_attn_Wv, L0_attn_bv, L0_attn_Wo, L0_attn_bo, L0_attn_slopes, L0_ffn_gate_w, L0_ffn_gate_bias, L0_ffn_eg_w, L0_ffn_eu_w, L0_ffn_ed_w, L0_ffn_sg_w, L0_ffn_su_w, L0_ffn_sd_w):
    import jax
    import jax.numpy as jnp

    def _L0_tok_ref(input_ids, tw0, tw1, tw2, tw3, ts0, ts1, ts2, ts3):
        import jax, jax.numpy as jnp
        import numpy as np
        TIER_BITS = [16, 8, 6, 4]

        def quantize_ste(x, bits):
            if bits >= 16:
                return x
            max_val = float(2 ** (bits - 1) - 1)
            scale = jnp.maximum(jnp.max(jnp.abs(x)), 1e-08) / max_val
            x_q = jnp.clip(jnp.round(x / scale), -max_val, max_val) * scale
            return x + jax.lax.stop_gradient(x_q - x)
        tws = [tw0, tw1, tw2, tw3]
        tss = [ts0, ts1, ts2, ts3]
        table = jnp.concatenate([quantize_ste(tws[i] * tss[i], TIER_BITS[i]) for i in range(4)], axis=0)
        return jnp.take(table, input_ids, axis=0)

    def _L0_attn_ref(x, Wq, bq, Wk, bk, Wv, bv, Wo, bo, slopes):
        import jax, jax.numpy as jnp
        import numpy as np
        import math
        B, S, HID, H = (2, 512, 256, 16)
        D = HID // H

        def _get_slopes(n):
            start = 2 ** (-2 ** (-(math.log2(n) - 3)))
            return np.array([start * 2 ** (-i) for i in range(n)], dtype=np.float32)
        b, s, hid = x.shape
        h = slopes.shape[0]
        d = hid // h
        q = (x @ Wq.T + bq).reshape(b, s, h, d).transpose(0, 2, 1, 3)
        k = (x @ Wk.T + bk).reshape(b, s, h, d).transpose(0, 2, 1, 3)
        v = (x @ Wv.T + bv).reshape(b, s, h, d).transpose(0, 2, 1, 3)
        scores = jnp.einsum('bhqd,bhkd->bhqk', q, k) / jnp.sqrt(jnp.float32(d))
        pos = jnp.arange(s)
        dist = (pos[None, :] - pos[:, None]).astype(x.dtype)
        scores = scores + slopes[None, :, None, None] * dist[None, None]
        attn = jax.nn.softmax(scores, axis=-1)
        ctx = jnp.einsum('bhqk,bhkd->bhqd', attn, v)
        ctx = ctx.transpose(0, 2, 1, 3).reshape(b, s, hid)
        return ctx @ Wo.T + bo

    def _L0_ffn_ref(hidden_states, gate_w, gate_bias, eg_w, eu_w, ed_w, sg_w, su_w, sd_w):
        import jax, jax.numpy as jnp
        import numpy as np
        from jax import lax
        HIDDEN = 256
        INTER = 128
        E = 64
        K = 6
        G = 8
        TG = 4
        NSH = 2
        ISH = INTER * NSH

        def _moe_forward(hidden_states, gate_w, gate_bias, eg_w, eu_w, ed_w, sg_w, su_w, sd_w):
            B, S, H = hidden_states.shape
            x = hidden_states.reshape(-1, H)
            T = x.shape[0]
            shared = jax.nn.silu(x @ sg_w.T) * (x @ su_w.T) @ sd_w.T
            logits = x @ gate_w.T
            scores = jax.nn.sigmoid(logits) + gate_bias
            group_scores = scores.reshape(T, G, E // G).max(axis=-1)
            _, sel_groups = lax.top_k(group_scores, TG)
            group_mask = jnp.zeros((T, G), scores.dtype).at[jnp.arange(T)[:, None], sel_groups].set(1.0)
            mask = jnp.repeat(group_mask, E // G, axis=1)
            masked_scores = scores * mask
            topk_w, topk_i = lax.top_k(masked_scores, K)
            topk_w = topk_w / (topk_w.sum(axis=-1, keepdims=True) + 1e-08)
            comb = jnp.zeros((T, E), x.dtype).at[jnp.arange(T)[:, None], topk_i].add(topk_w)
            h = jax.nn.silu(jnp.einsum('th,eih->eti', x, eg_w)) * jnp.einsum('th,eih->eti', x, eu_w)
            routed = jnp.einsum('eti,ehi,te->th', h, ed_w, comb)
            return (shared + routed).reshape(B, S, H)
        return _moe_forward(hidden_states, gate_w, gate_bias, eg_w, eu_w, ed_w, sg_w, su_w, sd_w)
    h = _L0_tok_ref(x, L0_tok_tw0, L0_tok_tw1, L0_tok_tw2, L0_tok_tw3, L0_tok_ts0, L0_tok_ts1, L0_tok_ts2, L0_tok_ts3)
    h = h + _L0_attn_ref(_layernorm(h, axis=-1), L0_attn_Wq, L0_attn_bq, L0_attn_Wk, L0_attn_bk, L0_attn_Wv, L0_attn_bv, L0_attn_Wo, L0_attn_bo, L0_attn_slopes)
    h = h + _L0_ffn_ref(_layernorm(h, axis=-1), L0_ffn_gate_w, L0_ffn_gate_bias, L0_ffn_eg_w, L0_ffn_eu_w, L0_ffn_ed_w, L0_ffn_sg_w, L0_ffn_su_w, L0_ffn_sd_w)
    return h

_drawn_inputs = setup_inputs


def setup_inputs(seed=0):
    import zlib

    import numpy as np

    out = dict(_drawn_inputs(seed))
    spreads = {'L0_tok_ts0': (0.10000000149011612, 0.6),
     'L0_tok_ts1': (0.10000000149011612, 0.6),
     'L0_tok_ts2': (0.10000000149011612, 0.2),
     'L0_tok_ts3': (0.10000000149011612, 0.2),
     'L0_attn_bq': (0.0, 0.294),
     'L0_attn_bk': (0.0, 2.0),
     'L0_attn_bv': (0.0, 0.1),
     'L0_attn_bo': (0.0, 0.1),
     'L0_ffn_gate_bias': (0.0, 2.0)}
    factors = {'L0_tok_tw0': 72.438, 'L0_ffn_gate_w': 11.315}
    for name, (base, spread) in spreads.items():
        noise = np.random.default_rng([zlib.crc32(name.encode()), seed]).standard_normal(out[name].shape)
        drawn = base * np.exp(spread * noise) if base else spread * noise
        out[name] = jnp.asarray(drawn.astype(out[name].dtype))
    for name, factor in factors.items():
        out[name] = (out[name] * factor).astype(out[name].dtype)
    return out
```

```python
from contextlib import ExitStack

import numpy as np

import concourse.bass as bass
from concourse import mybir

F32, BF16, I32, U32 = mybir.dt.float32, mybir.dt.bfloat16, mybir.dt.int32, mybir.dt.uint32
ALU = mybir.AluOpType
ACT = mybir.ActivationFunctionType
AX_X = mybir.AxisListType.X
RMAX = bass.bass_isa.ReduceOp.max

P = 128
B, S, D, H, HD = 8, 256, 256, 16, 16
T = B * S
NT = T // P
QT = S // P
KC = D // P
E, INTER, TOPK, G, TG = 64, 128, 6, 8, 4
ISH = 256
EPS = 1e-5
TIERS = (64, 512, 4096, 50257)
MAXQ = (127.0, 31.0, 7.0)
ROUND = 12582912.0

SPLIT = 6 * HD
ROWS_B = SPLIT + 6
ROWS_C = ROWS_B + 3
Q_PARTS = (0, 0, 0, 1, 1, 2)
K_PARTS = (0, 1, 2, 0, 1, 0)

SCAN_ROWS = 15
SCAN_RING = 6
N3 = (TIERS[3] - TIERS[2]) // P
REST3 = TIERS[3] - TIERS[2] - N3 * P
CHUNKS = N3 // SCAN_ROWS
assert CHUNKS * SCAN_ROWS == N3 and CHUNKS % SCAN_RING == 0

ROW = 272
TOKCOL, SLOTCOL, WCOL = 256, 257, 263
CAP = T + P
TILES = E + (T * TOPK - E) // P + 1
RING = 8
TILES = -(-TILES // RING) * RING
NACC = 4
MG = 4
LAG = 8
RACC = T + P
LINKS_A, LINKS_D, LINKS_R = 4 * QT + 3, 4, 25
HEAD0 = 2
T1P = (TIERS[1] - TIERS[0]) // 4
MBANK = (1, 0, 0, 1)
NLOADS = 14
WROW = 3 * D


def tower(nc, ids, table, ts, wqk, wv, wo, bqk, bv, bo, slopes, gate, gbias, experts, sgu, sdown, out):
    with ExitStack() as ctx:
        def sb(name, shape, dt=F32):
            return ctx.enter_context(nc.sbuf_tensor(name, shape, dt))

        def ps(name, shape, dt=F32):
            return ctx.enter_context(nc.psum_tensor(name, shape, dt))

        def sem(name):
            return ctx.enter_context(nc.semaphore(name))

        qk_scr = nc.dram_tensor("qk_scr", [2, 3, 2, D, S], BF16).ap()
        rows_scr = nc.dram_tensor("rows_scr", [6, H * S], BF16).ap()
        max_scr = nc.dram_tensor("max_scr", [2, 3, H * S], BF16).ap()
        xT_scr = nc.dram_tensor("xT_scr", [B, P, KC * S], F32).ap()
        xs = nc.dram_tensor("xs", [E * CAP, ROW], F32).ap()
        acc_scr = [nc.dram_tensor(f"acc_scr{i}", [RACC, D], F32).ap() for i in range(NACC)]
        tile_scr = nc.dram_tensor("tile_scr", [2, P], F32).ap()

        ident = sb("ident", [P, P])
        before = sb("before", [P, P], BF16)
        ones = sb("ones", [P, P], BF16)
        zeros = sb("zeros", [P, RACC * D // P // 4])
        padrow = sb("padrow", [P, ROW])
        part_i = sb("part_i", [P, 2], I32)
        part_f = sb("part_f", [P, 3])
        tok_u = sb("tok_u", [P, NT], I32)
        eidx = sb("eidx", [P, E])
        ebase = sb("ebase", [P, E])
        iota_i = sb("iota_i", [P, S], I32)
        lower = sb("lower", [P, G, G])
        wqk_sb = sb("wqk_sb", [P, KC, 2 * D])
        wv_sb = sb("wv_sb", [P, KC, D])
        wo_sb = sb("wo_sb", [P, KC, D])
        gate_sb = sb("gate_sb", [P, KC, E])
        gbias_sb = sb("gbias_sb", [P, E])
        bqk_sb = sb("bqk_sb", [P, 4])
        bv_sb = sb("bv_sb", [P, D])
        bo_sb = sb("bo_sb", [P, D])
        tsb = sb("tsb", [P, 4, D])
        half = sb("half", [P, QT])
        sparts = sb("sparts", [H, 4], BF16)

        ids_sb = sb("ids_sb", [P, NT], I32)
        tier_u = sb("tier_u", [P, NT], U32)
        idf = sb("idf", [P, NT])
        ge = sb("ge", [P, 4, NT])
        intier = sb("intier", [P, 3, NT])
        maxq = sb("maxq", [P, NT])
        nmaxq = sb("nmaxq", [P, NT])
        scale = sb("scale", [P, NT])
        inv = sb("inv", [P, NT])
        emb = sb("emb", [P, NT, D])
        tsel = sb("tsel", [P, NT, D])
        ring = sb("ring", [P, SCAN_RING, SCAN_ROWS, D])
        flat = ring[:, :, :, :].rearrange("p a b d -> p (a b d)")
        taken = [0]

        def carve(n):
            taken[0] += n
            assert taken[0] <= SCAN_RING * SCAN_ROWS * D
            return flat[:, taken[0] - n:taken[0]]

        cmax = sb("cmax", [P, 3, D])
        cnew = sb("cnew", [P, D])
        pmax = sb("pmax", [P, 4])
        amax = sb("amax", [P, 4])
        sc3 = sb("sc3", [P, 4])

        xq = carve(QT * D).rearrange("p (t d) -> p t d", t=QT)
        stats = sb("stats", [P, QT, 6])
        mv = sb("mv", [P, QT, 2])
        mv_eps = sb("mv_eps", [P, QT])
        rstd = sb("rstd", [P, QT])
        xn = carve(QT * D).rearrange("p (t d) -> p t d", t=QT)
        xT = sb("xT", [P, KC, S])
        qk32 = carve(4 * S).rearrange("p (m s) -> p m s", m=4)
        qkr = carve(4 * S).rearrange("p (m s) -> p m s", m=4)
        parts = sb("parts", [P, 3, 4, S], BF16)
        at = taken[0]
        Qs = [carve(H * S // 2).bitcast(BF16).rearrange("p (h s) -> p h s", h=H) for _ in range(2)]
        Ks = [carve(H * S // 2).bitcast(BF16).rearrange("p (h s) -> p h s", h=H) for _ in range(2)]
        fin = [flat[:, at + i * NACC * 4 * D:at + (i + 1) * NACC * 4 * D].rearrange("p (a n d) -> p a n d", a=NACC, n=4)
               for i in range(2)]
        V = [sb(f"V{i}", [P, QT, H, HD + 1]) for i in range(2)]
        slope_in = sb("slope_in", [H, 4])
        pos_f = sb("pos_f", [H, S])
        onesrow = sb("onesrow", [H, S])
        slope_p = sb("slope_p", [H, 3, S], BF16)
        pos_p = sb("pos_p", [H, 3, S], BF16)
        nmax = sb("nmax", [P, H, QT])
        m32 = sb("m32", [MG * QT, P])
        mparts = [sb(f"mparts{i}", [MG * QT, 3, P], BF16) for i in range(2)]
        PT = [sb(f"PT{i}", [P, QT, S]) for i in range(2)]
        rsum = sb("rsum", [P, QT, H])
        cn = carve(QT * D).rearrange("p (t d) -> p t d", t=QT)
        cT = sb("cT", [P, KC, S])

        stats2 = sb("stats2", [P, QT, 6])
        mv2 = sb("mv2", [P, QT, 2])
        mv2_eps = sb("mv2_eps", [P, QT])
        xo = carve(QT * D).rearrange("p (t d) -> p t d", t=QT)
        rstd2 = sb("rstd2", [P, QT])
        x2 = [sb(f"x2_{i}", [P, QT, ROW]) for i in range(2)]
        x2T = sb("x2T", [P, KC, S])
        esig = sb("esig", [P, QT, E])
        score = sb("score", [P, QT, E])
        gs = sb("gs", [P, QT, G])
        cmp_a = sb("cmp_a", [P, QT, G, G])
        cmp_b = sb("cmp_b", [P, QT, G, G])
        gmask = sb("gmask", [P, QT, G])
        ms = sb("ms", [P, QT, E])
        top = sb("top", [P, QT, 8])
        topi = sb("topi", [P, QT, 8], U32)
        lastf = sb("lastf", [P, QT])
        wsum = sb("wsum", [P, QT])
        tie = sb("tie", [P, QT, E])
        M = sb("M", [P, QT, E], BF16)
        wn = sb("wn", [P, QT, E])
        key = sb("key", [P, QT, E])
        topk = sb("topk", [P, QT, 8])
        eq = sb("eq", [P, QT, TOPK, E])
        run = sb("run", [P, E])
        slot_u = [sb(f"slot_u{i}", [P, QT, TOPK], U32) for i in range(2)]

        nt_e = sb("nt_e", [P, E])
        end_e = sb("end_e", [P, E])
        one_e = sb("one_e", [P, E])
        tsc = sb("tsc", [P, 2, E])
        tinfo = sb("tinfo", [P, 2, 6])
        padreg = sb("padreg", [P, E], I32)
        treg_f = sb("treg_f", [1, 2 * P])
        treg = sb("treg", [1, 2 * P], I32)
        tslot = sb("tslot", [P, 2 * P])
        sgu_sb = sb("sgu_sb", [P, KC, 2 * ISH])
        sdown_sb = sb("sdown_sb", [P, ISH // P, D])

        w_t = [flat[:, at + i * WROW:at + (i + 1) * WROW] for i in range(RING)]
        assert RING * WROW <= 2 * H * S
        x_t = [carve(ROW) for _ in range(RING)]
        y_t = [carve(D) for _ in range(RING)]
        xT_t = [carve(KC * P) for _ in range(2)]
        sg_t = [carve(P) for _ in range(2)]
        h_t = [carve(P) for _ in range(2)]
        wt_t = [carve(4) for _ in range(RING)]
        eq_t = [carve(8) for _ in range(RING)]
        sh_g = [carve(512) for _ in range(2)]
        sh_h = [carve(ISH // P * 512).rearrange("p (m t) -> p m t", m=ISH // P) for _ in range(2)]
        xT_all = tsel[:, :, :].rearrange("p n d -> p (n d)").rearrange("p (c t) -> p c t", c=KC)

        pS = [ps(f"pS{i}", [P, 512]) for i in range(2)]
        pT = [ps(f"pT{i}", [P, 512]) for i in range(2)]
        pC = ps("pC", [P, QT, 512])
        pF = [ps(f"pF{i}", [P, 512]) for i in range(2)]

        consts_p = sem("consts_p")
        consts_ok = sem("consts_ok")
        ids_in = sem("ids_in")
        w_in_sb = sem("w_in_sb")
        slope_in_s = sem("slope_in_s")
        emb_in = sem("emb_in")
        ts_in = sem("ts_in")
        tier_ok = sem("tier_ok")
        ring_in = [sem(f"ring_in{i}") for i in range(SCAN_RING)]
        ring_used = sem("ring_used")
        scan_v = sem("scan_v")
        pmax_ok = sem("pmax_ok")
        amax_ok = sem("amax_ok")
        bias_ok = sem("bias_ok")
        set_v = sem("set_v")
        rows_ok = sem("rows_ok")
        rows_out = sem("rows_out")
        rows_in = sem("rows_in")
        zero_out = sem("zero_out")

        chain_a, chain_d, chain_r, chain_m = sem("chain_a"), sem("chain_d"), sem("chain_r"), sem("chain_m")
        var_ok = sem("var_ok")
        rstd_ok = sem("rstd_ok")
        xn_ok = sem("xn_ok")
        xnT_ok = sem("xnT_ok")
        xT_ok = sem("xT_ok")
        qk_ok = sem("qk_ok")
        qk32_ok = sem("qk32_ok")
        chain_p = sem("chain_p")
        parts_ok = sem("parts_ok")
        qk_out = sem("qk_out")
        qk_in = sem("qk_in")
        v_ok = sem("v_ok")
        v_done = sem("v_done")
        s_ok = sem("s_ok")
        max_ok = sem("max_ok")
        mT_ok = sem("mT_ok")
        mparts_ok = sem("mparts_ok")
        max_out = sem("max_out")
        max_in = [sem(f"max_in{g}") for g in range(H // MG)]
        sT_ok = sem("sT_ok")
        exp_ok = sem("exp_ok")
        pv_ok = sem("pv_ok")
        cn_ok = sem("cn_ok")
        cnT_ok = sem("cnT_ok")
        cT_ok = sem("cT_ok")
        wo_ok = sem("wo_ok")
        res_ok = sem("res_ok")
        var2_ok = sem("var2_ok")
        rstd2_ok = sem("rstd2_ok")
        x2_ok = sem("x2_ok")
        x2T_ps = sem("x2T_ps")
        x2T_ok = sem("x2T_ok")
        logit_ok = sem("logit_ok")
        esig_ok = sem("esig_ok")
        sel_ok = sem("sel_ok")
        prefix_ok = sem("prefix_ok")
        slots_ok = sem("slots_ok")
        scat_ok = [sem(f"scat_ok{i}") for i in range(2)]

        chain_t = sem("chain_t")
        tinfo_ok = sem("tinfo_ok")
        tinfo_out = sem("tinfo_out")
        tinfo_in = sem("tinfo_in")
        padreg_ok = sem("padreg_ok")
        treg_ok = sem("treg_ok")
        tslot_ok = sem("tslot_ok")
        pad_out = sem("pad_out")
        sh_gu = sem("sh_gu")
        sh_silu = sem("sh_silu")
        sh_h_ok = sem("sh_h_ok")
        sh_y = sem("sh_y")
        sh_done = sem("sh_done")
        w_in = [sem(f"w_in{i}") for i in range(RING)]
        x_in = [sem(f"x_in{i}") for i in range(RING)]
        tT_ok = sem("tT_ok")
        tx_ok = sem("tx_ok")
        tw_ok = sem("tw_ok")
        tg_ok = sem("tg_ok")
        ts_ok = sem("ts_ok")
        th_ok = sem("th_ok")
        ty_ok = sem("ty_ok")
        te_ok = sem("te_ok")
        acc_ok = [sem(f"acc_ok{i}") for i in range(RING)]
        fin_in = [sem(f"fin_in{i}") for i in range(2)]
        fin_v = sem("fin_v")
        fin_ok = sem("fin_ok")
        out_done = sem("out_done")

        passed = {nc.sync: sem("passed_sp"), nc.gpsimd: sem("passed_pool"), nc.vector: sem("passed_dve")}
        block = ctx.enter_context(nc.Block())

        def apart(eng):
            eng.sem_inc(passed[eng], 1)

        def due(eng, s, value):
            if not isinstance(value, int) or value > 0:
                eng.wait_ge(s, value)

        class Chain:

            def __init__(self, eng, s, per):
                self.eng, self.s, self.per, self.base, self.n = eng, s, per, 0, 0

            def start(self, batch):
                assert self.n in (0, self.per), (self.n, self.per)
                self.base, self.n = batch * self.per, 0

            def link(self, ins):
                self.n += 1
                ins.then_inc(self.s, 1)
                self.eng.wait_ge(self.s, self.base + self.n)

        STEPS = B + 3
        LOOP = (3, B - 1)
        assert (LOOP[1] - LOOP[0]) % 2 == 0

        def stages(rep):
            return {k: 0 <= rep - lag < B for k, lag in (("A", 0), ("B", 1), ("D", 2), ("R", 3))}

        def c_head(s, rep, i):
            lag, h = (1, i - LAG) if i >= LAG else (2, i + H - LAG)
            return (s - lag, h) if 0 <= rep - lag < B else None

        def pipeline(eng, step):
            for s in range(LOOP[0]):
                step(s, s)
            with eng.Fori(LOOP[0], LOOP[1], 2) as s:
                step(s, LOOP[0])
                step(s + 1, LOOP[0] + 1)
            for s in range(LOOP[1], STEPS):
                step(s, s)

        def m_group(s, rep, i):
            if i % MG:
                return None
            lag, g = (1, i // MG - 1) if i else (2, H // MG - 1)
            return (s - lag, g) if 0 <= rep - lag < B else None

        NM = H // MG

        @block.sync
        def _(sp):
            sp.dma_start(ids_sb[:, :], ids).then_inc(ids_in, 16)

            def chunk(slot, src, parts, rows):
                sp.dma_start(ring[0:parts, slot, 0:rows, :], src).then_inc(ring_in[slot], 16)

            t2 = table[TIERS[1]:TIERS[2], :].rearrange("(p n) d -> p n d", p=P)
            half2 = t2.shape[1] // 2
            chunk(HEAD0, t2[:, 0:half2, :], P, half2)
            chunk(HEAD0 + 1, t2[:, half2:, :], P, half2)
            chunk(HEAD0 + 2, table[TIERS[0]:TIERS[1], :].rearrange("(p n) d -> p n d", n=4), T1P, 4)
            chunk(HEAD0 + 3, table[TIERS[3] - REST3:TIERS[3], :].rearrange("(p n) d -> p n d", n=1), REST3, 1)
            for dst, src in ((wqk_sb, wqk), (wv_sb, wv), (wo_sb, wo), (gate_sb, gate), (sgu_sb, sgu),
                             (sdown_sb, sdown)):
                sp.dma_start(dst[:, :, :], src).then_inc(w_in_sb, 16)
            sp.dma_start(bqk_sb[:, :], bqk).then_inc(w_in_sb, 16)
            for dst, src in ((bv_sb, bv), (bo_sb, bo), (gbias_sb, gbias)):
                sp.dma_start(dst[:, :], src.broadcast_to([P, src.shape[1]])).then_inc(w_in_sb, 16)
            for i in range(4):
                sp.dma_start(tsb[:, i, :], ts[i:i + 1, :].broadcast_to([P, D])).then_inc(w_in_sb, 16)
            sp.dma_start(slope_in[:, 0:1], slopes).then_inc(slope_in_s, 16)

            t3 = table[TIERS[2]:TIERS[3] - REST3, :].rearrange("(p n) d -> p n d", p=P)
            def turn(i):
                for j in range(SCAN_RING):
                    if not isinstance(i, int) or j >= HEAD0:
                        sp.wait_ge(ring_used, i * SCAN_RING + j + 1 - HEAD0)
                    chunk(j, t3[:, bass.ds((i * SCAN_RING + j) * SCAN_ROWS, SCAN_ROWS), :], P, SCAN_ROWS)

            turn(0)
            with sp.Fori(1, CHUNKS // SCAN_RING) as i:
                turn(i)

            sp.wait_ge(rows_ok, 2)
            sp.dma_start(rows_scr[0:3, :].rearrange("i (h s) -> h i s", h=H), slope_p[:, :, :]).then_inc(rows_out, 16)
            sp.dma_start(rows_scr[3:6, :].rearrange("i (h s) -> h i s", h=H), pos_p[:, :, :]).then_inc(rows_out, 16)
            sp.wait_ge(rows_out, 32)
            sp.wait_ge(pmax_ok, 1)
            for par in range(2):
                q_rows = Qs[par][:, :, :].rearrange("p h s -> p (h s)")
                k_rows = Ks[par][:, :, :].rearrange("p h s -> p (h s)")
                sp.dma_start(q_rows[SPLIT:SPLIT + 3, :], rows_scr[0:3, :]).then_inc(rows_in, 16)
                sp.dma_start(k_rows[SPLIT + 3:SPLIT + 6, :], rows_scr[0:3, :]).then_inc(rows_in, 16)
                for i in range(3):
                    for dst, row, src in ((q_rows, SPLIT + 3 + i, 3), (k_rows, SPLIT + i, 4),
                                          (k_rows, ROWS_B + i, 5)):
                        sp.dma_start(dst[row:row + 1, :], rows_scr[src:src + 1, :]).then_inc(rows_in, 16)
            sp.wait_ge(consts_ok, 1)
            quarter = RACC // P * D // 4
            for a in range(NACC):
                for i in range(4):
                    dst = acc_scr[a].rearrange("(p n) d -> p (n d)", p=P)[:, i * quarter:(i + 1) * quarter]
                    sp.dma_start(dst, zeros[:, :]).then_inc(zero_out, 16)

            def step(s, rep):
                on = stages(rep)
                par = rep % 2
                for i in range(H):
                    if mg := m_group(s, rep, i):
                        b, g = mg
                        mpar = (rep - (1 if i else 2)) % 2
                        sp.wait_ge(mparts_ok, b * NM + g + 1)
                        apart(sp)
                        due(sp, max_in[g], (b - 1) * 16)
                        src = mparts[g % 2]
                        dst = max_scr[mpar, :, g * MG * S:(g + 1) * MG * S]
                        sp.dma_start(dst.rearrange("i (r q) -> r i q", q=P), src[:, :, :]).then_inc(max_out, 16)
                        sp.wait_ge(max_out, (b * NM + g + 1) * 16)
                        rows = Qs[mpar][ROWS_B:ROWS_C, g * MG:(g + 1) * MG, :]
                        sp.dma_start(rows.rearrange("p h s -> p (h s)"), dst).then_inc(max_in[g], 16)
                    if on["A"] and i == 9:
                        sp.wait_ge(parts_ok, s + 1)
                        apart(sp)
                        due(sp, qk_in, (s - 1) * 192 if rep >= 2 else 0)
                        dst = qk_scr[par].rearrange("r w (c p) s -> p r (w c) s", p=P)
                        for r in range(3):
                            sp.dma_start(dst[:, r], parts[:, r, :, :]).then_inc(qk_out, 16)
                    if on["A"] and i == 11:
                        if rep >= 2:
                            sp.wait_ge(sT_ok, (s - 1) * H)
                            apart(sp)
                        sp.wait_ge(qk_out, (s + 1) * 48)
                        for w, (dst, blocks) in enumerate(((Qs[par], Q_PARTS), (Ks[par], K_PARTS))):
                            for j, r in enumerate(blocks):
                                sp.dma_start(dst[j * HD:(j + 1) * HD, :, :],
                                             qk_scr[par, r, w].rearrange("(h d) s -> d h s", d=HD))\
                                  .then_inc(qk_in, 16)

            pipeline(sp, step)

            sp.wait_ge(tinfo_ok, 1)
            for c in range(2):
                sp.dma_start(tile_scr[c:c + 1, :].rearrange("c p -> p c"), tinfo[:, c, 4:5],
                             allow_slow_non_contiguous=True).then_inc(tinfo_out, 16)
            sp.wait_ge(tinfo_out, 32)
            row = tile_scr.rearrange("c p -> (c p)").rearrange("(o x) -> o x", o=1)
            sp.dma_start(treg_f[:, :], row).then_inc(tinfo_in, 16)
            sp.dma_start(tslot[:, :], row.broadcast_to([P, 2 * P])).then_inc(tinfo_in, 16)

            sp.wait_ge(padreg_ok, 1)
            with sp.Fori(0, E) as e:
                row = sp.value_load(padreg[0:1, bass.ds(e, 1)], min_val=0, max_val=E * CAP - P)
                sp.dma_start(xs[bass.ds(row, P), :], padrow[:, :]).then_inc(pad_out, 16)
            sp.dma_start(xs[E * CAP - P:E * CAP, :], padrow[:, :]).then_inc(pad_out, 16)

            def load_tile(t, j, g, rep):
                first = sp.value_load(treg[0:1, bass.ds(t, 1)], min_val=0, max_val=E * CAP - P)
                if rep:
                    sp.wait_ge(acc_ok[j], g * 16)
                    apart(sp)
                    sp.wait_ge(tw_ok, t - RING + 1)
                sp.dma_start(x_t[j], xs[bass.ds(first, P), :]).then_inc(x_in[j], 16)
                if rep:
                    sp.wait_ge(ty_ok, t - RING + 1)
                    apart(sp)
                sp.dma_start(w_t[j], experts[bass.ds((first // CAP) * P, P), :]).then_inc(w_in[j], 16)

            sp.wait_ge(treg_ok, 1)
            sp.wait_ge(pad_out, (E + 1) * 16)
            for i in range(2):
                sp.wait_ge(scat_ok[i], B // 2 * QT * TOPK * 16)
            for j in range(RING):
                load_tile(j, j, 0, False)
            with sp.Fori(1, TILES // RING) as g:
                for j in range(RING):
                    load_tile(g * RING + j, j, g, True)

            for j in range(RING):
                sp.wait_ge(acc_ok[j], TILES // RING * 16)
            for n in range(NT // 4):
                if n >= 2:
                    sp.wait_ge(fin_ok, n - 1)
                for a in range(NACC):
                    sp.dma_start(fin[n % 2][:, a],
                                 acc_scr[a][n * 512:(n + 1) * 512, :].rearrange("(n p) d -> p n d", p=P))\
                      .then_inc(fin_in[n % 2], 16)
            for n in range(NT // 4):
                sp.wait_ge(fin_ok, n + 1)
                sp.dma_start(out[n * 512:(n + 1) * 512, :].rearrange("(n p) d -> p n d", p=P),
                             emb[:, n * 4:(n + 1) * 4, :]).then_inc(out_done, 16)
            sp.wait_ge(out_done, NT // 4 * 16)

        @block.gpsimd
        def _(pool):
            n_c = [0]

            def const(ins):
                n_c[0] += 1
                ins.then_inc(consts_p, 1)
                pool.wait_ge(consts_p, n_c[0])

            pool.wait_ge(ids_in, 16)
            for j in range(NT):
                pool.indirect_dma_start(emb[:, j, :], None, table,
                                        bass.IndirectOffsetOnAxis(ids_sb[:, j:j + 1].bitcast(U32), 0))\
                    .then_inc(emb_in, 16)
            pool.wait_ge(tier_ok, 1)
            for j in range(NT):
                pool.indirect_dma_start(tsel[:, j, :], None, ts,
                                        bass.IndirectOffsetOnAxis(tier_u[:, j:j + 1], 0)).then_inc(ts_in, 16)
            for t, v in ((ident, 0.0), (before, 0.0), (ones, 1.0), (zeros, 0.0), (padrow, 0.0), (lower, 0.0),
                         (half, -0.5), (one_e, 1.0), (run, 0.0), (onesrow, 1.0)):
                const(pool.memset(t[tuple(slice(None) for _ in t.shape)], v))
            const(pool.affine_select(out=ident[:, :], in_=ident[:, :], compare_op=ALU.not_equal, fill=1.0,
                                     base=0, pattern=[[-1, P]], channel_multiplier=1))
            const(pool.affine_select(out=before[:, :], in_=before[:, :], compare_op=ALU.is_ge, fill=1.0,
                                     base=0, pattern=[[-1, P]], channel_multiplier=1))
            const(pool.affine_select(out=lower[:, :, :], in_=lower[:, :, :], compare_op=ALU.is_ge, fill=1.0,
                                     base=0, pattern=[[-1, G], [1, G]], channel_multiplier=0))
            const(pool.iota(part_i[:, :], pattern=[[P, 2]], base=0, channel_multiplier=1))
            const(pool.tensor_copy(part_f[:, 0:2], part_i[:, :]))
            const(pool.iota(tok_u[:, :], pattern=[[P, NT]], base=0, channel_multiplier=1))
            const(pool.iota(iota_i[:, 0:E], pattern=[[1, E]], base=0, channel_multiplier=0))
            const(pool.tensor_copy(eidx[:, :], iota_i[:, 0:E]))
            const(pool.tensor_scalar(ebase[:, :], eidx[:, :], float(CAP), 1.0, ALU.mult, ALU.add))
            const(pool.iota(iota_i[:, :], pattern=[[1, S]], base=0, channel_multiplier=0))
            const(pool.tensor_copy(pos_f[:, :], iota_i[0:H, :]))
            const(pool.tensor_scalar(part_f[:, 2:3], part_f[:, 0:1], 1.0, None, ALU.add))
            const(pool.iota(padrow[:, TOKCOL:TOKCOL + 1].bitcast(I32), pattern=[[0, 1]], base=T,
                            channel_multiplier=1))
            for par in range(2):
                const(pool.memset(V[par][:, :, :, HD:HD + 1], 1.0))
                const(pool.memset(x2[par][:, :, WCOL + TOPK:ROW], 0.0))
            pool.memset(iota_i[:, 0:1], 0).then_inc(consts_ok, 1)

            pool.wait_ge(pmax_ok, 1)
            pool.partition_all_reduce(amax[:, 0:3], pmax[:, 0:3], P, RMAX).then_inc(amax_ok, 1)

            chain = Chain(pool, chain_p, 3)

            def scatters(r, rep, ks):
                rpar = rep % 2
                for t in range(QT):
                    for k in ks:
                        pool.indirect_dma_start(xs[:, :],
                                                bass.IndirectOffsetOnAxis(slot_u[rpar][:, t, k:k + 1], 0),
                                                x2[rpar][:, t, :], None).then_inc(scat_ok[rpar], 16)

            def step(s, rep):
                on = stages(rep)
                if on["A"]:
                    pool.wait_ge(var_ok, s + 1)
                    pool.tensor_tensor(rstd[:, :], mv_eps[:, :], half[:, :], ALU.pow).then_inc(rstd_ok, 1)
                    pool.wait_ge(qk32_ok, s * 4 + 4)
                    if rep >= 1:
                        pool.wait_ge(qk_out, s * 48)
                        apart(pool)
                    chain.start(s)
                    chain.link(pool.tensor_copy(parts[:, 0], qk32[:, :, :]))
                    chain.link(pool.tensor_tensor(qkr[:, :, :], qk32[:, :, :], parts[:, 0], ALU.subtract))
                    apart(pool)
                    chain.link(pool.tensor_copy(parts[:, 1], qkr[:, :, :]))
                    pool.tensor_tensor(parts[:, 2], qkr[:, :, :], parts[:, 1], ALU.subtract).then_inc(parts_ok, 1)
                if on["R"]:
                    pool.wait_ge(slots_ok, s - 3 + 1)
                    apart(pool)
                    scatters(s - 3, rep - 3, range(0, 2))
                if on["D"]:
                    pool.wait_ge(var2_ok, s - 2 + 1)
                    pool.tensor_tensor(rstd2[:, :], mv2_eps[:, :], half[:, :], ALU.pow).then_inc(rstd2_ok, 1)
                if on["R"]:
                    scatters(s - 3, rep - 3, range(2, TOPK))

            pipeline(pool, step)

            def accumulate(g, j, rep):
                pool.wait_ge(te_ok, g * RING + j + 1)
                if j >= NACC:
                    pool.wait_ge(acc_ok[j - NACC], (g + 1) * 16)
                elif rep:
                    pool.wait_ge(acc_ok[j - NACC + RING], g * 16)
                apart(pool)
                pool.indirect_dma_start(acc_scr[j % NACC], bass.IndirectOffsetOnAxis(
                    x_t[j][:, TOKCOL:TOKCOL + 1].bitcast(U32), 0), y_t[j], None, compute_op=ALU.add)\
                    .then_inc(acc_ok[j], 16)

            pool.wait_ge(zero_out, NACC * 4 * 16)
            for j in range(RING):
                accumulate(0, j, False)
            with pool.Fori(1, TILES // RING) as g:
                for j in range(RING):
                    accumulate(g, j, True)

        @block.scalar
        def _(act):
            def step(s, rep):
                on = stages(rep)
                for i in range(H):
                    if head := c_head(s, rep, i):
                        b, h = head
                        n = b * H + h
                        first = rep - (1 if i >= LAG else 2) == 0
                        act.wait_ge(sT_ok, n + 1)
                        if not (first and h < 2):
                            act.wait_ge(pv_ok, n - 1)
                        act.activation(PT[h % 2][:, :, :].rearrange("p k q -> p (k q)"), pT[h % 2][:, :],
                                       ACT.Exp).then_inc(exp_ok, 1)
                    if on["A"] and i == 3:
                        act.wait_ge(xnT_ok, s + 1)
                        act.activation(xT[:, :, :].rearrange("p c t -> p (c t)"), pF[0][:, :], ACT.Copy)\
                            .then_inc(xT_ok, 1)
                    if on["A"] and i == 5:
                        if rep >= 1:
                            act.wait_ge(parts_ok, s)
                        for w in range(2):
                            act.wait_ge(qk_ok, s * 2 + w + 1)
                            for m in range(2):
                                mm = 2 * w + m
                                act.activation(qk32[:, mm, :], pF[1 - w][:, m * S:(m + 1) * S], ACT.Identity,
                                               bias=bqk_sb[:, mm:mm + 1], scale=0.25 if w == 0 else 1.0)\
                                    .then_inc(qk32_ok, 1)
                    if on["D"] and i == 10:
                        act.wait_ge(cnT_ok, s - 2 + 1)
                        act.activation(cT[:, :, :].rearrange("p c t -> p (c t)"), pF[0][:, :], ACT.Copy)\
                            .then_inc(cT_ok, 1)
                    if on["D"] and i == 13:
                        act.wait_ge(x2T_ps, s - 2 + 1)
                        act.activation(x2T[:, :, :].rearrange("p c t -> p (c t)"), pF[0][:, :], ACT.Copy)\
                            .then_inc(x2T_ok, 1)
                        act.activation(xT_all[:, :, bass.ds((s - 2) * S, S)],
                                       pF[0][:, :].rearrange("p (c t) -> p c t", c=KC), ACT.Copy)\
                            .then_inc(x2T_ok, 1)
                    if on["D"] and i == 14:
                        act.wait_ge(logit_ok, s - 2 + 1)
                        if rep >= 3:
                            act.wait_ge(sel_ok, s - 2)
                        act.activation(esig[:, :, :].rearrange("p t e -> p (t e)"), pF[1][:, 0:QT * E],
                                       ACT.Exp, scale=-1.0).then_inc(esig_ok, 1)

            act.wait_ge(bias_ok, 1)
            pipeline(act, step)

            for n in range(T // 512):
                for m in range(ISH // P):
                    act.wait_ge(sh_gu, n * 2 + m + 1)
                    due(act, sh_h_ok, (n - 1) * 2 + m + 1)
                    act.activation(sh_g[m], pS[m][:, :], ACT.Silu).then_inc(sh_silu, 1)

            def silu(t, par, rep):
                act.wait_ge(tg_ok, t + 1)
                if rep >= 2:
                    act.wait_ge(th_ok, t - 1)
                act.activation(sg_t[par], pT[par][:, 0:P], ACT.Silu).then_inc(ts_ok, 1)

            def weigh(t, j, g, rep):
                act.wait_ge(ty_ok, t + 1)
                act.wait_ge(tw_ok, t + 1)
                if rep >= RING:
                    act.wait_ge(acc_ok[j], g * 16)
                act.activation(y_t[j], pF[j % 2][:, 0:D], ACT.Copy, scale=wt_t[j][:, 0:1]).then_inc(te_ok, 1)

            for t in range(RING):
                silu(t, t % 2, t)
                if t:
                    weigh(t - 1, t - 1, 0, t - 1)
            with act.Fori(1, TILES // RING) as g:
                for j in range(RING):
                    silu(g * RING + j, j % 2, RING)
                    if j:
                        weigh(g * RING + j - 1, j - 1, g, RING)
                    else:
                        weigh(g * RING - 1, RING - 1, g - 1, 2)
            weigh(TILES - 1, RING - 1, TILES // RING - 1, RING)

        @block.vector
        def _(dve):
            setup = Chain(dve, set_v, 1 << 20)

            dve.wait_ge(ids_in, 16)
            setup.link(dve.tensor_copy(idf[:, :], ids_sb[:, :]))
            for i in range(3):
                setup.link(dve.tensor_scalar(ge[:, i, :], idf[:, :], float(TIERS[i]), None, ALU.is_ge))
            setup.link(dve.tensor_tensor(ge[:, 3, :], ge[:, 0, :], ge[:, 1, :], ALU.add))
            dve.tensor_tensor(tier_u[:, :], ge[:, 3, :], ge[:, 2, :], ALU.add).then_inc(tier_ok, 1)
            setup.link(dve.tensor_scalar(intier[:, 0, :], ge[:, 0, :], -1.0, 1.0, ALU.mult, ALU.add))
            setup.link(dve.tensor_tensor(intier[:, 1, :], ge[:, 0, :], ge[:, 1, :], ALU.subtract))
            setup.link(dve.tensor_tensor(intier[:, 2, :], ge[:, 1, :], ge[:, 2, :], ALU.subtract))
            setup.link(dve.tensor_copy(maxq[:, :], intier[:, 0, :]))
            for i, of in enumerate((intier[:, 1, :], intier[:, 2, :], ge[:, 2, :])):
                setup.link(dve.scalar_tensor_tensor(maxq[:, :], of, MAXQ[i], maxq[:, :], ALU.mult, ALU.add))
            setup.link(dve.tensor_scalar(nmaxq[:, :], maxq[:, :], -1.0, None, ALU.mult))
            dve.memset(cmax[:, :, :], 0.0).then_inc(scan_v, 1)

            scan_links = [1]

            def reduce_chunk(slot, count, parts, rows, tier, links):
                dve.wait_ge(ring_in[slot], count)
                dve.wait_ge(scan_v, links)
                dve.tensor_reduce(cnew[0:parts, :], ring[0:parts, slot, 0:rows, :].rearrange("p n d -> p d n"),
                                  AX_X, ALU.max, apply_absolute_value=True).then_inc(ring_used, 1)
                return cmax[0:parts, tier, :], cnew[0:parts, :]

            def scan_chunk(slot, count, parts, rows, tier, index, links):
                into, new = reduce_chunk(slot, count, parts, rows, tier, links)
                dve.wait_ge(ring_used, index + 1)
                dve.tensor_tensor(into, into, new, ALU.max).then_inc(scan_v, 1)

            rows2 = (TIERS[2] - TIERS[1]) // P // 2
            heads = ((P, rows2, 1), (P, rows2, 1), (T1P, 4, 0), (REST3, 1, 2))
            for k, (parts_, rows, tier) in enumerate(heads):
                scan_chunk(HEAD0 + k, 16, parts_, rows, tier, k, k + 1)

            def turn(i):
                for j in range(SCAN_RING):
                    index = i * SCAN_RING + j + len(heads)
                    scan_chunk(j, (i + (2 if j >= HEAD0 else 1)) * 16, P, SCAN_ROWS, 2, index, index + 1)

            turn(0)
            dve.wait_ge(consts_ok, 1)
            dve.wait_ge(slope_in_s, 16)
            setup.link(dve.tensor_copy(sparts[:, 0:1], slope_in[:, 0:1]))
            setup.link(dve.tensor_tensor(slope_in[:, 1:2], slope_in[:, 0:1], sparts[:, 0:1], ALU.subtract))
            setup.link(dve.tensor_copy(sparts[:, 1:2], slope_in[:, 1:2]))
            setup.link(dve.tensor_tensor(slope_in[:, 2:3], slope_in[:, 1:2], sparts[:, 1:2], ALU.subtract))
            setup.link(dve.tensor_copy(sparts[:, 2:3], slope_in[:, 2:3]))
            for i in range(3):
                last = dve.tensor_scalar(slope_p[:, i, :], onesrow[:, :], sparts[:, i:i + 1], None, ALU.mult)
            last.then_inc(rows_ok, 1)
            dve.tensor_scalar(pos_p[:, 0, :], pos_f[:, :], -1.0, None, ALU.mult)
            dve.tensor_copy(pos_p[:, 1, :], pos_f[:, :])
            dve.tensor_copy(pos_p[:, 2, :], onesrow[:, :]).then_inc(rows_ok, 1)
            dve.wait_ge(w_in_sb, NLOADS * 16)
            dve.tensor_scalar(bqk_sb[:, 0:2], bqk_sb[:, 0:2], 0.25, None, ALU.mult).then_inc(bias_ok, 1)
            dve.wait_ge(emb_in, NT * 16)
            dve.wait_ge(ts_in, NT * 16)
            setup.link(dve.tensor_tensor(emb[:, :, :], emb[:, :, :], tsel[:, :, :], ALU.mult))
            with dve.Fori(1, CHUNKS // SCAN_RING) as i:
                turn(i)

            dve.wait_ge(scan_v, CHUNKS + len(heads) + 1)
            setup.link(dve.tensor_tensor(cmax[:, :, :], cmax[:, :, :], tsb[:, 1:4, :], ALU.mult))
            dve.tensor_reduce(pmax[:, 0:3], cmax[:, :, :], AX_X, ALU.max, apply_absolute_value=True)\
               .then_inc(pmax_ok, 1)
            dve.wait_ge(amax_ok, 1)
            setup.link(dve.tensor_scalar(sc3[:, 0:3], amax[:, 0:3], 1e-8, None, ALU.max))
            for i in range(3):
                setup.link(dve.tensor_scalar(sc3[:, i:i + 1], sc3[:, i:i + 1], float(np.float32(1) / np.float32(MAXQ[i])),
                                             None, ALU.mult))
            src = intier[:, 0, :]
            for i, of in enumerate((intier[:, 1, :], intier[:, 2, :], ge[:, 2, :])):
                setup.link(dve.scalar_tensor_tensor(scale[:, :], of, sc3[:, i:i + 1], src, ALU.mult, ALU.add))
                src = scale[:, :]
            setup.link(dve.reciprocal(inv[:, :], scale[:, :]))

            ca, cd, cr, cm = (Chain(dve, s_, per) for s_, per in
                              ((chain_a, LINKS_A), (chain_d, LINKS_D), (chain_r, LINKS_R),
                               (chain_m, 3)))

            def token(t, b):
                return bass.ds(b * QT + t, 1)

            def quantise(b, rep):
                ca.start(b)
                pair = bass.ds(b * QT, QT)
                for t in range(QT):
                    k = token(t, b)
                    ca.link(dve.tensor_scalar(xq[:, t, :], emb[:, k, :].rearrange("p o d -> p (o d)"), inv[:, k],
                                              ROUND, ALU.mult, ALU.add))
                    ca.link(dve.tensor_scalar(xq[:, t, :], xq[:, t, :], -ROUND, maxq[:, k], ALU.add, ALU.min))
                    ca.link(dve.tensor_scalar(xq[:, t, :], xq[:, t, :], nmaxq[:, k], scale[:, k], ALU.max, ALU.mult))
                ca.link(dve.tensor_tensor(xq[:, :, :], xq[:, :, :], emb[:, pair, :], ALU.subtract))
                for t in range(QT):
                    e1 = emb[:, token(t, b), :].rearrange("p o d -> p (o d)")
                    last = dve.scalar_tensor_tensor(e1, xq[:, t, :], ge[:, 0, token(t, b)], e1, ALU.mult, ALU.add)
                    ca.link(last)

            def norm_stats(c, b, src, st, m, eps, signal):
                apart(dve)
                for t in range(QT):
                    ins = dve.bn_stats(st[:, t, :], src(t))
                c.link(ins)
                apart(dve)
                for t in range(QT):
                    ins = dve.bn_aggr(m[:, t, :], st[:, t, :])
                c.link(ins)
                dve.tensor_scalar(eps[:, :], m[:, :, 1], EPS, None, ALU.add).then_inc(signal, 1)

            def step(s, rep):
                on = stages(rep)
                par = rep % 2
                for i in range(H):
                    if on["B"]:
                        n = (s - 1) * H + i
                        dve.wait_ge(s_ok, n + 1)
                        if i % MG == 0 and rep >= 2:
                            dve.wait_ge(mT_ok, (s - 2) * NM + i // MG + 1)
                        dve.tensor_reduce(nmax[:, i, :], pS[i % 2][:, :].rearrange("p (t k) -> p t k", t=QT),
                                          AX_X, ALU.max, negate=True).then_inc(max_ok, 1)
                    if mg := m_group(s, rep, i):
                        b, g = mg
                        n = b * NM + g
                        dve.wait_ge(mT_ok, n + 1)
                        if rep - (1 if i else 2) > 0 or g >= 2:
                            dve.wait_ge(max_out, (n - 1) * 16)
                        cm.start(n)
                        mrow = pF[MBANK[g]][0:MG * QT, 0:P]
                        mp = mparts[g % 2]
                        cm.link(dve.tensor_copy(mp[:, 0, :], mrow))
                        cm.link(dve.tensor_tensor(m32[:, :], mrow, mp[:, 0, :], ALU.subtract))
                        cm.link(dve.tensor_copy(mp[:, 1, :], m32[:, :]))
                        dve.tensor_tensor(mp[:, 2, :], m32[:, :], mp[:, 1, :], ALU.subtract).then_inc(mparts_ok, 1)
                    if on["A"] and i == 0:
                        quantise(s, rep)
                    if on["A"] and i == 1:
                        norm_stats(ca, s, lambda t: emb[:, token(t, s), :].rearrange("p o d -> p (o d)"),
                                   stats, mv, mv_eps, var_ok)
                    if on["A"] and i == 2:
                        dve.wait_ge(rstd_ok, s + 1)
                        if rep >= 1:
                            dve.wait_ge(xnT_ok, s)
                        for t in range(QT):
                            ins = dve.tensor_scalar(xn[:, t, :], emb[:, token(t, s), :].rearrange("p o d -> p (o d)"),
                                                    mv[:, t, 0:1], rstd[:, t:t + 1], ALU.subtract, ALU.mult)
                        ins.then_inc(xn_ok, 1)
                    if on["R"] and i == 3:
                        choose(s - 3, rep - 3)
                    if on["A"] and i == 8:
                        dve.wait_ge(v_ok, s + 1)
                        if rep >= 2:
                            dve.wait_ge(pv_ok, (s - 1) * H)
                        dve.tensor_tensor(V[par][:, :, :, 0:HD], pF[1][:, :].rearrange("p (t h d) -> p t h d", t=QT, h=H),
                                          bv_sb[:, :].rearrange("p (h d) -> p h d", h=H).unsqueeze(1)
                                          .broadcast_to([P, QT, H, HD]), ALU.add).then_inc(v_done, 1)
                    if on["R"] and i == 7:
                        slots(s - 3, rep - 3)
                    if on["D"] and i == 9:
                        d = s - 2
                        cd.start(d)
                        dve.wait_ge(pv_ok, (d + 1) * H)
                        c4 = pC[:, :, 0:H * (HD + 1)].rearrange("p t (h d) -> p t h d", h=H)
                        cd.link(dve.reciprocal(rsum[:, :, :], c4[:, :, :, HD]))
                        if rep - 2 >= 1:
                            dve.wait_ge(cnT_ok, d)
                        dve.tensor_tensor(cn[:, :, :].rearrange("p t (h d) -> p t h d", h=H), c4[:, :, :, 0:HD],
                                          rsum[:, :, :].unsqueeze(3).broadcast_to([P, QT, H, HD]), ALU.mult)\
                           .then_inc(cn_ok, 1)
                    if on["D"] and i == 12:
                        d = s - 2
                        pair = bass.ds(d * QT, QT)
                        dve.wait_ge(wo_ok, d + 1)
                        cd.link(dve.tensor_tensor(xo[:, :, :], pF[1][:, :].rearrange("p (t d) -> p t d", t=QT),
                                                  bo_sb[:, :].unsqueeze(1).broadcast_to([P, QT, D]), ALU.add))
                        dve.tensor_tensor(emb[:, pair, :], emb[:, pair, :], xo[:, :, :], ALU.add).then_inc(res_ok, 1)
                        dve.wait_ge(res_ok, d + 1)
                        norm_stats(cd, d, lambda t: emb[:, token(t, d), :].rearrange("p o d -> p (o d)"),
                                   stats2, mv2, mv2_eps, var2_ok)
                        dve.wait_ge(rstd2_ok, d + 1)
                        due(dve, scat_ok[par], (d - par) * (QT * TOPK * 16 // 2))
                        for t in range(QT):
                            ins = dve.tensor_scalar(x2[par][:, t, 0:D], emb[:, token(t, d), :].rearrange("p o d -> p (o d)"),
                                                    mv2[:, t, 0:1], rstd2[:, t:t + 1], ALU.subtract, ALU.mult)
                        ins.then_inc(x2_ok, 1)

            def choose(r, rep):
                cr.start(r)
                dve.wait_ge(esig_ok, r + 1)
                cr.link(dve.tensor_scalar(score[:, :, :], esig[:, :, :], 1.0, None, ALU.add))
                cr.link(dve.reciprocal(score[:, :, :], score[:, :, :]))
                cr.link(dve.tensor_tensor(score[:, :, :], score[:, :, :],
                                          gbias_sb[:, :].unsqueeze(1).broadcast_to([P, QT, E]), ALU.add))
                by_group = score[:, :, :].rearrange("p t (g e) -> p (t g) e", g=G)
                cr.link(dve.tensor_reduce(gs[:, :, :].rearrange("p t g -> p (t g)"), by_group, AX_X, ALU.max))
                other = gs[:, :, :].unsqueeze(2).broadcast_to([P, QT, G, G])
                own = gs[:, :, :].unsqueeze(3).broadcast_to([P, QT, G, G])
                dve.tensor_tensor(cmp_a[:, :, :, :], other, own, ALU.is_gt)
                cr.link(dve.tensor_tensor(cmp_b[:, :, :, :], other, own, ALU.is_equal))
                cr.link(dve.tensor_tensor(cmp_b[:, :, :, :], cmp_b[:, :, :, :],
                                          lower[:, :, :].unsqueeze(1).broadcast_to([P, QT, G, G]), ALU.mult))
                cr.link(dve.tensor_tensor(cmp_a[:, :, :, :], cmp_a[:, :, :, :], cmp_b[:, :, :, :], ALU.add))
                cr.link(dve.tensor_reduce(gmask[:, :, :], cmp_a[:, :, :, :], AX_X, ALU.add))
                cr.link(dve.tensor_scalar(gmask[:, :, :], gmask[:, :, :], float(TG), None, ALU.is_lt))
                cr.link(dve.tensor_tensor(ms[:, :, :].rearrange("p t (g e) -> p t g e", g=G),
                                          score[:, :, :].rearrange("p t (g e) -> p t g e", g=G),
                                          gmask[:, :, :].unsqueeze(3).broadcast_to([P, QT, G, E // G]), ALU.mult))
                cr.link(dve.tensor_scalar(ms[:, :, :], ms[:, :, :], 0.0, None, ALU.add))
                apart(dve)
                for t in range(QT):
                    ins = dve.max(top[:, t, :], ms[:, t, :])
                cr.link(ins)
                apart(dve)
                for t in range(QT):
                    ins = dve.max_index(topi[:, t, :], top[:, t, :], ms[:, t, :])
                cr.link(ins)
                dve.tensor_reduce(wsum[:, :], top[:, :, 0:TOPK], AX_X, ALU.add)
                cr.link(dve.tensor_copy(lastf[:, :], topi[:, :, TOPK - 1]))
                cr.link(dve.tensor_scalar(wsum[:, :], wsum[:, :], 1e-8, None, ALU.add))
                cr.link(dve.reciprocal(wsum[:, :], wsum[:, :]))
                due(dve, prefix_ok, r)
                for t in range(QT):
                    ins = dve.tensor_scalar(tie[:, t, :], eidx[:, :], lastf[:, t:t + 1], None, ALU.is_le)
                cr.link(ins)
                for t in range(QT):
                    ins = dve.scalar_tensor_tensor(tie[:, t, :], ms[:, t, :], top[:, t, TOPK - 1:TOPK], tie[:, t, :],
                                                   ALU.is_equal, ALU.mult)
                cr.link(ins)
                for t in range(QT):
                    ins = dve.scalar_tensor_tensor(M[:, t, :], ms[:, t, :], top[:, t, TOPK - 1:TOPK], tie[:, t, :],
                                                   ALU.is_gt, ALU.add)
                ins.then_inc(sel_ok, 1)
                dve.wait_ge(sel_ok, r + 1)
                for t in range(QT):
                    ins = dve.scalar_tensor_tensor(wn[:, t, :], ms[:, t, :], wsum[:, t:t + 1], M[:, t, :],
                                                   ALU.mult, ALU.mult)
                cr.link(ins)

            def slots(r, rep):
                par = rep % 2
                dve.wait_ge(prefix_ok, r + 1)
                pre = pF[0][:, 0:3 * E].rearrange("p (x e) -> p x e", x=3)
                cr.link(dve.tensor_tensor(key[:, :, :], pre[:, 0:QT, :], run[:, :].unsqueeze(1)
                                          .broadcast_to([P, QT, E]), ALU.add))
                dve.tensor_tensor(run[:, :], run[:, :], pre[:, QT, :], ALU.add)
                cr.link(dve.tensor_tensor(key[:, :, :], key[:, :, :], ebase[:, :].unsqueeze(1)
                                          .broadcast_to([P, QT, E]), ALU.add))
                cr.link(dve.tensor_tensor(key[:, :, :], key[:, :, :], M[:, :, :], ALU.mult))
                apart(dve)
                for t in range(QT):
                    ins = dve.max(topk[:, t, :], key[:, t, :])
                cr.link(ins)
                cr.link(dve.tensor_tensor(eq[:, :, :, :], key[:, :, :].unsqueeze(2).broadcast_to([P, QT, TOPK, E]),
                                          topk[:, :, 0:TOPK].unsqueeze(3).broadcast_to([P, QT, TOPK, E]), ALU.is_equal))
                cr.link(dve.tensor_tensor(eq[:, :, :, :], eq[:, :, :, :],
                                          wn[:, :, :].unsqueeze(2).broadcast_to([P, QT, TOPK, E]), ALU.mult))
                dve.tensor_reduce(x2[par][:, :, WCOL:WCOL + TOPK], eq[:, :, :, :], AX_X, ALU.add)
                dve.tensor_copy(x2[par][:, :, SLOTCOL:SLOTCOL + TOPK], topk[:, :, 0:TOPK])
                dve.tensor_copy(x2[par][:, :, TOKCOL:TOKCOL + 1].bitcast(I32),
                                tok_u[:, bass.ds(r * QT, QT)].unsqueeze(2))
                dve.tensor_scalar(slot_u[par][:, :, :], topk[:, :, 0:TOPK], -1.0, None, ALU.add).then_inc(slots_ok, 1)

            pipeline(dve, step)

            tab = Chain(dve, chain_t, 1 << 20)
            tab.link(dve.tensor_scalar(nt_e[:, :], run[:, :], 127.0, 1.0 / 128.0, ALU.add, ALU.mult))
            tab.link(dve.tensor_scalar(nt_e[:, :], nt_e[:, :], -127.0 / 256.0, ROUND, ALU.add, ALU.add))
            tab.link(dve.tensor_scalar(nt_e[:, :], nt_e[:, :], -ROUND, None, ALU.add))
            tab.link(dve.tensor_tensor_scan(end_e[:, :], one_e[:, :], nt_e[:, :], 0.0, ALU.mult, ALU.add))
            for c in range(2):
                tab.link(dve.tensor_scalar(tsc[:, c, :], end_e[:, :], part_f[:, c:c + 1], None, ALU.is_le))
                tab.link(dve.tensor_reduce(tinfo[:, c, 0:1], tsc[:, c, :], AX_X, ALU.add))
                tab.link(dve.tensor_tensor(tsc[:, c, :], tsc[:, c, :], nt_e[:, :], ALU.mult))
                tab.link(dve.tensor_reduce(tinfo[:, c, 1:2], tsc[:, c, :], AX_X, ALU.add))
                tab.link(dve.tensor_tensor(tinfo[:, c, 2:3], part_f[:, c:c + 1], tinfo[:, c, 1:2], ALU.subtract))
                tab.link(dve.tensor_scalar(tinfo[:, c, 2:3], tinfo[:, c, 2:3], float(P), None, ALU.mult))
                tab.link(dve.scalar_tensor_tensor(tinfo[:, c, 4:5], tinfo[:, c, 0:1], float(CAP), tinfo[:, c, 2:3],
                                                  ALU.mult, ALU.add))
                tab.link(dve.tensor_scalar(tinfo[:, c, 4:5], tinfo[:, c, 4:5], float(E * CAP - P), None, ALU.min))
            dve.engine_nop().then_inc(tinfo_ok, 1)
            tab.link(dve.tensor_tensor(one_e[:, :], run[:, :], ebase[:, :], ALU.add))
            dve.tensor_scalar(padreg[:, :], one_e[:, :], -1.0, None, ALU.add).then_inc(padreg_ok, 1)
            dve.wait_ge(tinfo_in, 32)
            dve.tensor_copy(treg[:, :], treg_f[:, :]).then_inc(treg_ok, 1)
            dve.tensor_scalar(tslot[:, :], tslot[:, :], part_f[:, 2:3], None, ALU.add).then_inc(tslot_ok, 1)

            for n in range(T // 512):
                for m in range(ISH // P):
                    dve.wait_ge(sh_silu, n * 2 + m + 1)
                    due(dve, sh_y, (n - 1) * 2)
                    dve.tensor_tensor(sh_h[n % 2][:, m, :], sh_g[m], pT[m][:, :], ALU.mult).then_inc(sh_h_ok, 1)
                for k in range(2):
                    dve.wait_ge(sh_y, n * 2 + k + 1)
                    pair = emb[:, n * 4 + 2 * k:n * 4 + 2 * k + 2, :]
                    dve.tensor_tensor(pair, pF[k][:, :].rearrange("p (t d) -> p t d", t=2), pair, ALU.add)\
                       .then_inc(sh_done, 1)

            def copy_x(t, j, g, rep):
                dve.wait_ge(tT_ok, t + 1)
                if rep >= 2:
                    dve.wait_ge(tg_ok, t - 1)
                dve.tensor_copy(xT_t[j % 2], pS[j % 2][:, 0:KC * P]).then_inc(tx_ok, 1)
                if rep >= RING:
                    dve.wait_ge(te_ok, t - RING + 1)
                dve.scalar_tensor_tensor(eq_t[j][:, 0:TOPK], x_t[j][:, SLOTCOL:SLOTCOL + TOPK], tslot[:, bass.ds(t, 1)],
                                         x_t[j][:, WCOL:WCOL + TOPK], ALU.is_equal, ALU.mult,
                                         accum_out=wt_t[j][:, 0:1]).then_inc(tw_ok, 1)

            def gate_up(t, j, rep):
                dve.wait_ge(ts_ok, t + 1)
                if rep >= 2:
                    dve.wait_ge(ty_ok, t - 1)
                dve.tensor_tensor(h_t[j % 2], sg_t[j % 2], pT[j % 2][:, P:2 * P], ALU.mult).then_inc(th_ok, 1)

            dve.wait_ge(tslot_ok, 1)
            for j in range(RING):
                copy_x(j, j, 0, j)
                if j:
                    gate_up(j - 1, j - 1, j - 1)
            with dve.Fori(1, TILES // RING) as g:
                for j in range(RING):
                    copy_x(g * RING + j, j, g, RING)
                    gate_up(g * RING + j - 1, (j - 1) % RING, RING)
            gate_up(TILES - 1, RING - 1, RING)

            for n in range(NT // 4):
                dve.wait_ge(fin_in[n % 2], (n // 2 + 1) * NACC * 16)
                for a in range(NACC):
                    four = emb[:, n * 4:(n + 1) * 4, :]
                    ins = dve.tensor_tensor(four, four, fin[n % 2][:, a], ALU.add)
                    if a < NACC - 1:
                        ins.then_inc(fin_v, 1)
                        dve.wait_ge(fin_v, n * (NACC - 1) + a + 1)
                    else:
                        ins.then_inc(fin_ok, 1)

        @block.tensor
        def _(pe):
            def transpose2(src, dst, rows):
                for t in range(QT):
                    for c in range(KC):
                        ins = pe.transpose(dst[:, c * S + t * P:c * S + (t + 1) * P], src(t)[:, c * P:(c + 1) * P],
                                           ident[:, :])
                return ins

            def step(s, rep):
                on = stages(rep)
                par = rep % 2
                for i in range(H):
                    if on["B"]:
                        b = s - 1
                        bpar = (rep - 1) % 2
                        if i == 0:
                            pe.wait_ge(qk_in, (b + 1) * 192)
                            if rep == 1:
                                pe.wait_ge(rows_in, 22 * 16)
                        n = b * H + i
                        if rep > 1 or i >= 2:
                            pe.wait_ge(max_ok, n - 1)
                        for t in range(QT):
                            ins = pe.matmul(pS[i % 2][:, t * S:(t + 1) * S], Qs[bpar][0:ROWS_B, i, t * P:(t + 1) * P],
                                            Ks[bpar][0:ROWS_B, i, :], start=True, stop=True)
                        ins.then_inc(s_ok, 1)
                    if mg := m_group(s, rep, i):
                        b, g = mg
                        n = b * NM + g
                        pe.wait_ge(max_ok, (n + 1) * MG)
                        if rep - (1 if i else 2) > 0 or g >= 1:
                            pe.wait_ge(mparts_ok, n)
                        if g == 0 and rep == 1:
                            pe.wait_ge(v_done, 1)
                        if g == 1:
                            if on["R"]:
                                pe.wait_ge(slots_ok, s - 2)
                            else:
                                pe.wait_ge(qk32_ok, s * 4 + 4)
                        if g == 2 and on["D"]:
                            pe.wait_ge(cT_ok, s - 1)
                        if g == 3:
                            if rep >= 3:
                                pe.wait_ge(esig_ok, s - 2)
                            else:
                                pe.wait_ge(v_done, 2)
                        pe.transpose(pF[MBANK[g]][0:MG * QT, 0:P],
                                     nmax[:, g * MG:(g + 1) * MG, :].rearrange("p h t -> p (h t)"), ident[:, :])\
                          .then_inc(mT_ok, 1)
                    if head := c_head(s, rep, i):
                        b, h = head
                        crep = rep - (1 if i >= LAG else 2)
                        cpar = crep % 2
                        n = b * H + h
                        if h % MG == 0:
                            pe.wait_ge(max_in[h // MG], (b + 1) * 16)
                        if crep > 0 or h >= 2:
                            pe.wait_ge(exp_ok, n - 1)
                        for kt in range(QT):
                            ins = pe.matmul(pT[h % 2][:, kt * S:(kt + 1) * S], Ks[cpar][0:ROWS_C, h, kt * P:(kt + 1) * P],
                                            Qs[cpar][0:ROWS_C, h, :], start=True, stop=True)
                        ins.then_inc(sT_ok, 1)
                    back = c_head(s, rep, i - 1) if i else None
                    if i == 0 and rep >= 1:
                        back = c_head(s - 1, rep - 1, H - 1)
                    if back:
                        b, h = back
                        brep = rep - (1 if i - 1 >= LAG else 2) if i else rep - 1 - 1
                        vpar = brep % 2
                        n = b * H + h
                        pe.wait_ge(exp_ok, n + 1)
                        if h == 0:
                            pe.wait_ge(v_done, b + 1)
                            if brep > 0:
                                pe.wait_ge(cn_ok, b)
                        for qt in range(QT):
                            for kt in range(QT):
                                ins = pe.matmul(pC[:, qt, h * (HD + 1):(h + 1) * (HD + 1)],
                                                PT[h % 2][:, kt, qt * P:(qt + 1) * P], V[vpar][:, kt, h, :],
                                                start=(kt == 0), stop=(kt == QT - 1))
                        ins.then_inc(pv_ok, 1)
                    if on["A"] and i == 3:
                        pe.wait_ge(xn_ok, s + 1)
                        if rep >= 3:
                            pe.wait_ge(x2T_ok, (s - 2) * 2)
                        elif rep == 2:
                            pe.wait_ge(mparts_ok, 3)
                        elif rep == 1:
                            pe.wait_ge(qk32_ok, 4)
                        if rep == 0:
                            pe.wait_ge(consts_ok, 1)
                        transpose2(lambda t: xn[:, t, :], pF[0], P).then_inc(xnT_ok, 1)
                    if on["A"] and i == 5:
                        if rep == 0:
                            pe.wait_ge(w_in_sb, NLOADS * 16)
                        pe.wait_ge(xT_ok, s + 1)
                        if rep >= 1:
                            pe.wait_ge(mparts_ok, (s - 1) * NM + 1)
                        for w in range(2):
                            for m in range(2):
                                for c in range(KC):
                                    ins = pe.matmul(pF[1 - w][:, m * S:(m + 1) * S],
                                                    wqk_sb[:, c, w * D + m * P:w * D + (m + 1) * P], xT[:, c, :],
                                                    start=(c == 0), stop=(c == KC - 1))
                            ins.then_inc(qk_ok, 1)
                    if on["A"] and i == 7:
                        pe.wait_ge(qk32_ok, s * 4 + 2)
                        for t in range(QT):
                            for c in range(KC):
                                ins = pe.matmul(pF[1][:, t * D:(t + 1) * D], xT[:, c, t * P:(t + 1) * P],
                                                wv_sb[:, c, :], start=(c == 0), stop=(c == KC - 1))
                        ins.then_inc(v_ok, 1)
                    if on["R"] and i == 6:
                        r = s - 3
                        pe.wait_ge(sel_ok, r + 1)
                        if on["A"]:
                            pe.wait_ge(qk32_ok, s * 4 + 4)
                        else:
                            pe.wait_ge(x2T_ok, (s - 2) * 2)
                        pre = pF[0][:, 0:3 * E]
                        pe.matmul(pre[:, 0:E], before[:, :], M[:, 0, :], start=True, stop=True)
                        pe.matmul(pre[:, E:2 * E], before[:, :], M[:, 1, :], start=True, stop=False)
                        pe.matmul(pre[:, E:2 * E], ones[:, :], M[:, 0, :], start=False, stop=True)
                        pe.matmul(pre[:, 2 * E:3 * E], ones[:, :], M[:, 0, :], start=True, stop=False)
                        pe.matmul(pre[:, 2 * E:3 * E], ones[:, :], M[:, 1, :], start=False, stop=True)\
                          .then_inc(prefix_ok, 1)
                    if on["D"] and i == 10:
                        d = s - 2
                        pe.wait_ge(cn_ok, d + 1)
                        if on["B"]:
                            pe.wait_ge(mparts_ok, (s - 1) * NM + 2)
                        else:
                            pe.wait_ge(slots_ok, s - 2)
                        transpose2(lambda t: cn[:, t, :], pF[0], P).then_inc(cnT_ok, 1)
                    if on["D"] and i == 11:
                        d = s - 2
                        pe.wait_ge(cT_ok, d + 1)
                        if on["A"]:
                            pe.wait_ge(v_done, s + 1)
                        elif on["B"]:
                            pe.wait_ge(mparts_ok, (s - 1) * NM + 1)
                        else:
                            pe.wait_ge(mparts_ok, B * NM)
                        for t in range(QT):
                            for c in range(KC):
                                ins = pe.matmul(pF[1][:, t * D:(t + 1) * D], cT[:, c, t * P:(t + 1) * P],
                                                wo_sb[:, c, :], start=(c == 0), stop=(c == KC - 1))
                        ins.then_inc(wo_ok, 1)
                    if on["D"] and i == 13:
                        pe.wait_ge(x2_ok, s - 2 + 1)
                        if on["B"]:
                            pe.wait_ge(mparts_ok, (s - 1) * NM + 3)
                        transpose2(lambda t: x2[par][:, t, :], pF[0], P).then_inc(x2T_ps, 1)
                    if on["D"] and i == 14:
                        pe.wait_ge(x2T_ok, (s - 2) * 2 + 1)
                        for t in range(QT):
                            for c in range(KC):
                                ins = pe.matmul(pF[1][:, t * E:(t + 1) * E], x2T[:, c, t * P:(t + 1) * P],
                                                gate_sb[:, c, :], start=(c == 0), stop=(c == KC - 1))
                        ins.then_inc(logit_ok, 1)

            pipeline(pe, step)

            pe.wait_ge(x2T_ok, B * 2)
            pe.wait_ge(esig_ok, B)

            def shared_gate_up(n):
                for m in range(ISH // P):
                    due(pe, sh_h_ok, (n - 1) * 2 + m + 1)
                    for w, dst in ((0, pS[m]), (1, pT[m])):
                        for c in range(KC):
                            ins = pe.matmul(dst[:, :], sgu_sb[:, c, w * ISH + m * P:w * ISH + (m + 1) * P],
                                            xT_all[:, c, n * 512:(n + 1) * 512], start=(c == 0), stop=(c == KC - 1))
                    ins.then_inc(sh_gu, 1)

            def shared_down(n):
                pe.wait_ge(sh_h_ok, (n + 1) * 2)
                for k in range(2):
                    due(pe, sh_done, (n - 1) * 2 + k + 1)
                    for t in range(2):
                        for m in range(ISH // P):
                            ins = pe.matmul(pF[k][:, t * D:(t + 1) * D],
                                            sh_h[n % 2][:, m, (2 * k + t) * P:(2 * k + t + 1) * P], sdown_sb[:, m, :],
                                            start=(m == 0), stop=(m == ISH // P - 1))
                    ins.then_inc(sh_y, 1)

            for n in range(T // 512):
                shared_gate_up(n)
                if n:
                    shared_down(n - 1)
            shared_down(T // 512 - 1)

            def rows_t(t, j, g, rep):
                pe.wait_ge(x_in[j], (g + 1) * 16)
                if rep >= 2:
                    pe.wait_ge(tx_ok, t - 1)
                for c in range(KC):
                    ins = pe.transpose(pS[j % 2][:, c * P:(c + 1) * P], x_t[j][:, c * P:(c + 1) * P], ident[:, :])
                ins.then_inc(tT_ok, 1)

            def gate_up(t, j, g, rep):
                pe.wait_ge(w_in[j], (g + 1) * 16)
                pe.wait_ge(tx_ok, t + 1)
                if rep >= 2:
                    pe.wait_ge(th_ok, t - 1)
                for w in range(2):
                    for c in range(KC):
                        ins = pe.matmul(pT[j % 2][:, w * P:(w + 1) * P], w_t[j][:, c * 2 * P + w * P:c * 2 * P + (w + 1) * P],
                                        xT_t[j % 2][:, c * P:(c + 1) * P], start=(c == 0), stop=(c == KC - 1))
                ins.then_inc(tg_ok, 1)

            def down(t, j, rep):
                pe.wait_ge(th_ok, t + 1)
                if rep >= 2:
                    pe.wait_ge(te_ok, t - 1)
                pe.matmul(pF[j % 2][:, 0:D], h_t[j % 2], w_t[j][:, 2 * D:3 * D], start=True, stop=True)\
                  .then_inc(ty_ok, 1)

            pe.wait_ge(sh_done, T // 256)
            for j in range(RING):
                rows_t(j, j, 0, j)
                if j >= 1:
                    gate_up(j - 1, j - 1, 0, j - 1)
                if j >= 2:
                    down(j - 2, j - 2, j - 2)
            with pe.Fori(1, TILES // RING) as g:
                for j in range(RING):
                    rows_t(g * RING + j, j, g, RING)
                    gate_up(g * RING + j - 1, (j - 1) % RING, g if j else g - 1, RING)
                    down(g * RING + j - 2, (j - 2) % RING, RING)
            gate_up(TILES - 1, RING - 1, TILES // RING - 1, RING)
            down(TILES - 2, RING - 2, RING)
            down(TILES - 1, RING - 1, RING)


def kernel(**inputs):
    import concourse.bacc as _bacc
    from concourse.bass_utils import run_bass_kernel_spmd as _run

    a = {n: np.asarray(v) for n, v in inputs.items()}

    def chunks(m):
        return np.ascontiguousarray(m.reshape(-1, P, m.shape[1]).transpose(1, 0, 2))

    f = "L0_ffn_"
    t = "L0_attn_"
    experts = np.empty((E, P, 3 * D), np.float32)
    for c in range(KC):
        experts[:, :, c * D:c * D + P] = a[f + "eg_w"][:, :, c * P:(c + 1) * P].transpose(0, 2, 1)
        experts[:, :, c * D + P:(c + 1) * D] = a[f + "eu_w"][:, :, c * P:(c + 1) * P].transpose(0, 2, 1)
    experts[:, :, 2 * D:] = a[f + "ed_w"].transpose(0, 2, 1)
    arrays = {
        "ids": np.ascontiguousarray(a["x"].reshape(NT, P).T),
        "table": np.concatenate([a[f"L0_tok_tw{i}"] for i in range(4)]),
        "ts": np.concatenate([a[f"L0_tok_ts{i}"] for i in range(4)]),
        "wqk": chunks(np.concatenate([a[t + "Wq"].T, a[t + "Wk"].T], axis=1)),
        "wv": chunks(a[t + "Wv"].T),
        "wo": chunks(a[t + "Wo"].T),
        "bqk": np.ascontiguousarray(np.concatenate([a[t + "bq"], a[t + "bk"]]).reshape(4, P).T),
        "bv": a[t + "bv"].reshape(1, D),
        "bo": a[t + "bo"].reshape(1, D),
        "slopes": a[t + "slopes"].reshape(H, 1),
        "gate": chunks(a[f + "gate_w"].T),
        "gbias": a[f + "gate_bias"].reshape(1, E),
        "experts": experts.reshape(E * P, 3 * D),
        "sgu": chunks(np.concatenate([a[f + "sg_w"].T, a[f + "su_w"].T], axis=1)),
        "sdown": chunks(a[f + "sd_w"].T),
    }
    nc = _bacc.Bacc("TRN2", target_bir_lowering=False, num_devices=1)
    args = [nc.dram_tensor(f"in_{n}", v.shape, mybir.dt.from_np(v.dtype), kind="ExternalInput").ap()
            for n, v in arrays.items()]
    out = nc.dram_tensor("out_dram", (T, D), F32, kind="ExternalOutput").ap()
    tower(nc, *args, out)
    r = _run(nc, [{f"in_{n}": v for n, v in arrays.items()}], core_ids=[0])
    return r.results[0]["out_dram"].reshape(B, S, D)
```

```python
from contextlib import ExitStack

import numpy as np

import concourse.bass as bass
from concourse import mybir

F32, BF16, I32, U32 = mybir.dt.float32, mybir.dt.bfloat16, mybir.dt.int32, mybir.dt.uint32
ALU = mybir.AluOpType
ACT = mybir.ActivationFunctionType
AX_X = mybir.AxisListType.X
RMAX = bass.bass_isa.ReduceOp.max

P = 128
B, S, D, H, HD = 8, 256, 256, 16, 16
T = B * S
NT = T // P
QT = S // P
KC = D // P
E, INTER, TOPK, G, TG = 64, 128, 6, 8, 4
VW = 32
ISH = 256
EPS = 1e-5
TIERS = (64, 512, 4096, 50257)
MAXQ = (127.0, 31.0, 7.0)
ROUND = 12582912.0

SPLIT = 6 * HD
ROWS_B = SPLIT + 6
ROWS_C = ROWS_B + 1
Q_PARTS = (0, 0, 0, 1, 1, 2)
K_PARTS = (0, 1, 2, 0, 1, 0)

SCAN_ROWS = 15
SCAN_RING = 6
N3 = (TIERS[3] - TIERS[2]) // P
REST3 = TIERS[3] - TIERS[2] - N3 * P
CHUNKS = N3 // SCAN_ROWS
assert CHUNKS * SCAN_ROWS == N3 and CHUNKS % SCAN_RING == 0

ROW = 272
TOKCOL, SLOTCOL, WCOL = 256, 257, 263
CAP = T + P
TILES = E + (T * TOPK - E) // P + 1
SP_PADS, ACT_PADS = 28, 16
RING = 8
TILES = -(-TILES // RING) * RING
NACC = 4
MG = 4
LAG = 8
RACC = T + P
LINKS_A, LINKS_D, LINKS_R = 7, 4, 23
HEAD0 = 2
T1P = (TIERS[1] - TIERS[0]) // 4
MBANK = (1, 0, 0, 1)
NLOADS = 14
WROW = 3 * D


def tower(nc, ids, table, ts, wqk, wv, wo, bqk, bv, bo, slopes, gate, gbias, experts, sgu, sdown, out):
    with ExitStack() as ctx:
        def sb(name, shape, dt=F32):
            return ctx.enter_context(nc.sbuf_tensor(name, shape, dt))

        def ps(name, shape, dt=F32):
            return ctx.enter_context(nc.psum_tensor(name, shape, dt))

        def sem(name):
            return ctx.enter_context(nc.semaphore(name))

        qk_scr = nc.dram_tensor("qk_scr", [2, 3, 2, D, S], BF16).ap()
        rows_scr = nc.dram_tensor("rows_scr", [6, H * S], BF16).ap()
        max_scr = nc.dram_tensor("max_scr", [2, H * S], BF16).ap()
        xT_scr = nc.dram_tensor("xT_scr", [B, P, KC * S], F32).ap()
        xs = nc.dram_tensor("xs", [E * CAP, ROW], F32).ap()
        acc_scr = [nc.dram_tensor(f"acc_scr{i}", [RACC, D], F32).ap() for i in range(NACC)]
        tile_scr = nc.dram_tensor("tile_scr", [2, P], F32).ap()

        ident = sb("ident", [P, P])
        before = sb("before", [P, P], BF16)
        ones = sb("ones", [P, P], BF16)
        zeros = sb("zeros", [P, RACC * D // P // 4])
        padrow = sb("padrow", [P, ROW])
        part_i = sb("part_i", [P, 2], I32)
        part_f = sb("part_f", [P, 3])
        tok_u = sb("tok_u", [P, NT], I32)
        eidx = sb("eidx", [P, E])
        ebase = sb("ebase", [P, E])
        iota_i = sb("iota_i", [P, S], I32)
        lower = sb("lower", [P, G, G])
        wqk_sb = sb("wqk_sb", [P, KC, 2 * D])
        wv_sb = sb("wv_sb", [P, KC, D])
        wo_sb = sb("wo_sb", [P, KC, D])
        gate_sb = sb("gate_sb", [P, KC, E])
        gbias_sb = sb("gbias_sb", [P, E])
        bqk_sb = sb("bqk_sb", [P, 4])
        bv_sb = sb("bv_sb", [P, KC])
        bo_sb = sb("bo_sb", [P, D])
        tsb = sb("tsb", [P, 4, D])
        half = sb("half", [P, QT])
        sparts = sb("sparts", [H, 4], BF16)

        ids_sb = sb("ids_sb", [P, NT], I32)
        tier_u = sb("tier_u", [P, NT], U32)
        idf = sb("idf", [P, NT])
        ge = sb("ge", [P, 4, NT])
        intier = sb("intier", [P, 3, NT])
        maxq = sb("maxq", [P, NT])
        nmaxq = sb("nmaxq", [P, NT])
        scale = sb("scale", [P, NT])
        inv = sb("inv", [P, NT])
        emb = sb("emb", [P, NT, D])
        tsel = sb("tsel", [P, NT, D])
        ring = sb("ring", [P, SCAN_RING, SCAN_ROWS, D])
        flat = ring[:, :, :, :].rearrange("p a b d -> p (a b d)")
        taken = [0]

        def carve(n):
            taken[0] += n
            assert taken[0] <= SCAN_RING * SCAN_ROWS * D
            return flat[:, taken[0] - n:taken[0]]

        cmax = sb("cmax", [P, 3, D])
        cnew = sb("cnew", [P, D])
        pmax = sb("pmax", [P, 4])
        amax = sb("amax", [P, 4])
        sc3 = sb("sc3", [P, 4])

        xq = carve(QT * D).rearrange("p (t d) -> p t d", t=QT)
        stats = sb("stats", [P, QT, 6])
        mv = sb("mv", [P, QT, 2])
        mv_eps = sb("mv_eps", [P, 2, QT])
        rstd = sb("rstd", [P, 2, QT])
        xn = carve(QT * D).rearrange("p (t d) -> p t d", t=QT)
        xT = sb("xT", [P, KC, S])
        qk32 = carve(4 * S).rearrange("p (m s) -> p m s", m=4)
        qkr = carve(4 * S).rearrange("p (m s) -> p m s", m=4)
        parts = sb("parts", [P, 3, 4, S], BF16)
        at = taken[0]
        Qs = [carve(H * S // 2).bitcast(BF16).rearrange("p (h s) -> p h s", h=H) for _ in range(2)]
        Ks = [carve(H * S // 2).bitcast(BF16).rearrange("p (h s) -> p h s", h=H) for _ in range(2)]
        fin = [flat[:, at + i * NACC * 4 * D:at + (i + 1) * NACC * 4 * D].rearrange("p (a n d) -> p a n d", a=NACC, n=4)
               for i in range(2)]
        V = [sb(f"V{i}", [P, QT, H, VW]) for i in range(2)]
        slope_in = sb("slope_in", [H, 4])
        pos_f = sb("pos_f", [H, S])
        onesrow = sb("onesrow", [H, S])
        slope_p = sb("slope_p", [H, 3, S], BF16)
        pos_p = sb("pos_p", [H, 3, S], BF16)
        nmax = sb("nmax", [P, H, QT])
        mrows = [sb(f"mrows{i}", [MG * QT, P], BF16) for i in range(2)]
        PT = [sb(f"PT{i}", [P, QT, S]) for i in range(2)]
        rsum = sb("rsum", [P, QT, H])
        cn = carve(QT * D).rearrange("p (t d) -> p t d", t=QT)
        ctx_sb = carve(512)
        cT = sb("cT", [P, KC, S])

        stats2 = sb("stats2", [P, QT, 6])
        mv2 = sb("mv2", [P, QT, 2])
        mv2_eps = sb("mv2_eps", [P, 2, QT])
        xo = carve(QT * D).rearrange("p (t d) -> p t d", t=QT)
        rstd2 = sb("rstd2", [P, 2, QT])
        x2 = [sb(f"x2_{i}", [P, QT, ROW]) for i in range(2)]
        x2T = sb("x2T", [P, KC, S])
        esig = sb("esig", [P, QT, E])
        score = sb("score", [P, QT, E])
        gs = sb("gs", [P, QT, G])
        cmp_a = sb("cmp_a", [P, QT, G, G])
        cmp_b = sb("cmp_b", [P, QT, G, G])
        gmask = sb("gmask", [P, QT, G])
        ms = sb("ms", [P, QT, E])
        top = sb("top", [P, QT, 8])
        topi = sb("topi", [P, QT, 8], U32)
        lastf = sb("lastf", [P, QT])
        wsum = sb("wsum", [P, QT])
        tie = sb("tie", [P, QT, E])
        M = sb("M", [P, QT, E], BF16)
        wn = sb("wn", [P, QT, E])
        key = sb("key", [P, QT, E])
        topk = sb("topk", [P, QT, 8])
        eq = sb("eq", [P, QT, TOPK, E])
        run = sb("run", [P, E])
        slot_u = [sb(f"slot_u{i}", [P, QT, TOPK], U32) for i in range(2)]

        nt_e = sb("nt_e", [P, E])
        end_e = sb("end_e", [P, E])
        one_e = sb("one_e", [P, E])
        pad_e = sb("pad_e", [P, E])
        tsc = sb("tsc", [P, 2, E])
        tinfo = sb("tinfo", [P, 2, 6])
        padreg = sb("padreg", [P, E], I32)
        treg_f = sb("treg_f", [1, 2 * P])
        treg = sb("treg", [1, 2 * P], I32)
        tslot = sb("tslot", [P, 2 * P])
        sgu_sb = sb("sgu_sb", [P, KC, 2 * ISH])
        sdown_sb = sb("sdown_sb", [P, ISH // P, D])

        w_t = [flat[:, at + i * WROW:at + (i + 1) * WROW] for i in range(RING)]
        assert RING * WROW <= 2 * H * S
        x_t = [carve(ROW) for _ in range(RING)]
        y_t = [carve(D) for _ in range(RING)]
        xT_t = [carve(KC * P) for _ in range(2)]
        sg_t = [carve(P) for _ in range(2)]
        h_t = [carve(P) for _ in range(2)]
        wt_t = [carve(4) for _ in range(RING)]
        eq_t = [carve(8) for _ in range(RING)]
        sh_g = [carve(512) for _ in range(2)]
        sh_h = [carve(ISH // P * 512).rearrange("p (m t) -> p m t", m=ISH // P) for _ in range(2)]
        xT_all = tsel[:, :, :].rearrange("p n d -> p (n d)").rearrange("p (c t) -> p c t", c=KC)

        pS = [ps(f"pS{i}", [P, 512]) for i in range(2)]
        pT = [ps(f"pT{i}", [P, 512]) for i in range(2)]
        pC = ps("pC", [P, 2, 512])
        pF = [ps(f"pF{i}", [P, 512]) for i in range(2)]

        consts_p = sem("consts_p")
        consts_ok = sem("consts_ok")
        ids_in = sem("ids_in")
        w_in_sb = sem("w_in_sb")
        slope_in_s = sem("slope_in_s")
        emb_in = sem("emb_in")
        ts_in = sem("ts_in")
        tier_ok = sem("tier_ok")
        ring_in = [sem(f"ring_in{i}") for i in range(SCAN_RING)]
        ring_used = sem("ring_used")
        scan_v = sem("scan_v")
        pmax_ok = sem("pmax_ok")
        amax_ok = sem("amax_ok")
        bias_ok = sem("bias_ok")
        set_v = sem("set_v")
        rows_ok = sem("rows_ok")
        rows_out = sem("rows_out")
        rows_in = sem("rows_in")
        zero_out = sem("zero_out")

        chain_a, chain_d, chain_r = sem("chain_a"), sem("chain_d"), sem("chain_r")
        var_ok = sem("var_ok")
        rstd_ok = sem("rstd_ok")
        xn_ok = sem("xn_ok")
        xnT_ok = sem("xnT_ok")
        xT_ok = sem("xT_ok")
        qk_ok = sem("qk_ok")
        qk32_ok = sem("qk32_ok")
        rest_ok = sem("rest_ok")
        part1_ok = sem("part1_ok")
        part2_ok = sem("part2_ok")
        qk_out = [sem(f"qk_out{i}") for i in range(3)]
        qk_in = sem("qk_in")
        v_ok = sem("v_ok")
        v_done = sem("v_done")
        s_ok = sem("s_ok")
        max_ok = sem("max_ok")
        mT_ok = sem("mT_ok")
        mrows_ok = sem("mrows_ok")
        max_out = sem("max_out")
        max_in = [sem(f"max_in{g}") for g in range(H // MG)]
        sT_ok = sem("sT_ok")
        exp_ok = sem("exp_ok")
        pv_ok = sem("pv_ok")
        ctx_ok = sem("ctx_ok")
        half_ok = sem("half_ok")
        cn_ok = sem("cn_ok")
        cnT_ok = sem("cnT_ok")
        cT_ok = sem("cT_ok")
        wo_ok = sem("wo_ok")
        embo_ok = sem("embo_ok")
        res_ok = sem("res_ok")
        var2_ok = sem("var2_ok")
        rstd2_ok = sem("rstd2_ok")
        x2_ok = sem("x2_ok")
        x2T_ps = sem("x2T_ps")
        x2T_ok = sem("x2T_ok")
        logit_ok = sem("logit_ok")
        esig_ok = sem("esig_ok")
        sel_ok = sem("sel_ok")
        prefix_ok = sem("prefix_ok")
        prefix_used = sem("prefix_used")
        slots_ok = sem("slots_ok")
        scat_ok = [sem(f"scat_ok{i}") for i in range(2)]

        chain_t = sem("chain_t")
        tinfo_ok = sem("tinfo_ok")
        tinfo_out = sem("tinfo_out")
        tinfo_in = sem("tinfo_in")
        padreg_ok = sem("padreg_ok")
        treg_ok = sem("treg_ok")
        tslot_ok = sem("tslot_ok")
        pad_out = sem("pad_out")
        pad_out_a = sem("pad_out_a")
        pad_out_p = sem("pad_out_p")
        sh_gu = sem("sh_gu")
        sh_silu = sem("sh_silu")
        sh_h_ok = sem("sh_h_ok")
        sh_y = sem("sh_y")
        sh_done = sem("sh_done")
        w_in = [sem(f"w_in{i}") for i in range(RING)]
        x_in = [sem(f"x_in{i}") for i in range(RING)]
        tT_ok = sem("tT_ok")
        tx_ok = sem("tx_ok")
        tw_ok = sem("tw_ok")
        tg_ok = sem("tg_ok")
        ts_ok = sem("ts_ok")
        th_ok = sem("th_ok")
        ty_ok = sem("ty_ok")
        te_ok = sem("te_ok")
        acc_ok = [sem(f"acc_ok{i}") for i in range(RING)]
        fin_in = [sem(f"fin_in{i}") for i in range(2)]
        fin_v = sem("fin_v")
        fin_ok = sem("fin_ok")
        out_done = sem("out_done")

        passed = {nc.sync: sem("passed_sp"), nc.scalar: sem("passed_act"), nc.gpsimd: sem("passed_pool"), nc.vector: sem("passed_dve")}
        block = ctx.enter_context(nc.Block())

        def apart(eng):
            eng.sem_inc(passed[eng], 1)

        def due(eng, s, value):
            if not isinstance(value, int) or value > 0:
                eng.wait_ge(s, value)

        class Chain:

            def __init__(self, eng, s, per):
                self.eng, self.s, self.per, self.base, self.n = eng, s, per, 0, 0

            def start(self, batch):
                assert self.n in (0, self.per), (self.n, self.per)
                self.base, self.n = batch * self.per, 0

            def link(self, ins):
                self.n += 1
                ins.then_inc(self.s, 1)
                self.eng.wait_ge(self.s, self.base + self.n)

        STEPS = B + 3
        LOOP = (4, B)
        assert (LOOP[1] - LOOP[0]) % 2 == 0

        def stages(rep):
            return {k: 0 <= rep - lag < B for k, lag in (("A", 0), ("B", 1), ("D", 2), ("R", 3), ("S", 4))}

        def c_head(s, rep, i):
            lag, h = (1, i - LAG) if i >= LAG else (2, i + H - LAG)
            return (s - lag, h) if 0 <= rep - lag < B else None

        def pipeline(eng, step):
            for s in range(LOOP[0]):
                step(s, s)
            with eng.Fori(LOOP[0], LOOP[1] - 1, 2) as s:
                step(s, LOOP[0])
                step(s + 1, LOOP[0] + 1)
            for s in range(LOOP[1], STEPS):
                step(s, s)

        def m_group(s, rep, i):
            if i % MG:
                return None
            lag, g = (1, i // MG - 1) if i else (2, H // MG - 1)
            return (s - lag, g) if 0 <= rep - lag < B else None

        NM = H // MG
        CLEARING = (1, 2, 3, 8)
        assert len(CLEARING) == NACC

        def pad_lists(eng, first, end, done):
            with eng.Fori(first, end - 3, 4) as e:
                for k in range(4):
                    row = eng.value_load(padreg[0:1, bass.ds(e + k, 1)], min_val=0, max_val=E * CAP - P)
                    eng.dma_start(xs[bass.ds(row, P), :], padrow[:, :]).then_inc(done, 16)

        @block.sync
        def _(sp):
            sp.dma_start(ids_sb[:, :], ids).then_inc(ids_in, 16)

            def chunk(slot, src, parts, rows):
                sp.dma_start(ring[0:parts, slot, 0:rows, :], src).then_inc(ring_in[slot], 16)

            t2 = table[TIERS[1]:TIERS[2], :].rearrange("(p n) d -> p n d", p=P)
            half2 = t2.shape[1] // 2
            chunk(HEAD0, t2[:, 0:half2, :], P, half2)
            chunk(HEAD0 + 1, t2[:, half2:, :], P, half2)
            chunk(HEAD0 + 2, table[TIERS[0]:TIERS[1], :].rearrange("(p n) d -> p n d", n=4), T1P, 4)
            chunk(HEAD0 + 3, table[TIERS[3] - REST3:TIERS[3], :].rearrange("(p n) d -> p n d", n=1), REST3, 1)
            for dst, src in ((wqk_sb, wqk), (wv_sb, wv), (wo_sb, wo), (gate_sb, gate), (sgu_sb, sgu),
                             (sdown_sb, sdown)):
                sp.dma_start(dst[:, :, :], src).then_inc(w_in_sb, 16)
            sp.dma_start(bqk_sb[:, :], bqk).then_inc(w_in_sb, 16)
            sp.dma_start(bv_sb[:, :], bv).then_inc(w_in_sb, 16)
            for dst, src in ((bo_sb, bo), (gbias_sb, gbias)):
                sp.dma_start(dst[:, :], src.broadcast_to([P, src.shape[1]])).then_inc(w_in_sb, 16)
            for i in range(4):
                sp.dma_start(tsb[:, i, :], ts[i:i + 1, :].broadcast_to([P, D])).then_inc(w_in_sb, 16)
            sp.dma_start(slope_in[:, 0:1], slopes).then_inc(slope_in_s, 16)

            t3 = table[TIERS[2]:TIERS[3] - REST3, :].rearrange("(p n) d -> p n d", p=P)
            def turn(i):
                for j in range(SCAN_RING):
                    if not isinstance(i, int) or j >= HEAD0:
                        sp.wait_ge(ring_used, i * SCAN_RING + j + 1 - HEAD0)
                    chunk(j, t3[:, bass.ds((i * SCAN_RING + j) * SCAN_ROWS, SCAN_ROWS), :], P, SCAN_ROWS)

            turn(0)
            with sp.Fori(1, CHUNKS // SCAN_RING) as i:
                turn(i)

            sp.wait_ge(rows_ok, 2)
            sp.dma_start(rows_scr[0:3, :].rearrange("i (h s) -> h i s", h=H), slope_p[:, :, :]).then_inc(rows_out, 16)
            sp.dma_start(rows_scr[3:6, :].rearrange("i (h s) -> h i s", h=H), pos_p[:, :, :]).then_inc(rows_out, 16)
            sp.wait_ge(rows_out, 32)
            sp.wait_ge(pmax_ok, 1)
            for par in range(2):
                q_rows = Qs[par][:, :, :].rearrange("p h s -> p (h s)")
                k_rows = Ks[par][:, :, :].rearrange("p h s -> p (h s)")
                sp.dma_start(q_rows[SPLIT:SPLIT + 3, :], rows_scr[0:3, :]).then_inc(rows_in, 16)
                sp.dma_start(k_rows[SPLIT + 3:SPLIT + 6, :], rows_scr[0:3, :]).then_inc(rows_in, 16)
                for dst, row, src in ([(q_rows, SPLIT + 3 + i, 3) for i in range(3)] +
                                      [(k_rows, SPLIT + i, 4) for i in range(3)] + [(k_rows, ROWS_B, 5)]):
                    sp.dma_start(dst[row:row + 1, :], rows_scr[src:src + 1, :]).then_inc(rows_in, 16)
            quarter = RACC // P * D // 4

            def clear(a):
                for i in range(4):
                    dst = acc_scr[a].rearrange("(p n) d -> p (n d)", p=P)[:, i * quarter:(i + 1) * quarter]
                    sp.dma_start(dst, zeros[:, :]).then_inc(zero_out, 16)

            def step(s, rep):
                on = stages(rep)
                par = rep % 2
                for i in range(H):
                    if mg := m_group(s, rep, i):
                        b, g = mg
                        mpar = (rep - (1 if i else 2)) % 2
                        sp.wait_ge(mrows_ok, b * NM + g + 1)
                        apart(sp)
                        due(sp, max_in[g], (b - 1) * 16)
                        dst = max_scr[mpar:mpar + 1, g * MG * S:(g + 1) * MG * S]
                        sp.dma_start(dst.rearrange("i (r q) -> (i r) q", q=P), mrows[g % 2][:, :]).then_inc(max_out, 16)
                        sp.wait_ge(max_out, (b * NM + g + 1) * 16)
                        rows = Qs[mpar][ROWS_B:ROWS_C, g * MG:(g + 1) * MG, :]
                        sp.dma_start(rows.rearrange("p h s -> p (h s)"), dst).then_inc(max_in[g], 16)
                    if on["A"]:
                        move_parts(s, rep, par, i)
                    if i == 12 and rep in CLEARING:
                        if rep == CLEARING[0]:
                            sp.wait_ge(consts_ok, 1)
                        clear(CLEARING.index(rep))

            def move_parts(s, rep, par, i):
                dst = qk_scr[par].rearrange("r w (c p) s -> p r (w c) s", p=P)
                if i == 8:
                    sp.wait_ge(qk32_ok, s * 4 + 4)
                    apart(sp)
                    due(sp, qk_in, (s - 1) * 192 if rep >= 2 else 0)
                    sp.dma_start(dst[:, 0], parts[:, 0, :, :]).then_inc(qk_out[0], 16)
                    if rep >= 2:
                        sp.wait_ge(sT_ok, (s - 1) * H)
                        apart(sp)
                if i in (9, 10):
                    r = i - 8
                    sp.wait_ge((part1_ok, part2_ok)[r - 1], s + 1)
                    sp.dma_start(dst[:, r], parts[:, r, :, :]).then_inc(qk_out[r], 16)
                if i in (9, 10, 11):
                    r = i - 9
                    sp.wait_ge(qk_out[r], (s + 1) * 16)
                    for w, (to, blocks) in enumerate(((Qs[par], Q_PARTS), (Ks[par], K_PARTS))):
                        for j, part in enumerate(blocks):
                            if part == r:
                                sp.dma_start(to[j * HD:(j + 1) * HD, :, :],
                                             qk_scr[par, r, w].rearrange("(h d) s -> d h s", d=HD))\
                                  .then_inc(qk_in, 16)

            pipeline(sp, step)

            sp.wait_ge(padreg_ok, 1)
            sp.dma_start(xs[E * CAP - P:E * CAP, :], padrow[:, :]).then_inc(pad_out, 16)
            pad_lists(sp, 0, 12, pad_out)
            sp.wait_ge(tinfo_ok, 1)
            for c in range(2):
                sp.dma_start(tile_scr[c:c + 1, :].rearrange("c p -> p c"), tinfo[:, c, 4:5],
                             allow_slow_non_contiguous=True).then_inc(tinfo_out, 16)
            pad_lists(sp, 12, 20, pad_out)
            sp.wait_ge(tinfo_out, 32)
            row = tile_scr.rearrange("c p -> (c p)").rearrange("(o x) -> o x", o=1)
            sp.dma_start(treg_f[:, :], row).then_inc(tinfo_in, 16)
            sp.dma_start(tslot[:, :], row.broadcast_to([P, 2 * P])).then_inc(tinfo_in, 16)
            pad_lists(sp, 20, SP_PADS, pad_out)

            def load_tile(t, j, g, rep):
                first = sp.value_load(treg[0:1, bass.ds(t, 1)], min_val=0, max_val=E * CAP - P)
                if rep:
                    sp.wait_ge(acc_ok[j], g * 16)
                    apart(sp)
                    sp.wait_ge(tw_ok, t - RING + 1)
                sp.dma_start(x_t[j], xs[bass.ds(first, P), :]).then_inc(x_in[j], 16)
                if rep:
                    sp.wait_ge(ty_ok, t - RING + 1)
                    apart(sp)
                sp.dma_start(w_t[j], experts[bass.ds((first // CAP) * P, P), :]).then_inc(w_in[j], 16)

            sp.wait_ge(treg_ok, 1)
            sp.wait_ge(pad_out, (SP_PADS + 1) * 16)
            sp.wait_ge(pad_out_a, ACT_PADS * 16)
            sp.wait_ge(pad_out_p, (E - SP_PADS - ACT_PADS) * 16)
            for i in range(2):
                sp.wait_ge(scat_ok[i], B // 2 * QT * TOPK * 16)
            for j in range(RING):
                load_tile(j, j, 0, False)
            with sp.Fori(1, TILES // RING) as g:
                for j in range(RING):
                    load_tile(g * RING + j, j, g, True)

            for j in range(RING):
                sp.wait_ge(acc_ok[j], TILES // RING * 16)
            for n in range(NT // 4):
                if n >= 2:
                    sp.wait_ge(fin_ok, n - 1)
                for a in range(NACC):
                    sp.dma_start(fin[n % 2][:, a],
                                 acc_scr[a][n * 512:(n + 1) * 512, :].rearrange("(n p) d -> p n d", p=P))\
                      .then_inc(fin_in[n % 2], 16)
            for n in range(NT // 4):
                sp.wait_ge(fin_ok, n + 1)
                sp.dma_start(out[n * 512:(n + 1) * 512, :].rearrange("(n p) d -> p n d", p=P),
                             emb[:, n * 4:(n + 1) * 4, :]).then_inc(out_done, 16)
            sp.wait_ge(out_done, NT // 4 * 16)

        @block.gpsimd
        def _(pool):
            n_c = [0]

            def const(ins):
                n_c[0] += 1
                ins.then_inc(consts_p, 1)
                pool.wait_ge(consts_p, n_c[0])

            pool.wait_ge(ids_in, 16)
            for j in range(NT):
                pool.indirect_dma_start(emb[:, j, :], None, table,
                                        bass.IndirectOffsetOnAxis(ids_sb[:, j:j + 1].bitcast(U32), 0))\
                    .then_inc(emb_in, 16)
            pool.wait_ge(tier_ok, 1)
            for j in range(NT):
                pool.indirect_dma_start(tsel[:, j, :], None, ts,
                                        bass.IndirectOffsetOnAxis(tier_u[:, j:j + 1], 0)).then_inc(ts_in, 16)
            for t, v in ((ident, 0.0), (before, 0.0), (ones, 1.0), (zeros, 0.0), (padrow, 0.0), (lower, 0.0),
                         (half, -0.5), (one_e, 1.0), (run, 0.0), (onesrow, 1.0)):
                const(pool.memset(t[tuple(slice(None) for _ in t.shape)], v))
            const(pool.affine_select(out=ident[:, :], in_=ident[:, :], compare_op=ALU.not_equal, fill=1.0,
                                     base=0, pattern=[[-1, P]], channel_multiplier=1))
            const(pool.affine_select(out=before[:, :], in_=before[:, :], compare_op=ALU.is_ge, fill=1.0,
                                     base=0, pattern=[[-1, P]], channel_multiplier=1))
            const(pool.affine_select(out=lower[:, :, :], in_=lower[:, :, :], compare_op=ALU.is_ge, fill=1.0,
                                     base=0, pattern=[[-1, G], [1, G]], channel_multiplier=0))
            const(pool.iota(part_i[:, :], pattern=[[P, 2]], base=0, channel_multiplier=1))
            const(pool.tensor_copy(part_f[:, 0:2], part_i[:, :]))
            const(pool.iota(tok_u[:, :], pattern=[[P, NT]], base=0, channel_multiplier=1))
            const(pool.iota(iota_i[:, 0:E], pattern=[[1, E]], base=0, channel_multiplier=0))
            const(pool.tensor_copy(eidx[:, :], iota_i[:, 0:E]))
            const(pool.tensor_scalar(ebase[:, :], eidx[:, :], float(CAP), 1.0, ALU.mult, ALU.add))
            const(pool.iota(iota_i[:, :], pattern=[[1, S]], base=0, channel_multiplier=0))
            const(pool.tensor_copy(pos_f[:, :], iota_i[0:H, :]))
            const(pool.tensor_scalar(part_f[:, 2:3], part_f[:, 0:1], 1.0, None, ALU.add))
            const(pool.iota(padrow[:, TOKCOL:TOKCOL + 1].bitcast(I32), pattern=[[0, 1]], base=T,
                            channel_multiplier=1))
            for par in range(2):
                const(pool.memset(V[par][:, :, :, HD:HD + 1], 1.0))
                const(pool.memset(V[par][:, :, :, HD + 1:VW], 0.0))
                const(pool.memset(x2[par][:, :, WCOL + TOPK:ROW], 0.0))
            pool.memset(iota_i[:, 0:1], 0).then_inc(consts_ok, 1)

            pool.wait_ge(pmax_ok, 1)
            pool.partition_all_reduce(amax[:, 0:3], pmax[:, 0:3], P, RMAX).then_inc(amax_ok, 1)

            def factors(b, of, to, done):
                pool.tensor_tensor(to[:, 0, :], of[:, 0, :], half[:, :], ALU.pow).then_inc(done, 1)
                pool.wait_ge(done, 2 * b + 1)
                pool.tensor_tensor(to[:, 1, :], of[:, 1, :], to[:, 0, :], ALU.mult).then_inc(done, 1)

            def scatters(r, rep, ks):
                rpar = rep % 2
                for t in range(QT):
                    for k in ks:
                        pool.indirect_dma_start(xs[:, :],
                                                bass.IndirectOffsetOnAxis(slot_u[rpar][:, t, k:k + 1], 0),
                                                x2[rpar][:, t, :], None).then_inc(scat_ok[rpar], 16)

            def step(s, rep):
                on = stages(rep)
                if on["S"]:
                    pool.wait_ge(slots_ok, s - 4 + 1)
                    pool.wait_ge(x2_ok, s - 4 + 1)
                    apart(pool)
                    scatters(s - 4, rep - 4, range(0, 4))
                if on["A"]:
                    pool.wait_ge(var_ok, s + 1)
                    if rep >= 1:
                        pool.wait_ge(xn_ok, s)
                    factors(s, mv_eps, rstd, rstd_ok)
                if on["S"]:
                    scatters(s - 4, rep - 4, range(4, TOPK))
                if on["A"]:
                    pool.wait_ge(qk32_ok, s * 4 + 4)
                    if rep >= 1:
                        pool.wait_ge(part1_ok, s)
                    pool.tensor_tensor(qkr[:, :, :], qk32[:, :, :], parts[:, 0], ALU.subtract).then_inc(rest_ok, 1)
                    pool.wait_ge(part1_ok, s + 1)
                    if rep >= 1:
                        pool.wait_ge(qk_out[2], s * 16)
                    pool.tensor_tensor(parts[:, 2], qkr[:, :, :], parts[:, 1], ALU.subtract).then_inc(part2_ok, 1)
                if on["D"]:
                    if rep >= 3:
                        pool.wait_ge(res_ok, s - 2)
                    apart(pool)
                    pool.tensor_tensor(xo[:, :, :], emb[:, bass.ds((s - 2) * QT, QT), :],
                                       bo_sb[:, :].unsqueeze(1).broadcast_to([P, QT, D]), ALU.add).then_inc(embo_ok, 1)
                    pool.wait_ge(var2_ok, s - 2 + 1)
                    if rep >= 3:
                        pool.wait_ge(x2_ok, s - 2)
                    factors(s - 2, mv2_eps, rstd2, rstd2_ok)

            pipeline(pool, step)
            pool.wait_ge(slots_ok, B)
            pool.wait_ge(x2_ok, B)
            scatters(B - 1, B - 1, range(TOPK))

            def accumulate(g, j, rep):
                pool.wait_ge(te_ok, g * RING + j + 1)
                if j >= NACC:
                    pool.wait_ge(acc_ok[j - NACC], (g + 1) * 16)
                elif rep:
                    pool.wait_ge(acc_ok[j - NACC + RING], g * 16)
                apart(pool)
                pool.indirect_dma_start(acc_scr[j % NACC], bass.IndirectOffsetOnAxis(
                    x_t[j][:, TOKCOL:TOKCOL + 1].bitcast(U32), 0), y_t[j], None, compute_op=ALU.add)\
                    .then_inc(acc_ok[j], 16)

            pool.wait_ge(padreg_ok, 1)
            pad_lists(pool, SP_PADS + ACT_PADS, E, pad_out_p)

            pool.wait_ge(zero_out, NACC * 4 * 16)
            for j in range(RING):
                accumulate(0, j, False)
            with pool.Fori(1, TILES // RING) as g:
                for j in range(RING):
                    accumulate(g, j, True)

        @block.scalar
        def _(act):
            def step(s, rep):
                on = stages(rep)
                for i in range(H):
                    if mg := m_group(s, rep, i):
                        b, g = mg
                        n = b * NM + g
                        act.wait_ge(mT_ok, n + 1)
                        if rep - (1 if i else 2) > 0 or g >= 2:
                            act.wait_ge(max_out, (n - 1) * 16)
                        act.activation(mrows[g % 2][:, :], pF[MBANK[g]][0:MG * QT, 0:P], ACT.Copy).then_inc(mrows_ok, 1)
                    if head := c_head(s, rep, i):
                        b, h = head
                        n = b * H + h
                        first = rep - (1 if i >= LAG else 2) == 0
                        act.wait_ge(sT_ok, n + 1)
                        if not (first and h < 2):
                            act.wait_ge(pv_ok, n - 1)
                        act.activation(PT[h % 2][:, :, :].rearrange("p k q -> p (k q)"), pT[h % 2][:, :],
                                       ACT.Exp).then_inc(exp_ok, 1)
                    if on["D"] and i in (1, 8):
                        k = 2 * (s - 2) + (i == 8)
                        act.wait_ge(pv_ok, (k + 1) * (H // 2))
                        if rep > 2 or i == 8:
                            act.wait_ge(half_ok, k)
                        act.activation(ctx_sb, pC[:, int(i == 8), :], ACT.Copy).then_inc(ctx_ok, 1)
                    if on["A"] and i == 4:
                        act.wait_ge(rstd_ok, 2 * (s + 1))
                        apart(act)
                        for t in range(QT):
                            ins = act.activation(xn[:, t, :], emb[:, bass.ds(s * QT + t, 1), :].rearrange("p o d -> p (o d)"),
                                                 ACT.Identity, bias=rstd[:, 1, t:t + 1], scale=rstd[:, 0, t:t + 1])
                        ins.then_inc(xn_ok, 1)
                    if on["A"] and i == 9:
                        act.wait_ge(v_ok, s + 1)
                        if rep >= 2:
                            act.wait_ge(pv_ok, (s - 1) * H)
                        act.activation(V[rep % 2][:, :, :, 0:HD], pF[1][:, :].rearrange("p (t h d) -> p t h d", t=QT, h=H),
                                       ACT.Copy).then_inc(v_done, 1)
                    if on["A"] and i == 5:
                        act.wait_ge(xnT_ok, s + 1)
                        act.activation(xT[:, :, :].rearrange("p c t -> p (c t)"), pF[0][:, :], ACT.Copy)\
                            .then_inc(xT_ok, 1)
                    if on["A"] and i == 6:
                        if rep >= 1:
                            act.wait_ge(part2_ok, s)
                            act.wait_ge(qk_out[0], s * 16)
                        for w in range(2):
                            act.wait_ge(qk_ok, s * 2 + w + 1)
                            for m in range(2):
                                mm = 2 * w + m
                                for dst in (qk32[:, mm, :], parts[:, 0, mm, :]):
                                    ins = act.activation(dst, pF[1 - w][:, m * S:(m + 1) * S], ACT.Identity,
                                                         bias=bqk_sb[:, mm:mm + 1], scale=0.25 if w == 0 else 1.0)
                                ins.then_inc(qk32_ok, 1)
                    if on["A"] and i == 8:
                        act.wait_ge(rest_ok, s + 1)
                        if rep >= 1:
                            act.wait_ge(qk_out[1], s * 16)
                        act.activation(parts[:, 1], qkr[:, :, :], ACT.Copy).then_inc(part1_ok, 1)
                    if on["D"] and i == 10:
                        act.wait_ge(cnT_ok, s - 2 + 1)
                        for c in range(KC):
                            ins = act.activation(cT[:, c, :], pF[0][:, c * S:(c + 1) * S], ACT.Identity,
                                                 bias=bv_sb[:, c:c + 1])
                        ins.then_inc(cT_ok, 1)
                    if on["D"] and i == 13:
                        act.wait_ge(rstd2_ok, 2 * (s - 1))
                        due(act, scat_ok[rep % 2], (s - 2 - rep % 2) * (QT * TOPK * 16 // 2))
                        apart(act)
                        for t in range(QT):
                            ins = act.activation(x2[rep % 2][:, t, 0:D],
                                                 emb[:, bass.ds((s - 2) * QT + t, 1), :].rearrange("p o d -> p (o d)"),
                                                 ACT.Identity, bias=rstd2[:, 1, t:t + 1], scale=rstd2[:, 0, t:t + 1])
                        ins.then_inc(x2_ok, 1)
                    if on["D"] and i == 14:
                        act.wait_ge(x2T_ps, s - 2 + 1)
                        act.activation(x2T[:, :, :].rearrange("p c t -> p (c t)"), pF[0][:, :], ACT.Copy)\
                            .then_inc(x2T_ok, 1)
                        act.activation(xT_all[:, :, bass.ds((s - 2) * S, S)],
                                       pF[0][:, :].rearrange("p (c t) -> p c t", c=KC), ACT.Copy)\
                            .then_inc(x2T_ok, 1)
                    if on["D"] and i == 15:
                        act.wait_ge(logit_ok, s - 2 + 1)
                        if rep >= 3:
                            act.wait_ge(sel_ok, s - 2)
                        act.activation(esig[:, :, :].rearrange("p t e -> p (t e)"), pF[1][:, 0:QT * E],
                                       ACT.Exp, scale=-1.0).then_inc(esig_ok, 1)
                    if rep == STEPS - 2 and i == 15:
                        shared_silu(0)

            def shared_silu(n):
                for m in range(ISH // P):
                    act.wait_ge(sh_gu, n * 2 + m + 1)
                    due(act, sh_h_ok, (n - 1) * 2 + m + 1)
                    act.activation(sh_g[m], pS[m][:, :], ACT.Silu).then_inc(sh_silu, 1)

            act.wait_ge(bias_ok, 1)
            pipeline(act, step)

            for n in range(1, T // 512):
                shared_silu(n)
                if n == 1:
                    act.wait_ge(padreg_ok, 1)
                if n < 3:
                    pad_lists(act, SP_PADS + (n - 1) * ACT_PADS // 2, SP_PADS + n * ACT_PADS // 2, pad_out_a)

            def silu(t, par, rep):
                act.wait_ge(tg_ok, t + 1)
                if rep >= 2:
                    act.wait_ge(th_ok, t - 1)
                act.activation(sg_t[par], pT[par][:, 0:P], ACT.Silu).then_inc(ts_ok, 1)

            def weigh(t, j, g, rep):
                act.wait_ge(ty_ok, t + 1)
                act.wait_ge(tw_ok, t + 1)
                if rep >= RING:
                    act.wait_ge(acc_ok[j], g * 16)
                act.activation(y_t[j], pF[j % 2][:, 0:D], ACT.Copy, scale=wt_t[j][:, 0:1]).then_inc(te_ok, 1)

            for t in range(RING):
                silu(t, t % 2, t)
                if t:
                    weigh(t - 1, t - 1, 0, t - 1)
            with act.Fori(1, TILES // RING) as g:
                for j in range(RING):
                    silu(g * RING + j, j % 2, RING)
                    if j:
                        weigh(g * RING + j - 1, j - 1, g, RING)
                    else:
                        weigh(g * RING - 1, RING - 1, g - 1, 2)
            weigh(TILES - 1, RING - 1, TILES // RING - 1, RING)

        @block.vector
        def _(dve):
            setup = Chain(dve, set_v, 1 << 20)

            dve.wait_ge(ids_in, 16)
            setup.link(dve.tensor_copy(idf[:, :], ids_sb[:, :]))
            for i in range(3):
                setup.link(dve.tensor_scalar(ge[:, i, :], idf[:, :], float(TIERS[i]), None, ALU.is_ge))
            setup.link(dve.tensor_tensor(ge[:, 3, :], ge[:, 0, :], ge[:, 1, :], ALU.add))
            dve.tensor_tensor(tier_u[:, :], ge[:, 3, :], ge[:, 2, :], ALU.add).then_inc(tier_ok, 1)
            setup.link(dve.tensor_scalar(intier[:, 0, :], ge[:, 0, :], -1.0, 1.0, ALU.mult, ALU.add))
            setup.link(dve.tensor_tensor(intier[:, 1, :], ge[:, 0, :], ge[:, 1, :], ALU.subtract))
            setup.link(dve.tensor_tensor(intier[:, 2, :], ge[:, 1, :], ge[:, 2, :], ALU.subtract))
            setup.link(dve.tensor_copy(maxq[:, :], intier[:, 0, :]))
            for i, of in enumerate((intier[:, 1, :], intier[:, 2, :], ge[:, 2, :])):
                setup.link(dve.scalar_tensor_tensor(maxq[:, :], of, MAXQ[i], maxq[:, :], ALU.mult, ALU.add))
            setup.link(dve.tensor_scalar(nmaxq[:, :], maxq[:, :], -1.0, None, ALU.mult))
            dve.memset(cmax[:, :, :], 0.0).then_inc(scan_v, 1)

            scan_links = [1]

            def reduce_chunk(slot, count, parts, rows, tier, links):
                dve.wait_ge(ring_in[slot], count)
                dve.wait_ge(scan_v, links)
                dve.tensor_reduce(cnew[0:parts, :], ring[0:parts, slot, 0:rows, :].rearrange("p n d -> p d n"),
                                  AX_X, ALU.max, apply_absolute_value=True).then_inc(ring_used, 1)
                return cmax[0:parts, tier, :], cnew[0:parts, :]

            def scan_chunk(slot, count, parts, rows, tier, index, links):
                into, new = reduce_chunk(slot, count, parts, rows, tier, links)
                dve.wait_ge(ring_used, index + 1)
                dve.tensor_tensor(into, into, new, ALU.max).then_inc(scan_v, 1)

            rows2 = (TIERS[2] - TIERS[1]) // P // 2
            heads = ((P, rows2, 1), (P, rows2, 1), (T1P, 4, 0), (REST3, 1, 2))
            for k, (parts_, rows, tier) in enumerate(heads):
                scan_chunk(HEAD0 + k, 16, parts_, rows, tier, k, k + 1)

            def turn(i):
                for j in range(SCAN_RING):
                    index = i * SCAN_RING + j + len(heads)
                    scan_chunk(j, (i + (2 if j >= HEAD0 else 1)) * 16, P, SCAN_ROWS, 2, index, index + 1)

            turn(0)
            dve.wait_ge(consts_ok, 1)
            dve.wait_ge(slope_in_s, 16)
            setup.link(dve.tensor_copy(sparts[:, 0:1], slope_in[:, 0:1]))
            setup.link(dve.tensor_tensor(slope_in[:, 1:2], slope_in[:, 0:1], sparts[:, 0:1], ALU.subtract))
            setup.link(dve.tensor_copy(sparts[:, 1:2], slope_in[:, 1:2]))
            setup.link(dve.tensor_tensor(slope_in[:, 2:3], slope_in[:, 1:2], sparts[:, 1:2], ALU.subtract))
            setup.link(dve.tensor_copy(sparts[:, 2:3], slope_in[:, 2:3]))
            for i in range(3):
                last = dve.tensor_scalar(slope_p[:, i, :], onesrow[:, :], sparts[:, i:i + 1], None, ALU.mult)
            last.then_inc(rows_ok, 1)
            dve.tensor_scalar(pos_p[:, 0, :], pos_f[:, :], -1.0, None, ALU.mult)
            dve.tensor_copy(pos_p[:, 1, :], pos_f[:, :])
            dve.tensor_copy(pos_p[:, 2, :], onesrow[:, :]).then_inc(rows_ok, 1)
            dve.wait_ge(w_in_sb, NLOADS * 16)
            dve.tensor_scalar(bqk_sb[:, 0:2], bqk_sb[:, 0:2], 0.25, None, ALU.mult).then_inc(bias_ok, 1)
            dve.wait_ge(emb_in, NT * 16)
            dve.wait_ge(ts_in, NT * 16)
            setup.link(dve.tensor_tensor(emb[:, :, :], emb[:, :, :], tsel[:, :, :], ALU.mult))
            with dve.Fori(1, CHUNKS // SCAN_RING) as i:
                turn(i)

            dve.wait_ge(scan_v, CHUNKS + len(heads) + 1)
            setup.link(dve.tensor_tensor(cmax[:, :, :], cmax[:, :, :], tsb[:, 1:4, :], ALU.mult))
            dve.tensor_reduce(pmax[:, 0:3], cmax[:, :, :], AX_X, ALU.max, apply_absolute_value=True)\
               .then_inc(pmax_ok, 1)
            dve.wait_ge(amax_ok, 1)
            setup.link(dve.tensor_scalar(sc3[:, 0:3], amax[:, 0:3], 1e-8, None, ALU.max))
            for i in range(3):
                setup.link(dve.tensor_scalar(sc3[:, i:i + 1], sc3[:, i:i + 1], float(np.float32(1) / np.float32(MAXQ[i])),
                                             None, ALU.mult))
            src = intier[:, 0, :]
            for i, of in enumerate((intier[:, 1, :], intier[:, 2, :], ge[:, 2, :])):
                setup.link(dve.scalar_tensor_tensor(scale[:, :], of, sc3[:, i:i + 1], src, ALU.mult, ALU.add))
                src = scale[:, :]
            setup.link(dve.reciprocal(inv[:, :], scale[:, :]))

            ca, cd, cr = (Chain(dve, s_, per) for s_, per in
                          ((chain_a, LINKS_A), (chain_d, LINKS_D), (chain_r, LINKS_R)))

            def token(t, b):
                return bass.ds(b * QT + t, 1)

            def quantise(b, part):
                for t in range(QT):
                    k = token(t, b)
                    if part == 0:
                        ins = dve.tensor_scalar(xq[:, t, :], emb[:, k, :].rearrange("p o d -> p (o d)"), inv[:, k],
                                                ROUND, ALU.mult, ALU.add)
                    elif part == 1:
                        ins = dve.tensor_scalar(xq[:, t, :], xq[:, t, :], -ROUND, maxq[:, k], ALU.add, ALU.min)
                    else:
                        ins = dve.tensor_scalar(xq[:, t, :], xq[:, t, :], nmaxq[:, k], scale[:, k], ALU.max, ALU.mult)
                ca.link(ins)

            def straight_through(b):
                ca.link(dve.tensor_tensor(xq[:, :, :], xq[:, :, :], emb[:, bass.ds(b * QT, QT), :], ALU.subtract))
                for t in range(QT):
                    e1 = emb[:, token(t, b), :].rearrange("p o d -> p (o d)")
                    ins = dve.scalar_tensor_tensor(e1, xq[:, t, :], ge[:, 0, token(t, b)], e1, ALU.mult, ALU.add)
                ca.link(ins)

            def norm_stats(c, b, src, st, m, eps, signal, used):
                apart(dve)
                for t in range(QT):
                    ins = dve.bn_stats(st[:, t, :], src(t))
                c.link(ins)
                apart(dve)
                for t in range(QT):
                    ins = dve.bn_aggr(m[:, t, :], st[:, t, :])
                c.link(ins)
                due(dve, used, 2 * b)
                dve.tensor_scalar(eps[:, 1, :], m[:, :, 0], -1.0, None, ALU.mult)
                dve.tensor_scalar(eps[:, 0, :], m[:, :, 1], EPS, None, ALU.add).then_inc(signal, 1)

            def step(s, rep):
                on = stages(rep)
                par = rep % 2
                for i in range(H):
                    if on["B"]:
                        n = (s - 1) * H + i
                        dve.wait_ge(s_ok, n + 1)
                        if i % MG == 0 and rep >= 2:
                            dve.wait_ge(mT_ok, (s - 2) * NM + i // MG + 1)
                        dve.tensor_reduce(nmax[:, i, :], pS[i % 2][:, :].rearrange("p (t k) -> p t k", t=QT),
                                          AX_X, ALU.max, negate=True).then_inc(max_ok, 1)
                    if on["A"] and i == 0:
                        ca.start(s)
                        quantise(s, 0)
                        quantise(s, 1)
                    if on["A"] and i == 1:
                        quantise(s, 2)
                    if on["A"] and i == 2:
                        straight_through(s)
                    if on["A"] and i == 3:
                        norm_stats(ca, s, lambda t: emb[:, token(t, s), :].rearrange("p o d -> p (o d)"),
                                   stats, mv, mv_eps, var_ok, rstd_ok)
                    if on["D"] and i in (3, 9):
                        d, half_no = s - 2, int(i == 9)
                        if i == 3:
                            cd.start(d)
                        dve.wait_ge(half_ok, 2 * d + half_no + 1)
                        c4 = pF[0][:, :].rearrange("p (t h d) -> p t h d", t=QT, h=H // 2)
                        sums = rsum[:, :, half_no * (H // 2):(half_no + 1) * (H // 2)]
                        cd.link(dve.reciprocal(sums, c4[:, :, :, HD]))
                        if rep - 2 >= 1:
                            dve.wait_ge(cnT_ok, d)
                        dve.tensor_tensor(cn[:, :, half_no * P:(half_no + 1) * P].rearrange("p t (h d) -> p t h d", d=HD),
                                          c4[:, :, :, 0:HD], sums.unsqueeze(3).broadcast_to([P, QT, H // 2, HD]),
                                          ALU.mult).then_inc(cn_ok, 1)
                    if on["R"] and i in (5, 6, 7):
                        (scores, groups, sixth)[i - 5](s - 3)
                    if rep == STEPS - 1 and i == 0:
                        shared_product(0)
                    if on["R"] and i == 9:
                        chosen(s - 3)
                        if rep == STEPS - 1:
                            shared_sum(0)
                    if on["R"] and i == 11:
                        places(s - 3)
                    if on["D"] and i == 12:
                        d = s - 2
                        pair = bass.ds(d * QT, QT)
                        dve.wait_ge(wo_ok, d + 1)
                        dve.wait_ge(embo_ok, d + 1)
                        apart(dve)
                        dve.tensor_tensor(emb[:, pair, :], pF[1][:, :].rearrange("p (t d) -> p t d", t=QT), xo[:, :, :],
                                          ALU.add).then_inc(res_ok, 1)
                        dve.wait_ge(res_ok, d + 1)
                        norm_stats(cd, d, lambda t: emb[:, token(t, d), :].rearrange("p o d -> p (o d)"),
                                   stats2, mv2, mv2_eps, var2_ok, rstd2_ok)
                    if on["R"] and i == 13:
                        slots(s - 3, rep - 3)
                    if on["R"] and i == 14:
                        weights(s - 3, rep - 3)

            def shared_product(n):
                for m in range(ISH // P):
                    dve.wait_ge(sh_silu, n * 2 + m + 1)
                    due(dve, sh_y, (n - 1) * 2)
                    dve.tensor_tensor(sh_h[n % 2][:, m, :], sh_g[m], pT[m][:, :], ALU.mult).then_inc(sh_h_ok, 1)

            def shared_sum(n):
                for k in range(2):
                    dve.wait_ge(sh_y, n * 2 + k + 1)
                    pair = emb[:, n * 4 + 2 * k:n * 4 + 2 * k + 2, :]
                    dve.tensor_tensor(pair, pF[k][:, :].rearrange("p (t d) -> p t d", t=2), pair, ALU.add)\
                       .then_inc(sh_done, 1)

            def scores(r):
                cr.start(r)
                dve.wait_ge(esig_ok, r + 1)
                cr.link(dve.tensor_scalar(score[:, :, :], esig[:, :, :], 1.0, None, ALU.add))
                cr.link(dve.reciprocal(score[:, :, :], score[:, :, :]))
                cr.link(dve.tensor_tensor(score[:, :, :], score[:, :, :],
                                          gbias_sb[:, :].unsqueeze(1).broadcast_to([P, QT, E]), ALU.add))
                by_group = score[:, :, :].rearrange("p t (g e) -> p (t g) e", g=G)
                cr.link(dve.tensor_reduce(gs[:, :, :].rearrange("p t g -> p (t g)"), by_group, AX_X, ALU.max))

            def groups(r):
                other = gs[:, :, :].unsqueeze(2).broadcast_to([P, QT, G, G])
                own = gs[:, :, :].unsqueeze(3).broadcast_to([P, QT, G, G])
                dve.tensor_tensor(cmp_a[:, :, :, :], other, own, ALU.is_gt)
                cr.link(dve.tensor_tensor(cmp_b[:, :, :, :], other, own, ALU.is_equal))
                cr.link(dve.tensor_tensor(cmp_b[:, :, :, :], cmp_b[:, :, :, :],
                                          lower[:, :, :].unsqueeze(1).broadcast_to([P, QT, G, G]), ALU.mult))
                cr.link(dve.tensor_tensor(cmp_a[:, :, :, :], cmp_a[:, :, :, :], cmp_b[:, :, :, :], ALU.add))
                cr.link(dve.tensor_reduce(gmask[:, :, :], cmp_a[:, :, :, :], AX_X, ALU.add))
                cr.link(dve.tensor_scalar(gmask[:, :, :], gmask[:, :, :], float(TG), None, ALU.is_lt))
                cr.link(dve.tensor_tensor(ms[:, :, :].rearrange("p t (g e) -> p t g e", g=G),
                                          score[:, :, :].rearrange("p t (g e) -> p t g e", g=G),
                                          gmask[:, :, :].unsqueeze(3).broadcast_to([P, QT, G, E // G]), ALU.mult))
                cr.link(dve.tensor_scalar(ms[:, :, :], ms[:, :, :], 0.0, None, ALU.add))

            def sixth(r):
                apart(dve)
                for t in range(QT):
                    ins = dve.max(top[:, t, :], ms[:, t, :])
                cr.link(ins)
                apart(dve)
                for t in range(QT):
                    ins = dve.max_index(topi[:, t, :], top[:, t, :], ms[:, t, :])
                cr.link(ins)
                dve.tensor_reduce(wsum[:, :], top[:, :, 0:TOPK], AX_X, ALU.add)
                cr.link(dve.tensor_copy(lastf[:, :], topi[:, :, TOPK - 1]))
                cr.link(dve.tensor_scalar(wsum[:, :], wsum[:, :], 1e-8, None, ALU.add))
                cr.link(dve.reciprocal(wsum[:, :], wsum[:, :]))

            def chosen(r):
                due(dve, prefix_ok, r)
                for t in range(QT):
                    ins = dve.tensor_scalar(tie[:, t, :], eidx[:, :], lastf[:, t:t + 1], None, ALU.is_le)
                cr.link(ins)
                for t in range(QT):
                    ins = dve.scalar_tensor_tensor(tie[:, t, :], ms[:, t, :], top[:, t, TOPK - 1:TOPK], tie[:, t, :],
                                                   ALU.is_equal, ALU.mult)
                cr.link(ins)
                for t in range(QT):
                    ins = dve.scalar_tensor_tensor(M[:, t, :], ms[:, t, :], top[:, t, TOPK - 1:TOPK], tie[:, t, :],
                                                   ALU.is_gt, ALU.add)
                ins.then_inc(sel_ok, 1)
                dve.wait_ge(sel_ok, r + 1)
                for t in range(QT):
                    ins = dve.scalar_tensor_tensor(wn[:, t, :], ms[:, t, :], wsum[:, t:t + 1], M[:, t, :],
                                                   ALU.mult, ALU.mult)
                cr.link(ins)

            def places(r):
                dve.wait_ge(prefix_ok, r + 1)
                pre = pF[0][:, 0:3 * E].rearrange("p (x e) -> p x e", x=3)
                cr.link(dve.tensor_tensor(key[:, :, :], pre[:, 0:QT, :], run[:, :].unsqueeze(1)
                                          .broadcast_to([P, QT, E]), ALU.add))
                dve.tensor_tensor(run[:, :], run[:, :], pre[:, QT, :], ALU.add).then_inc(prefix_used, 1)

            def slots(r, rep):
                cr.link(dve.tensor_tensor(key[:, :, :], key[:, :, :], ebase[:, :].unsqueeze(1)
                                          .broadcast_to([P, QT, E]), ALU.add))
                cr.link(dve.tensor_tensor(key[:, :, :], key[:, :, :], M[:, :, :], ALU.mult))
                apart(dve)
                for t in range(QT):
                    ins = dve.max(topk[:, t, :], key[:, t, :])
                cr.link(ins)

            def weights(r, rep):
                par = rep % 2
                due(dve, scat_ok[par], (r - par) * (QT * TOPK * 16 // 2))
                for t in range(QT):
                    for k in range(TOPK):
                        dve.scalar_tensor_tensor(eq[:, t, k, :], key[:, t, :], topk[:, t, k:k + 1], wn[:, t, :],
                                                 ALU.is_equal, ALU.mult, accum_out=x2[par][:, t, WCOL + k:WCOL + k + 1])
                dve.tensor_copy(x2[par][:, :, SLOTCOL:SLOTCOL + TOPK], topk[:, :, 0:TOPK])
                dve.tensor_copy(x2[par][:, :, TOKCOL:TOKCOL + 1].bitcast(I32),
                                tok_u[:, bass.ds(r * QT, QT)].unsqueeze(2))
                dve.tensor_scalar(slot_u[par][:, :, :], topk[:, :, 0:TOPK], -1.0, None, ALU.add).then_inc(slots_ok, 1)

            pipeline(dve, step)

            tab = Chain(dve, chain_t, 1 << 20)
            dve.wait_ge(prefix_used, B)
            tab.link(dve.tensor_tensor(pad_e[:, :], run[:, :], ebase[:, :], ALU.add))
            dve.tensor_scalar(padreg[:, :], pad_e[:, :], -1.0, None, ALU.add).then_inc(padreg_ok, 1)
            shared_product(1)
            tab.link(dve.tensor_scalar(nt_e[:, :], run[:, :], 127.0, 1.0 / 128.0, ALU.add, ALU.mult))
            tab.link(dve.tensor_scalar(nt_e[:, :], nt_e[:, :], -127.0 / 256.0, ROUND, ALU.add, ALU.add))
            tab.link(dve.tensor_scalar(nt_e[:, :], nt_e[:, :], -ROUND, None, ALU.add))
            tab.link(dve.tensor_tensor_scan(end_e[:, :], one_e[:, :], nt_e[:, :], 0.0, ALU.mult, ALU.add))
            for c in range(2):
                tab.link(dve.tensor_scalar(tsc[:, c, :], end_e[:, :], part_f[:, c:c + 1], None, ALU.is_le))
                tab.link(dve.tensor_reduce(tinfo[:, c, 0:1], tsc[:, c, :], AX_X, ALU.add))
                tab.link(dve.tensor_tensor(tsc[:, c, :], tsc[:, c, :], nt_e[:, :], ALU.mult))
                tab.link(dve.tensor_reduce(tinfo[:, c, 1:2], tsc[:, c, :], AX_X, ALU.add))
                tab.link(dve.tensor_tensor(tinfo[:, c, 2:3], part_f[:, c:c + 1], tinfo[:, c, 1:2], ALU.subtract))
                tab.link(dve.tensor_scalar(tinfo[:, c, 2:3], tinfo[:, c, 2:3], float(P), None, ALU.mult))
                tab.link(dve.scalar_tensor_tensor(tinfo[:, c, 4:5], tinfo[:, c, 0:1], float(CAP), tinfo[:, c, 2:3],
                                                  ALU.mult, ALU.add))
                tab.link(dve.tensor_scalar(tinfo[:, c, 4:5], tinfo[:, c, 4:5], float(E * CAP - P), None, ALU.min))
            dve.engine_nop().then_inc(tinfo_ok, 1)
            shared_sum(1)
            shared_product(2)
            shared_sum(2)
            dve.wait_ge(tinfo_in, 32)
            dve.tensor_copy(treg[:, :], treg_f[:, :]).then_inc(treg_ok, 1)
            dve.tensor_scalar(tslot[:, :], tslot[:, :], part_f[:, 2:3], None, ALU.add).then_inc(tslot_ok, 1)

            shared_product(3)
            shared_sum(3)

            def copy_x(t, j, g, rep):
                dve.wait_ge(tT_ok, t + 1)
                if rep >= 2:
                    dve.wait_ge(tg_ok, t - 1)
                dve.tensor_copy(xT_t[j % 2], pS[j % 2][:, 0:KC * P]).then_inc(tx_ok, 1)
                if rep >= RING:
                    dve.wait_ge(te_ok, t - RING + 1)
                dve.scalar_tensor_tensor(eq_t[j][:, 0:TOPK], x_t[j][:, SLOTCOL:SLOTCOL + TOPK], tslot[:, bass.ds(t, 1)],
                                         x_t[j][:, WCOL:WCOL + TOPK], ALU.is_equal, ALU.mult,
                                         accum_out=wt_t[j][:, 0:1]).then_inc(tw_ok, 1)

            def gate_up(t, j, rep):
                dve.wait_ge(ts_ok, t + 1)
                if rep >= 2:
                    dve.wait_ge(ty_ok, t - 1)
                dve.tensor_tensor(h_t[j % 2], sg_t[j % 2], pT[j % 2][:, P:2 * P], ALU.mult).then_inc(th_ok, 1)

            dve.wait_ge(tslot_ok, 1)
            for j in range(RING):
                copy_x(j, j, 0, j)
                if j:
                    gate_up(j - 1, j - 1, j - 1)
            with dve.Fori(1, TILES // RING) as g:
                for j in range(RING):
                    copy_x(g * RING + j, j, g, RING)
                    gate_up(g * RING + j - 1, (j - 1) % RING, RING)
            gate_up(TILES - 1, RING - 1, RING)

            for n in range(NT // 4):
                dve.wait_ge(fin_in[n % 2], (n // 2 + 1) * NACC * 16)
                for a in range(NACC):
                    four = emb[:, n * 4:(n + 1) * 4, :]
                    ins = dve.tensor_tensor(four, four, fin[n % 2][:, a], ALU.add)
                    if a < NACC - 1:
                        ins.then_inc(fin_v, 1)
                        dve.wait_ge(fin_v, n * (NACC - 1) + a + 1)
                    else:
                        ins.then_inc(fin_ok, 1)

        @block.tensor
        def _(pe):
            def transpose2(src, dst, rows):
                for t in range(QT):
                    for c in range(KC):
                        ins = pe.transpose(dst[:, c * S + t * P:c * S + (t + 1) * P], src(t)[:, c * P:(c + 1) * P],
                                           ident[:, :])
                return ins

            def step(s, rep):
                on = stages(rep)
                par = rep % 2
                for i in range(H):
                    if on["B"]:
                        b = s - 1
                        bpar = (rep - 1) % 2
                        if i == 0:
                            pe.wait_ge(qk_in, (b + 1) * 192)
                            if rep == 1:
                                pe.wait_ge(rows_in, 18 * 16)
                        n = b * H + i
                        if rep > 1 or i >= 2:
                            pe.wait_ge(max_ok, n - 1)
                        for t in range(QT):
                            ins = pe.matmul(pS[i % 2][:, t * S:(t + 1) * S], Qs[bpar][0:ROWS_B, i, t * P:(t + 1) * P],
                                            Ks[bpar][0:ROWS_B, i, :], start=True, stop=True)
                        ins.then_inc(s_ok, 1)
                    if mg := m_group(s, rep, i):
                        b, g = mg
                        n = b * NM + g
                        pe.wait_ge(max_ok, (n + 1) * MG)
                        if rep - (1 if i else 2) > 0 or g >= 1:
                            pe.wait_ge(mrows_ok, n)
                        if g == 0 and rep == 1:
                            pe.wait_ge(v_done, 1)
                        if g == 1:
                            if on["A"]:
                                pe.wait_ge(qk32_ok, s * 4 + 4)
                            else:
                                pe.wait_ge(cn_ok, (s - 2) * 2 + 1)
                        if g == 2:
                            if on["R"]:
                                pe.wait_ge(prefix_used, s - 2)
                            elif on["D"]:
                                pe.wait_ge(cT_ok, s - 1)
                        if g == 3:
                            if rep >= 3:
                                pe.wait_ge(esig_ok, s - 2)
                            else:
                                pe.wait_ge(v_done, 2)
                        pe.transpose(pF[MBANK[g]][0:MG * QT, 0:P],
                                     nmax[:, g * MG:(g + 1) * MG, :].rearrange("p h t -> p (h t)"), ident[:, :])\
                          .then_inc(mT_ok, 1)
                    if head := c_head(s, rep, i):
                        b, h = head
                        crep = rep - (1 if i >= LAG else 2)
                        cpar = crep % 2
                        n = b * H + h
                        if h % MG == 0:
                            pe.wait_ge(max_in[h // MG], (b + 1) * 16)
                        if crep > 0 or h >= 2:
                            pe.wait_ge(exp_ok, n - 1)
                        for kt in range(QT):
                            ins = pe.matmul(pT[h % 2][:, kt * S:(kt + 1) * S], Ks[cpar][0:ROWS_C, h, kt * P:(kt + 1) * P],
                                            Qs[cpar][0:ROWS_C, h, :], start=True, stop=True)
                        ins.then_inc(sT_ok, 1)
                    back = c_head(s, rep, i - 1) if i else None
                    if i == 0 and rep >= 1:
                        back = c_head(s - 1, rep - 1, H - 1)
                    if back:
                        b, h = back
                        brep = rep - (1 if i - 1 >= LAG else 2) if i else rep - 1 - 1
                        vpar = brep % 2
                        n = b * H + h
                        pe.wait_ge(exp_ok, n + 1)
                        if h == 0:
                            pe.wait_ge(v_done, b + 1)
                        if h % (H // 2) == 0 and brep > 0:
                            pe.wait_ge(ctx_ok, 2 * b - (1 if h == 0 else 0))
                        rows = slice(h % 4 * VW, (h % 4 + 1) * VW)
                        cols = slice(h // 4 % 2 * S, (h // 4 % 2 + 1) * S)
                        for kt in range(QT):
                            ins = pe.matmul(pC[rows, h // 8, cols], V[vpar][:, kt, h, :], PT[h % 2][:, kt, :],
                                            start=(kt == 0), stop=(kt == QT - 1))
                        ins.then_inc(pv_ok, 1)
                    if on["D"] and i in (2, 9):
                        d = s - 2
                        pe.wait_ge(ctx_ok, 2 * d + (1 if i == 2 else 2))
                        if i == 2 and rep > 2:
                            pe.wait_ge(x2T_ok, (s - 2) * 2)
                        elif i == 2:
                            pe.wait_ge(mrows_ok, 3)
                        elif on["B"]:
                            pe.wait_ge(mrows_ok, (s - 1) * NM + 2)
                        else:
                            pe.wait_ge(cn_ok, 2 * d + 1)
                        for t in range(QT):
                            for c in range(2):
                                ins = pe.transpose(pF[0][:, (2 * t + c) * P:(2 * t + c + 1) * P],
                                                   ctx_sb[:, c * S + t * P:c * S + (t + 1) * P], ident[:, :])
                        ins.then_inc(half_ok, 1)
                    if on["A"] and i == 5:
                        pe.wait_ge(xn_ok, s + 1)
                        if on["D"]:
                            pe.wait_ge(cn_ok, (s - 2) * 2 + 1)
                        elif rep == 1:
                            pe.wait_ge(qk32_ok, 4)
                        if rep == 0:
                            pe.wait_ge(consts_ok, 1)
                        transpose2(lambda t: xn[:, t, :], pF[0], P).then_inc(xnT_ok, 1)
                    if on["A"] and i == 6:
                        if rep == 0:
                            pe.wait_ge(w_in_sb, NLOADS * 16)
                        pe.wait_ge(xT_ok, s + 1)
                        if rep >= 1:
                            pe.wait_ge(mrows_ok, (s - 1) * NM + 1)
                        for w in range(2):
                            for m in range(2):
                                for c in range(KC):
                                    ins = pe.matmul(pF[1 - w][:, m * S:(m + 1) * S],
                                                    wqk_sb[:, c, w * D + m * P:w * D + (m + 1) * P], xT[:, c, :],
                                                    start=(c == 0), stop=(c == KC - 1))
                            ins.then_inc(qk_ok, 1)
                    if on["A"] and i == 8:
                        pe.wait_ge(qk32_ok, s * 4 + 2)
                        for t in range(QT):
                            for c in range(KC):
                                ins = pe.matmul(pF[1][:, t * D:(t + 1) * D], xT[:, c, t * P:(t + 1) * P],
                                                wv_sb[:, c, :], start=(c == 0), stop=(c == KC - 1))
                        ins.then_inc(v_ok, 1)
                    if on["D"] and i == 10:
                        pe.wait_ge(cn_ok, (s - 2) * 2 + 2)
                        transpose2(lambda t: cn[:, t, :], pF[0], P).then_inc(cnT_ok, 1)
                    if on["D"] and i == 11:
                        d = s - 2
                        pe.wait_ge(cT_ok, d + 1)
                        if on["A"]:
                            pe.wait_ge(v_done, s + 1)
                        elif on["B"]:
                            pe.wait_ge(mrows_ok, (s - 1) * NM + 1)
                        else:
                            pe.wait_ge(mrows_ok, B * NM)
                        for t in range(QT):
                            for c in range(KC):
                                ins = pe.matmul(pF[1][:, t * D:(t + 1) * D], cT[:, c, t * P:(t + 1) * P],
                                                wo_sb[:, c, :], start=(c == 0), stop=(c == KC - 1))
                        ins.then_inc(wo_ok, 1)
                    if rep == STEPS - 2 and i == 11:
                        pe.wait_ge(exp_ok, B * H)
                        shared_gate_up(0)
                    if rep == STEPS - 1 and i == 0:
                        pe.wait_ge(x2T_ok, B * 2)
                        pe.wait_ge(esig_ok, B)
                        shared_gate_up(1)
                        shared_down(0)
                    if on["R"] and i == 11:
                        r = s - 3
                        if rep == STEPS - 1:
                            pe.wait_ge(sh_done, 1)
                        pe.wait_ge(sel_ok, r + 1)
                        if on["D"]:
                            pe.wait_ge(cT_ok, s - 1)
                        else:
                            pe.wait_ge(x2T_ok, (s - 2) * 2)
                        pre = pF[0][:, 0:3 * E]
                        pe.matmul(pre[:, 0:E], before[:, :], M[:, 0, :], start=True, stop=True)
                        pe.matmul(pre[:, E:2 * E], before[:, :], M[:, 1, :], start=True, stop=False)
                        pe.matmul(pre[:, E:2 * E], ones[:, :], M[:, 0, :], start=False, stop=True)
                        pe.matmul(pre[:, 2 * E:3 * E], ones[:, :], M[:, 0, :], start=True, stop=False)
                        pe.matmul(pre[:, 2 * E:3 * E], ones[:, :], M[:, 1, :], start=False, stop=True)\
                          .then_inc(prefix_ok, 1)
                    if on["D"] and i == 14:
                        pe.wait_ge(x2_ok, s - 2 + 1)
                        if on["B"]:
                            pe.wait_ge(mrows_ok, (s - 1) * NM + 3)
                        else:
                            pe.wait_ge(prefix_used, s - 2)
                        transpose2(lambda t: x2[par][:, t, :], pF[0], P).then_inc(x2T_ps, 1)
                    if on["D"] and i == 15:
                        pe.wait_ge(x2T_ok, (s - 2) * 2 + 1)
                        for t in range(QT):
                            for c in range(KC):
                                ins = pe.matmul(pF[1][:, t * E:(t + 1) * E], x2T[:, c, t * P:(t + 1) * P],
                                                gate_sb[:, c, :], start=(c == 0), stop=(c == KC - 1))
                        ins.then_inc(logit_ok, 1)

            def shared_gate_up(n):
                for m in range(ISH // P):
                    due(pe, sh_h_ok, (n - 1) * 2 + m + 1)
                    for w, dst in ((0, pS[m]), (1, pT[m])):
                        for c in range(KC):
                            ins = pe.matmul(dst[:, :], sgu_sb[:, c, w * ISH + m * P:w * ISH + (m + 1) * P],
                                            xT_all[:, c, n * 512:(n + 1) * 512], start=(c == 0), stop=(c == KC - 1))
                    ins.then_inc(sh_gu, 1)

            def shared_down(n):
                pe.wait_ge(sh_h_ok, (n + 1) * 2)
                for k in range(2):
                    due(pe, sh_done, (n - 1) * 2 + k + 1)
                    for t in range(2):
                        for m in range(ISH // P):
                            ins = pe.matmul(pF[k][:, t * D:(t + 1) * D],
                                            sh_h[n % 2][:, m, (2 * k + t) * P:(2 * k + t + 1) * P], sdown_sb[:, m, :],
                                            start=(m == 0), stop=(m == ISH // P - 1))
                    ins.then_inc(sh_y, 1)

            pipeline(pe, step)
            for n in range(2, T // 512):
                shared_gate_up(n)
                shared_down(n - 1)
            shared_down(T // 512 - 1)

            def rows_t(t, j, g, rep):
                pe.wait_ge(x_in[j], (g + 1) * 16)
                if rep >= 2:
                    pe.wait_ge(tx_ok, t - 1)
                for c in range(KC):
                    ins = pe.transpose(pS[j % 2][:, c * P:(c + 1) * P], x_t[j][:, c * P:(c + 1) * P], ident[:, :])
                ins.then_inc(tT_ok, 1)

            def gate_up(t, j, g, rep):
                pe.wait_ge(w_in[j], (g + 1) * 16)
                pe.wait_ge(tx_ok, t + 1)
                if rep >= 2:
                    pe.wait_ge(th_ok, t - 1)
                for w in range(2):
                    for c in range(KC):
                        ins = pe.matmul(pT[j % 2][:, w * P:(w + 1) * P], w_t[j][:, c * 2 * P + w * P:c * 2 * P + (w + 1) * P],
                                        xT_t[j % 2][:, c * P:(c + 1) * P], start=(c == 0), stop=(c == KC - 1))
                ins.then_inc(tg_ok, 1)

            def down(t, j, rep):
                pe.wait_ge(th_ok, t + 1)
                if rep >= 2:
                    pe.wait_ge(te_ok, t - 1)
                pe.matmul(pF[j % 2][:, 0:D], h_t[j % 2], w_t[j][:, 2 * D:3 * D], start=True, stop=True)\
                  .then_inc(ty_ok, 1)

            pe.wait_ge(sh_done, T // 256)
            for j in range(RING):
                rows_t(j, j, 0, j)
                if j >= 1:
                    gate_up(j - 1, j - 1, 0, j - 1)
                if j >= 2:
                    down(j - 2, j - 2, j - 2)
            with pe.Fori(1, TILES // RING) as g:
                for j in range(RING):
                    rows_t(g * RING + j, j, g, RING)
                    gate_up(g * RING + j - 1, (j - 1) % RING, g if j else g - 1, RING)
                    down(g * RING + j - 2, (j - 2) % RING, RING)
            gate_up(TILES - 1, RING - 1, TILES // RING - 1, RING)
            down(TILES - 2, RING - 2, RING)
            down(TILES - 1, RING - 1, RING)


def kernel(**inputs):
    import concourse.bacc as _bacc
    from concourse.bass_utils import run_bass_kernel_spmd as _run

    a = {n: np.asarray(v) for n, v in inputs.items()}

    def chunks(m):
        return np.ascontiguousarray(m.reshape(-1, P, m.shape[1]).transpose(1, 0, 2))

    f = "L0_ffn_"
    t = "L0_attn_"
    experts = np.empty((E, P, 3 * D), np.float32)
    for c in range(KC):
        experts[:, :, c * D:c * D + P] = a[f + "eg_w"][:, :, c * P:(c + 1) * P].transpose(0, 2, 1)
        experts[:, :, c * D + P:(c + 1) * D] = a[f + "eu_w"][:, :, c * P:(c + 1) * P].transpose(0, 2, 1)
    experts[:, :, 2 * D:] = a[f + "ed_w"].transpose(0, 2, 1)
    arrays = {
        "ids": np.ascontiguousarray(a["x"].reshape(NT, P).T),
        "table": np.concatenate([a[f"L0_tok_tw{i}"] for i in range(4)]),
        "ts": np.concatenate([a[f"L0_tok_ts{i}"] for i in range(4)]),
        "wqk": chunks(np.concatenate([a[t + "Wq"].T, a[t + "Wk"].T], axis=1)),
        "wv": chunks(a[t + "Wv"].T),
        "wo": chunks(a[t + "Wo"].T),
        "bqk": np.ascontiguousarray(np.concatenate([a[t + "bq"], a[t + "bk"]]).reshape(4, P).T),
        "bv": np.ascontiguousarray(a[t + "bv"].reshape(KC, P).T),
        "bo": a[t + "bo"].reshape(1, D),
        "slopes": a[t + "slopes"].reshape(H, 1),
        "gate": chunks(a[f + "gate_w"].T),
        "gbias": a[f + "gate_bias"].reshape(1, E),
        "experts": experts.reshape(E * P, 3 * D),
        "sgu": chunks(np.concatenate([a[f + "sg_w"].T, a[f + "su_w"].T], axis=1)),
        "sdown": chunks(a[f + "sd_w"].T),
    }
    nc = _bacc.Bacc("TRN2", target_bir_lowering=False, num_devices=1)
    args = [nc.dram_tensor(f"in_{n}", v.shape, mybir.dt.from_np(v.dtype), kind="ExternalInput").ap()
            for n, v in arrays.items()]
    out = nc.dram_tensor("out_dram", (T, D), F32, kind="ExternalOutput").ap()
    tower(nc, *args, out)
    r = _run(nc, [{f"in_{n}": v for n, v in arrays.items()}], core_ids=[0])
    return r.results[0]["out_dram"].reshape(B, S, D)
```

```python
from contextlib import ExitStack

import numpy as np

import concourse.bass as bass
from concourse import mybir

F32, BF16, I32, U32 = mybir.dt.float32, mybir.dt.bfloat16, mybir.dt.int32, mybir.dt.uint32
ALU = mybir.AluOpType
ACT = mybir.ActivationFunctionType
AX_X = mybir.AxisListType.X
RMAX = bass.bass_isa.ReduceOp.max

P = 128
B, S, D, H, HD = 8, 256, 256, 16, 16
T = B * S
NT = T // P
QT = S // P
KC = D // P
E, INTER, TOPK, G, TG = 64, 128, 6, 8, 4
VW = 32
ISH = 256
EPS = 1e-5
TIERS = (64, 512, 4096, 50257)
MAXQ = (127.0, 31.0, 7.0)
ROUND = 12582912.0

SPLIT = 6 * HD
ROWS_B = SPLIT + 6
ROWS_C = ROWS_B + 1
Q_PARTS = (0, 0, 0, 1, 1, 2)
K_PARTS = (0, 1, 2, 0, 1, 0)

SCAN_ROWS = 15
SCAN_RING = 6
QPAIRS = NT // 2
N3 = (TIERS[3] - TIERS[2]) // P
REST3 = TIERS[3] - TIERS[2] - N3 * P
CHUNKS = N3 // SCAN_ROWS
assert CHUNKS * SCAN_ROWS == N3 and CHUNKS % SCAN_RING == 0

ROW = 272
TOKCOL, SLOTCOL, WCOL = 256, 257, 263
CAP = P + T
TILES = E + (T * TOPK - E) // P + 1
RING = 8
TILES = -(-TILES // RING) * RING
NACC = 4
FG, FBUF = 2, 4
AHEAD = 2
MG = 4
LAG = 8
RACC = T + P
LINKS_A, LINKS_D, LINKS_R = 7, 4, 23
HEAD0 = 2
T1P = (TIERS[1] - TIERS[0]) // 4
MBANK = (1, 0, 0, 1)
START = 6
NLOADS = 12
WROW = 3 * D


def tower(nc, ids, table, ts, wqk, wv, wo, bqk, bv, bo, slopes, gate, gbias, experts, sgu, sdown, out):
    with ExitStack() as ctx:
        def sb(name, shape, dt=F32):
            return ctx.enter_context(nc.sbuf_tensor(name, shape, dt))

        def ps(name, shape, dt=F32):
            return ctx.enter_context(nc.psum_tensor(name, shape, dt))

        def sem(name):
            return ctx.enter_context(nc.semaphore(name))

        qk_scr = nc.dram_tensor("qk_scr", [2, 3, 2, D, S], BF16).ap()
        rows_scr = nc.dram_tensor("rows_scr", [6, H * S], BF16).ap()
        max_scr = nc.dram_tensor("max_scr", [2, H * S], BF16).ap()
        xT_scr = nc.dram_tensor("xT_scr", [B, P, KC * S], F32).ap()
        xs = nc.dram_tensor("xs", [E * CAP, ROW], F32).ap()
        acc_scr = [nc.dram_tensor(f"acc_scr{i}", [RACC, D], F32).ap() for i in range(NACC)]
        tile_scr = nc.dram_tensor("tile_scr", [2, 2, P], F32).ap()

        ident = sb("ident", [P, P])
        before = sb("before", [P, P], BF16)
        ones = sb("ones", [P, P], BF16)
        zeros = sb("zeros", [P, RACC * D // P // 4])
        padrow = sb("padrow", [P, ROW])
        part_i = sb("part_i", [P, 2], I32)
        part_f = sb("part_f", [P, 3])
        tok_u = sb("tok_u", [P, NT], I32)
        eidx = sb("eidx", [P, E])
        ebase = sb("ebase", [P, E])
        iota_i = sb("iota_i", [P, S], I32)
        lower = sb("lower", [P, G, G])
        wqk_sb = sb("wqk_sb", [P, KC, 2 * D])
        wv_sb = sb("wv_sb", [P, KC, D])
        wo_sb = sb("wo_sb", [P, KC, D])
        gate_sb = sb("gate_sb", [P, KC, E])
        gbias_sb = sb("gbias_sb", [P, E])
        bqk_sb = sb("bqk_sb", [P, 4])
        bv_sb = sb("bv_sb", [P, KC])
        bo_sb = sb("bo_sb", [P, D])
        tsb = sb("tsb", [P, 4, D])
        half = sb("half", [P, QT])
        sparts = sb("sparts", [H, 4], BF16)

        ids_sb = sb("ids_sb", [P, NT], I32)
        idf = sb("idf", [P, NT])
        ge = sb("ge", [P, 4, NT])
        intier = sb("intier", [P, 3, NT])
        maxq = sb("maxq", [P, NT])
        nmaxq = sb("nmaxq", [P, NT])
        scale = sb("scale", [P, NT])
        inv = sb("inv", [P, NT])
        emb = sb("emb", [P, NT, D])
        tsel = sb("tsel", [P, NT, D])
        ring = sb("ring", [P, SCAN_RING, SCAN_ROWS, D])
        flat = ring[:, :, :, :].rearrange("p a b d -> p (a b d)")
        taken = [0]

        def carve(n):
            taken[0] += n
            assert taken[0] <= SCAN_RING * SCAN_ROWS * D
            return flat[:, taken[0] - n:taken[0]]

        cmax = sb("cmax", [P, 3, D])
        cnew = sb("cnew", [P, D])
        pmax = sb("pmax", [P, 4])
        amax = sb("amax", [P, 4])
        sc3 = sb("sc3", [P, 4])

        xq = carve(QT * D).rearrange("p (t d) -> p t d", t=QT)
        stats = sb("stats", [P, QT, 6])
        mv = sb("mv", [P, QT, 2])
        mv_eps = sb("mv_eps", [P, 2, QT])
        rstd = sb("rstd", [P, 2, QT])
        xn = carve(QT * D).rearrange("p (t d) -> p t d", t=QT)
        xT = sb("xT", [P, KC, S])
        qk32 = carve(4 * S).rearrange("p (m s) -> p m s", m=4)
        qkr = carve(4 * S).rearrange("p (m s) -> p m s", m=4)
        parts = sb("parts", [P, 3, 4, S], BF16)
        at = taken[0]
        Qs = [carve(H * S // 2).bitcast(BF16).rearrange("p (h s) -> p h s", h=H) for _ in range(2)]
        Ks = [carve(H * S // 2).bitcast(BF16).rearrange("p (h s) -> p h s", h=H) for _ in range(2)]
        fin = [flat[:, at + i * NACC * FG * D:at + (i + 1) * NACC * FG * D].rearrange("p (a n d) -> p a n d", a=NACC, n=FG)
               for i in range(FBUF)]
        assert FBUF * NACC * FG * D <= 2 * H * S
        V = [sb(f"V{i}", [P, QT, H, VW]) for i in range(2)]
        slope_in = sb("slope_in", [H, 4])
        pos_f = sb("pos_f", [H, S])
        onesrow = sb("onesrow", [H, S])
        slope_p = sb("slope_p", [H, 3, S], BF16)
        pos_p = sb("pos_p", [H, 3, S], BF16)
        nmax = sb("nmax", [P, H, QT])
        mrows = [sb(f"mrows{i}", [MG * QT, P], BF16) for i in range(2)]
        PT = [sb(f"PT{i}", [P, QT, S]) for i in range(2)]
        rsum = sb("rsum", [P, QT, H])
        cn = carve(QT * D).rearrange("p (t d) -> p t d", t=QT)
        ctx_sb = carve(512)
        cT = sb("cT", [P, KC, S])

        stats2 = sb("stats2", [P, QT, 6])
        mv2 = sb("mv2", [P, QT, 2])
        mv2_eps = sb("mv2_eps", [P, 2, QT])
        xo = carve(QT * D).rearrange("p (t d) -> p t d", t=QT)
        rstd2 = sb("rstd2", [P, 2, QT])
        x2 = [sb(f"x2_{i}", [P, QT, ROW]) for i in range(2)]
        x2T = sb("x2T", [P, KC, S])
        esig = sb("esig", [P, QT, E])
        score = sb("score", [P, QT, E])
        gs = sb("gs", [P, QT, G])
        cmp_a = sb("cmp_a", [P, QT, G, G])
        cmp_b = sb("cmp_b", [P, QT, G, G])
        gmask = sb("gmask", [P, QT, G])
        ms = sb("ms", [P, QT, E])
        top = sb("top", [P, QT, 8])
        topi = sb("topi", [P, QT, 8], U32)
        lastf = sb("lastf", [P, QT])
        wsum = sb("wsum", [P, QT])
        tie = sb("tie", [P, QT, E])
        M = sb("M", [P, QT, E], BF16)
        wn = sb("wn", [P, QT, E])
        key = sb("key", [P, QT, E])
        topk = sb("topk", [P, QT, 8])
        eq = sb("eq", [P, QT, TOPK, E])
        run = sb("run", [P, E])
        slot_u = [sb(f"slot_u{i}", [P, QT, TOPK], U32) for i in range(2)]

        nt_e = sb("nt_e", [P, E])
        end_e = sb("end_e", [P, E])
        one_e = sb("one_e", [P, E])
        start_e = sb("start_e", [P, E])
        ended = sb("ended", [P, 2, E])
        own = sb("own", [P, 2, E])
        tinfo = sb("tinfo", [P, 8, 2])
        treg_f = sb("treg_f", [1, 2 * P])
        treg = sb("treg", [1, 2 * P], I32)
        tslot = sb("tslot", [P, 2 * P])
        tfirst = sb("tfirst", [P, 2 * P])
        sgu_sb = sb("sgu_sb", [P, KC, 2 * ISH])
        sdown_sb = sb("sdown_sb", [P, ISH // P, D])

        w_t = [flat[:, at + i * WROW:at + (i + 1) * WROW] for i in range(RING)]
        assert RING * WROW <= 2 * H * S
        x_t = [carve(ROW) for _ in range(RING)]
        y_t = [carve(D) for _ in range(RING)]
        xT_t = [carve(KC * P) for _ in range(2)]
        sg_t = [carve(P) for _ in range(2)]
        h_t = [carve(P) for _ in range(2)]
        wt_t = [carve(4) for _ in range(RING)]
        eq_t = [carve(8) for _ in range(RING)]
        sh_g = carve(ISH)
        sh_h = carve(ISH).rearrange("p (m t) -> p m t", m=ISH // P)
        xT_all = tsel[:, :, :].rearrange("p n d -> p (n d)").rearrange("p (c t) -> p c t", c=KC)

        pS = [ps(f"pS{i}", [P, 512]) for i in range(2)]
        pT = [ps(f"pT{i}", [P, 512]) for i in range(2)]
        pC = ps("pC", [P, 2, 512])
        pF = [ps(f"pF{i}", [P, 512]) for i in range(2)]

        consts_p = sem("consts_p")
        consts_ok = sem("consts_ok")
        emb_ok = sem("emb_ok")
        tsel_ok = sem("tsel_ok")
        masked_ok = sem("masked_ok")
        added = sem("added")
        ids_in = sem("ids_in")
        w_in_sb = sem("w_in_sb")
        slope_in_s = sem("slope_in_s")
        emb_in = sem("emb_in")
        ring_in = [sem(f"ring_in{i}") for i in range(SCAN_RING)]
        ring_used = sem("ring_used")
        scan_v = sem("scan_v")
        pmax_ok = sem("pmax_ok")
        amax_ok = sem("amax_ok")
        bias_ok = sem("bias_ok")
        set_v = sem("set_v")
        rows_ok = sem("rows_ok")
        rows_out = sem("rows_out")
        rows_in = sem("rows_in")
        zero_out = sem("zero_out")

        chain_a, chain_d, chain_r = sem("chain_a"), sem("chain_d"), sem("chain_r")
        var_ok = sem("var_ok")
        rstd_ok = sem("rstd_ok")
        xn_ok = sem("xn_ok")
        xnT_ok = sem("xnT_ok")
        xT_ok = sem("xT_ok")
        qk_ok = sem("qk_ok")
        qk32_ok = sem("qk32_ok")
        rest_ok = sem("rest_ok")
        part1_ok = sem("part1_ok")
        part2_ok = sem("part2_ok")
        qk_out = [sem(f"qk_out{i}") for i in range(3)]
        qk_in = sem("qk_in")
        v_ok = sem("v_ok")
        v_done = sem("v_done")
        s_ok = sem("s_ok")
        max_ok = sem("max_ok")
        mT_ok = sem("mT_ok")
        mrows_ok = sem("mrows_ok")
        max_out = sem("max_out")
        max_in = [sem(f"max_in{g}") for g in range(H // MG)]
        sT_ok = sem("sT_ok")
        exp_ok = sem("exp_ok")
        pv_ok = sem("pv_ok")
        ctx_ok = sem("ctx_ok")
        half_ok = sem("half_ok")
        cn_ok = sem("cn_ok")
        cnT_ok = sem("cnT_ok")
        cT_ok = sem("cT_ok")
        wo_ok = sem("wo_ok")
        embo_ok = sem("embo_ok")
        res_ok = sem("res_ok")
        var2_ok = sem("var2_ok")
        rstd2_ok = sem("rstd2_ok")
        x2_ok = sem("x2_ok")
        x2T_ps = sem("x2T_ps")
        x2T_ok = sem("x2T_ok")
        logit_ok = sem("logit_ok")
        esig_ok = sem("esig_ok")
        sel_ok = sem("sel_ok")
        prefix_ok = sem("prefix_ok")
        prefix_used = sem("prefix_used")
        slots_ok = sem("slots_ok")
        scat_ok = [sem(f"scat_ok{i}") for i in range(2)]

        chain_t = sem("chain_t")
        tinfo_ok = sem("tinfo_ok")
        tinfo_out = sem("tinfo_out")
        tinfo_in = sem("tinfo_in")
        treg_ok = sem("treg_ok")
        tslot_ok = sem("tslot_ok")
        pad_out = sem("pad_out")
        sh_w_in = sem("sh_w_in")
        sh_gu = sem("sh_gu")
        sh_silu = sem("sh_silu")
        sh_h_ok = sem("sh_h_ok")
        sh_y = sem("sh_y")
        sh_done = sem("sh_done")
        w_in = [sem(f"w_in{i}") for i in range(RING)]
        x_in = [sem(f"x_in{i}") for i in range(RING)]
        tT_ok = sem("tT_ok")
        tx_ok = sem("tx_ok")
        tw_ok = sem("tw_ok")
        tg_ok = sem("tg_ok")
        ts_ok = sem("ts_ok")
        th_ok = sem("th_ok")
        ty_ok = sem("ty_ok")
        te_ok = sem("te_ok")
        acc_ok = [sem(f"acc_ok{i}") for i in range(RING)]
        fin_in = [sem(f"fin_in{i}") for i in range(FBUF)]
        fin_v = sem("fin_v")
        fin_ok = sem("fin_ok")
        out_done = sem("out_done")

        passed = {nc.sync: sem("passed_sp"), nc.scalar: sem("passed_act"), nc.gpsimd: sem("passed_pool"), nc.vector: sem("passed_dve")}
        block = ctx.enter_context(nc.Block())

        def apart(eng):
            eng.sem_inc(passed[eng], 1)

        def due(eng, s, value):
            if not isinstance(value, int) or value > 0:
                eng.wait_ge(s, value)

        class Chain:

            def __init__(self, eng, s, per):
                self.eng, self.s, self.per, self.base, self.n = eng, s, per, 0, 0

            def start(self, batch):
                assert self.n in (0, self.per), (self.n, self.per)
                self.base, self.n = batch * self.per, 0

            def link(self, ins):
                self.n += 1
                ins.then_inc(self.s, 1)
                self.eng.wait_ge(self.s, self.base + self.n)

        STEPS = B + 3
        LOOP = (4, B)
        assert (LOOP[1] - LOOP[0]) % 2 == 0

        def stages(rep):
            return {k: 0 <= rep - lag < B for k, lag in (("A", 0), ("B", 1), ("D", 2), ("R", 3), ("S", 4))}

        def c_head(s, rep, i):
            lag, h = (1, i - LAG) if i >= LAG else (2, i + H - LAG)
            return (s - lag, h) if 0 <= rep - lag < B else None

        def pipeline(eng, step):
            for s in range(LOOP[0]):
                step(s, s)
            with eng.Fori(LOOP[0], LOOP[1] - 1, 2) as s:
                step(s, LOOP[0])
                step(s + 1, LOOP[0] + 1)
            for s in range(LOOP[1], STEPS):
                step(s, s)

        def m_group(s, rep, i):
            if i % MG:
                return None
            lag, g = (1, i // MG - 1) if i else (2, H // MG - 1)
            return (s - lag, g) if 0 <= rep - lag < B else None

        def turns(eng, turn):
            turn(0, False, True)
            with eng.Fori(1, NT) as g:
                turn(g, True, True)
            with eng.Fori(NT, TILES // RING) as g:
                turn(g, True, False)

        NM = H // MG
        CLEARING = (1, 2, 3, 8)
        assert len(CLEARING) == NACC

        @block.sync
        def _(sp):
            sp.dma_start(ids_sb[:, :], ids).then_inc(ids_in, 16)

            def chunk(slot, src, parts, rows):
                sp.dma_start(ring[0:parts, slot, 0:rows, :], src).then_inc(ring_in[slot], 16)

            t2 = table[TIERS[1]:TIERS[2], :].rearrange("(p n) d -> p n d", p=P)
            half2 = t2.shape[1] // 2
            chunk(HEAD0, t2[:, 0:half2, :], P, half2)
            chunk(HEAD0 + 1, t2[:, half2:, :], P, half2)
            chunk(HEAD0 + 2, table[TIERS[0]:TIERS[1], :].rearrange("(p n) d -> p n d", n=4), T1P, 4)
            chunk(HEAD0 + 3, table[TIERS[3] - REST3:TIERS[3], :].rearrange("(p n) d -> p n d", n=1), REST3, 1)
            for dst, src in ((wqk_sb, wqk), (wv_sb, wv), (wo_sb, wo), (gate_sb, gate)):
                sp.dma_start(dst[:, :, :], src).then_inc(w_in_sb, 16)
            sp.dma_start(bqk_sb[:, :], bqk).then_inc(w_in_sb, 16)
            sp.dma_start(bv_sb[:, :], bv).then_inc(w_in_sb, 16)
            for dst, src in ((bo_sb, bo), (gbias_sb, gbias)):
                sp.dma_start(dst[:, :], src.broadcast_to([P, src.shape[1]])).then_inc(w_in_sb, 16)
            for i in range(4):
                sp.dma_start(tsb[:, i, :], ts[i:i + 1, :].broadcast_to([P, D])).then_inc(w_in_sb, 16)
            sp.dma_start(slope_in[:, 0:1], slopes).then_inc(slope_in_s, 16)

            t3 = table[TIERS[2]:TIERS[3] - REST3, :].rearrange("(p n) d -> p n d", p=P)
            def turn(i):
                for j in range(SCAN_RING):
                    if not isinstance(i, int) or j >= HEAD0:
                        sp.wait_ge(ring_used, i * SCAN_RING + j + 1 - HEAD0)
                    chunk(j, t3[:, bass.ds((i * SCAN_RING + j) * SCAN_ROWS, SCAN_ROWS), :], P, SCAN_ROWS)

            turn(0)
            with sp.Fori(1, CHUNKS // SCAN_RING) as i:
                turn(i)

            for dst, src in ((sgu_sb, sgu), (sdown_sb, sdown)):
                sp.dma_start(dst[:, :, :], src).then_inc(sh_w_in, 16)

            sp.wait_ge(rows_ok, 2)
            sp.dma_start(rows_scr[0:3, :].rearrange("i (h s) -> h i s", h=H), slope_p[:, :, :]).then_inc(rows_out, 16)
            sp.dma_start(rows_scr[3:6, :].rearrange("i (h s) -> h i s", h=H), pos_p[:, :, :]).then_inc(rows_out, 16)
            sp.wait_ge(rows_out, 32)
            sp.wait_ge(pmax_ok, 1)
            for par in range(2):
                q_rows = Qs[par][:, :, :].rearrange("p h s -> p (h s)")
                k_rows = Ks[par][:, :, :].rearrange("p h s -> p (h s)")
                sp.dma_start(q_rows[SPLIT:SPLIT + 3, :], rows_scr[0:3, :]).then_inc(rows_in, 16)
                sp.dma_start(k_rows[SPLIT + 3:SPLIT + 6, :], rows_scr[0:3, :]).then_inc(rows_in, 16)
                for dst, row, src in ([(q_rows, SPLIT + 3 + i, 3) for i in range(3)] +
                                      [(k_rows, SPLIT + i, 4) for i in range(3)] + [(k_rows, ROWS_B, 5)]):
                    sp.dma_start(dst[row:row + 1, :], rows_scr[src:src + 1, :]).then_inc(rows_in, 16)
            quarter = RACC // P * D // 4

            def pad(a):
                per = E // NACC
                rows = xs.rearrange("(e r) d -> r e d", r=CAP)
                sp.dma_start(rows[0:P, a * per:(a + 1) * per, :],
                             padrow[:, :].unsqueeze(1).broadcast_to([P, per, ROW])).then_inc(pad_out, 16)

            def clear(a):
                for i in range(4):
                    dst = acc_scr[a].rearrange("(p n) d -> p (n d)", p=P)[:, i * quarter:(i + 1) * quarter]
                    sp.dma_start(dst, zeros[:, :]).then_inc(zero_out, 16)

            def step(s, rep):
                on = stages(rep)
                par = rep % 2
                for i in range(H):
                    if mg := m_group(s, rep, i):
                        b, g = mg
                        mpar = (rep - (1 if i else 2)) % 2
                        sp.wait_ge(mrows_ok, b * NM + g + 1)
                        apart(sp)
                        due(sp, max_in[g], (b - 1) * 16)
                        dst = max_scr[mpar:mpar + 1, g * MG * S:(g + 1) * MG * S]
                        sp.dma_start(dst.rearrange("i (r q) -> (i r) q", q=P), mrows[g % 2][:, :]).then_inc(max_out, 16)
                        sp.wait_ge(max_out, (b * NM + g + 1) * 16)
                        rows = Qs[mpar][ROWS_B:ROWS_C, g * MG:(g + 1) * MG, :]
                        sp.dma_start(rows.rearrange("p h s -> p (h s)"), dst).then_inc(max_in[g], 16)
                    if on["A"]:
                        move_parts(s, rep, par, i)
                    if i == 2 and rep in CLEARING:
                        if rep == CLEARING[0]:
                            sp.wait_ge(consts_ok, 1)
                        pad(CLEARING.index(rep))
                    if i == 12 and rep in CLEARING:
                        clear(CLEARING.index(rep))

            def move_parts(s, rep, par, i):
                dst = qk_scr[par].rearrange("r w (c p) s -> p r (w c) s", p=P)
                if i == 8:
                    sp.wait_ge(qk32_ok, s * 4 + 4)
                    apart(sp)
                    due(sp, qk_in, (s - 1) * 192 if rep >= 2 else 0)
                    sp.dma_start(dst[:, 0], parts[:, 0, :, :]).then_inc(qk_out[0], 16)
                    if rep >= 2:
                        sp.wait_ge(sT_ok, (s - 1) * H)
                        apart(sp)
                if i in (9, 10):
                    r = i - 8
                    sp.wait_ge((part1_ok, part2_ok)[r - 1], s + 1)
                    sp.dma_start(dst[:, r], parts[:, r, :, :]).then_inc(qk_out[r], 16)
                if i in (9, 10, 11):
                    r = i - 9
                    sp.wait_ge(qk_out[r], (s + 1) * 16)
                    for w, (to, blocks) in enumerate(((Qs[par], Q_PARTS), (Ks[par], K_PARTS))):
                        for j, part in enumerate(blocks):
                            if part == r:
                                sp.dma_start(to[j * HD:(j + 1) * HD, :, :],
                                             qk_scr[par, r, w].rearrange("(h d) s -> d h s", d=HD))\
                                  .then_inc(qk_in, 16)

            pipeline(sp, step)

            sp.wait_ge(tinfo_ok, 1)
            for k in range(2):
                sp.dma_start(tile_scr[k].rearrange("c p -> p c"), tinfo[:, START + k, :],
                             allow_slow_non_contiguous=True).then_inc(tinfo_out, 16)
            sp.wait_ge(tinfo_out, 32)
            start_row, first_row = (tile_scr[k:k + 1].rearrange("k c p -> k (c p)") for k in range(2))
            sp.dma_start(treg_f[:, :], start_row).then_inc(tinfo_in, 16)
            sp.dma_start(tslot[:, :], start_row.broadcast_to([P, 2 * P])).then_inc(tinfo_in, 16)
            sp.dma_start(tfirst[:, :], first_row.broadcast_to([P, 2 * P])).then_inc(tinfo_in, 16)

            def first_slot(t):
                return sp.value_load(treg[0:1, bass.ds(t, 1)], min_val=0, max_val=E * CAP - P)

            def load_rows(first, j):
                sp.dma_start(x_t[j], xs[bass.ds(first, P), :]).then_inc(x_in[j], 16)

            def load_weights(first, j):
                sp.dma_start(w_t[j], experts[bass.ds((first // CAP) * P, P), :]).then_inc(w_in[j], 16)

            def load_tile(t, j, g):
                first = first_slot(t)
                sp.wait_ge(acc_ok[j], g * 16)
                apart(sp)
                sp.wait_ge(tw_ok, t - RING + 1)
                load_rows(first, j)
                sp.wait_ge(ty_ok, t - RING + 1)
                apart(sp)
                load_weights(first, j)

            sp.wait_ge(treg_ok, 1)
            sp.wait_ge(sT_ok, B * H)
            for j in range(AHEAD):
                load_weights(first_slot(j), j)
            sp.wait_ge(pad_out, NACC * 16)
            for i in range(2):
                sp.wait_ge(scat_ok[i], B // 2 * QT * TOPK * 16)
            for j in range(RING):
                first = first_slot(j)
                load_rows(first, j)
                if j >= AHEAD:
                    load_weights(first, j)
            with sp.Fori(1, TILES // RING) as g:
                for j in range(RING):
                    load_tile(g * RING + j, j, g)

            for j in range(RING):
                sp.wait_ge(acc_ok[j], TILES // RING * 16)
            def group(x, n):
                return x[n * FG * P:(n + 1) * FG * P, :].rearrange("(n p) d -> p n d", p=P)

            def store(n):
                sp.wait_ge(fin_ok, n + 1)
                sp.dma_start(group(out, n), emb[:, n * FG:(n + 1) * FG, :]).then_inc(out_done, 16)

            for n in range(NT // FG):
                if n >= FBUF:
                    store(n - FBUF)
                for a in range(NACC):
                    sp.dma_start(fin[n % FBUF][:, a], group(acc_scr[a], n)).then_inc(fin_in[n % FBUF], 16)
            for n in range(NT // FG - FBUF, NT // FG):
                store(n)
            sp.wait_ge(out_done, NT // FG * 16)

        @block.gpsimd
        def _(pool):
            n_c = [0]

            def const(ins):
                n_c[0] += 1
                ins.then_inc(consts_p, 1)
                pool.wait_ge(consts_p, n_c[0])

            pool.wait_ge(ids_in, 16)
            for j in range(NT):
                pool.indirect_dma_start(emb[:, j, :], None, table,
                                        bass.IndirectOffsetOnAxis(ids_sb[:, j:j + 1].bitcast(U32), 0))\
                    .then_inc(emb_in, 16)
            for t, v in ((ident, 0.0), (before, 0.0), (ones, 1.0), (zeros, 0.0), (padrow, 0.0), (lower, 0.0),
                         (half, -0.5), (one_e, 1.0), (run, 0.0), (onesrow, 1.0)):
                const(pool.memset(t[tuple(slice(None) for _ in t.shape)], v))
            const(pool.affine_select(out=ident[:, :], in_=ident[:, :], compare_op=ALU.not_equal, fill=1.0,
                                     base=0, pattern=[[-1, P]], channel_multiplier=1))
            const(pool.affine_select(out=before[:, :], in_=before[:, :], compare_op=ALU.is_ge, fill=1.0,
                                     base=0, pattern=[[-1, P]], channel_multiplier=1))
            const(pool.affine_select(out=lower[:, :, :], in_=lower[:, :, :], compare_op=ALU.is_ge, fill=1.0,
                                     base=0, pattern=[[-1, G], [1, G]], channel_multiplier=0))
            const(pool.iota(part_i[:, :], pattern=[[P, 2]], base=0, channel_multiplier=1))
            const(pool.tensor_copy(part_f[:, 0:2], part_i[:, :]))
            const(pool.iota(tok_u[:, :], pattern=[[P, NT]], base=0, channel_multiplier=1))
            const(pool.iota(iota_i[:, 0:E], pattern=[[1, E]], base=0, channel_multiplier=0))
            const(pool.tensor_copy(eidx[:, :], iota_i[:, 0:E]))
            const(pool.tensor_scalar(ebase[:, :], eidx[:, :], float(CAP), float(P + 1), ALU.mult, ALU.add))
            const(pool.iota(iota_i[:, :], pattern=[[1, S]], base=0, channel_multiplier=0))
            const(pool.tensor_copy(pos_f[:, :], iota_i[0:H, :]))
            const(pool.tensor_scalar(part_f[:, 2:3], part_f[:, 0:1], 1.0, None, ALU.add))
            const(pool.iota(padrow[:, TOKCOL:TOKCOL + 1].bitcast(I32), pattern=[[0, 1]], base=T,
                            channel_multiplier=1))
            for par in range(2):
                const(pool.memset(V[par][:, :, :, HD:HD + 1], 1.0))
                const(pool.memset(V[par][:, :, :, HD + 1:VW], 0.0))
                const(pool.memset(x2[par][:, :, WCOL + TOPK:ROW], 0.0))
            pool.memset(iota_i[:, 0:1], 0).then_inc(consts_ok, 1)

            pool.wait_ge(tsel_ok, 1)
            for k in range(3 * QPAIRS):
                two = tsel[:, 2 * (k % QPAIRS):2 * (k % QPAIRS) + 2, :]
                pool.wait_ge(masked_ok, k + 1)
                if k >= QPAIRS:
                    pool.wait_ge(added, k - QPAIRS + 1)
                pool.tensor_tensor(two, two, PT[k % 2][:, :, :], ALU.add).then_inc(added, 1)
            pool.wait_ge(added, 3 * QPAIRS)
            pool.wait_ge(emb_in, NT * 16)
            pool.tensor_tensor(emb[:, :, :], emb[:, :, :], tsel[:, :, :], ALU.mult).then_inc(emb_ok, 1)

            pool.wait_ge(pmax_ok, 1)
            pool.partition_all_reduce(amax[:, 0:3], pmax[:, 0:3], P, RMAX).then_inc(amax_ok, 1)

            def factors(b, of, to, done):
                pool.tensor_tensor(to[:, 0, :], of[:, 0, :], half[:, :], ALU.pow).then_inc(done, 1)
                pool.wait_ge(done, 2 * b + 1)
                pool.tensor_tensor(to[:, 1, :], of[:, 1, :], to[:, 0, :], ALU.mult).then_inc(done, 1)

            def scatters(r, rep, ks):
                rpar = rep % 2
                for t in range(QT):
                    for k in ks:
                        pool.indirect_dma_start(xs[:, :],
                                                bass.IndirectOffsetOnAxis(slot_u[rpar][:, t, k:k + 1], 0),
                                                x2[rpar][:, t, :], None).then_inc(scat_ok[rpar], 16)

            def step(s, rep):
                on = stages(rep)
                if on["S"]:
                    pool.wait_ge(slots_ok, s - 4 + 1)
                    pool.wait_ge(x2_ok, s - 4 + 1)
                    apart(pool)
                    scatters(s - 4, rep - 4, range(0, 4))
                if on["A"]:
                    pool.wait_ge(var_ok, s + 1)
                    if rep >= 1:
                        pool.wait_ge(xn_ok, s)
                    factors(s, mv_eps, rstd, rstd_ok)
                if on["S"]:
                    scatters(s - 4, rep - 4, range(4, TOPK))
                if on["A"]:
                    pool.wait_ge(qk32_ok, s * 4 + 4)
                    if rep >= 1:
                        pool.wait_ge(part1_ok, s)
                    pool.tensor_tensor(qkr[:, :, :], qk32[:, :, :], parts[:, 0], ALU.subtract).then_inc(rest_ok, 1)
                    pool.wait_ge(part1_ok, s + 1)
                    if rep >= 1:
                        pool.wait_ge(qk_out[2], s * 16)
                    pool.tensor_tensor(parts[:, 2], qkr[:, :, :], parts[:, 1], ALU.subtract).then_inc(part2_ok, 1)
                if on["D"]:
                    if rep >= 3:
                        pool.wait_ge(res_ok, s - 2)
                    apart(pool)
                    pool.tensor_tensor(xo[:, :, :], emb[:, bass.ds((s - 2) * QT, QT), :],
                                       bo_sb[:, :].unsqueeze(1).broadcast_to([P, QT, D]), ALU.add).then_inc(embo_ok, 1)
                    pool.wait_ge(var2_ok, s - 2 + 1)
                    if rep >= 3:
                        pool.wait_ge(x2_ok, s - 2)
                    factors(s - 2, mv2_eps, rstd2, rstd2_ok)

            pipeline(pool, step)
            pool.wait_ge(slots_ok, B)
            pool.wait_ge(x2_ok, B)
            scatters(B - 1, B - 1, range(TOPK))

            def accumulate(g, j, rep):
                pool.wait_ge(te_ok, g * RING + j + 1)
                if j >= NACC:
                    pool.wait_ge(acc_ok[j - NACC], (g + 1) * 16)
                elif rep:
                    pool.wait_ge(acc_ok[j - NACC + RING], g * 16)
                apart(pool)
                pool.indirect_dma_start(acc_scr[j % NACC], bass.IndirectOffsetOnAxis(
                    x_t[j][:, TOKCOL:TOKCOL + 1].bitcast(U32), 0), y_t[j], None, compute_op=ALU.add)\
                    .then_inc(acc_ok[j], 16)

            pool.wait_ge(zero_out, NACC * 4 * 16)
            for j in range(RING):
                accumulate(0, j, False)
            with pool.Fori(1, TILES // RING) as g:
                for j in range(RING):
                    accumulate(g, j, True)

        @block.scalar
        def _(act):
            def masked(dst, i, j):
                of = intier[:, i, j:j + 1] if i < 3 else ge[:, 2, j:j + 1]
                return act.activation(dst, tsb[:, i, :], ACT.Identity, bias=zeros[:, 0:1], scale=of)

            act.wait_ge(consts_ok, 1)
            act.wait_ge(scan_v, 1)
            act.wait_ge(w_in_sb, NLOADS * 16)
            for j in range(NT):
                ins = masked(tsel[:, j, :], 0, j)
            ins.then_inc(tsel_ok, 1)
            for k in range(3 * QPAIRS):
                if k >= 2:
                    act.wait_ge(added, k - 1)
                for t in range(2):
                    ins = masked(PT[k % 2][:, t, :], 1 + k // QPAIRS, 2 * (k % QPAIRS) + t)
                ins.then_inc(masked_ok, 1)

            def step(s, rep):
                on = stages(rep)
                for i in range(H):
                    if mg := m_group(s, rep, i):
                        b, g = mg
                        n = b * NM + g
                        act.wait_ge(mT_ok, n + 1)
                        if rep - (1 if i else 2) > 0 or g >= 2:
                            act.wait_ge(max_out, (n - 1) * 16)
                        act.activation(mrows[g % 2][:, :], pF[MBANK[g]][0:MG * QT, 0:P], ACT.Copy).then_inc(mrows_ok, 1)
                    if head := c_head(s, rep, i):
                        b, h = head
                        n = b * H + h
                        first = rep - (1 if i >= LAG else 2) == 0
                        act.wait_ge(sT_ok, n + 1)
                        if not (first and h < 2):
                            act.wait_ge(pv_ok, n - 1)
                        act.activation(PT[h % 2][:, :, :].rearrange("p k q -> p (k q)"), pT[h % 2][:, :],
                                       ACT.Exp).then_inc(exp_ok, 1)
                    if on["D"] and i in (1, 8):
                        k = 2 * (s - 2) + (i == 8)
                        act.wait_ge(pv_ok, (k + 1) * (H // 2))
                        if rep > 2 or i == 8:
                            act.wait_ge(half_ok, k)
                        act.activation(ctx_sb, pC[:, int(i == 8), :], ACT.Copy).then_inc(ctx_ok, 1)
                    if on["A"] and i == 4:
                        act.wait_ge(rstd_ok, 2 * (s + 1))
                        apart(act)
                        for t in range(QT):
                            ins = act.activation(xn[:, t, :], emb[:, bass.ds(s * QT + t, 1), :].rearrange("p o d -> p (o d)"),
                                                 ACT.Identity, bias=rstd[:, 1, t:t + 1], scale=rstd[:, 0, t:t + 1])
                        ins.then_inc(xn_ok, 1)
                    if on["A"] and i == 9:
                        act.wait_ge(v_ok, s + 1)
                        if rep >= 2:
                            act.wait_ge(pv_ok, (s - 1) * H)
                        act.activation(V[rep % 2][:, :, :, 0:HD], pF[1][:, :].rearrange("p (t h d) -> p t h d", t=QT, h=H),
                                       ACT.Copy).then_inc(v_done, 1)
                    if on["A"] and i == 5:
                        act.wait_ge(xnT_ok, s + 1)
                        act.activation(xT[:, :, :].rearrange("p c t -> p (c t)"), pF[0][:, :], ACT.Copy)\
                            .then_inc(xT_ok, 1)
                    if on["A"] and i == 6:
                        if rep >= 1:
                            act.wait_ge(part2_ok, s)
                            act.wait_ge(qk_out[0], s * 16)
                        for w in range(2):
                            act.wait_ge(qk_ok, s * 2 + w + 1)
                            for m in range(2):
                                mm = 2 * w + m
                                for dst in (qk32[:, mm, :], parts[:, 0, mm, :]):
                                    ins = act.activation(dst, pF[1 - w][:, m * S:(m + 1) * S], ACT.Identity,
                                                         bias=bqk_sb[:, mm:mm + 1], scale=0.25 if w == 0 else 1.0)
                                ins.then_inc(qk32_ok, 1)
                    if on["A"] and i == 8:
                        act.wait_ge(rest_ok, s + 1)
                        if rep >= 1:
                            act.wait_ge(qk_out[1], s * 16)
                        act.activation(parts[:, 1], qkr[:, :, :], ACT.Copy).then_inc(part1_ok, 1)
                    if on["D"] and i == 10:
                        act.wait_ge(cnT_ok, s - 2 + 1)
                        for c in range(KC):
                            ins = act.activation(cT[:, c, :], pF[0][:, c * S:(c + 1) * S], ACT.Identity,
                                                 bias=bv_sb[:, c:c + 1])
                        ins.then_inc(cT_ok, 1)
                    if on["D"] and i == 13:
                        act.wait_ge(rstd2_ok, 2 * (s - 1))
                        due(act, scat_ok[rep % 2], (s - 2 - rep % 2) * (QT * TOPK * 16 // 2))
                        apart(act)
                        for t in range(QT):
                            ins = act.activation(x2[rep % 2][:, t, 0:D],
                                                 emb[:, bass.ds((s - 2) * QT + t, 1), :].rearrange("p o d -> p (o d)"),
                                                 ACT.Identity, bias=rstd2[:, 1, t:t + 1], scale=rstd2[:, 0, t:t + 1])
                        ins.then_inc(x2_ok, 1)
                    if on["D"] and i == 14:
                        act.wait_ge(x2T_ps, s - 2 + 1)
                        act.activation(x2T[:, :, :].rearrange("p c t -> p (c t)"), pF[0][:, :], ACT.Copy)\
                            .then_inc(x2T_ok, 1)
                        act.activation(xT_all[:, :, bass.ds((s - 2) * S, S)],
                                       pF[0][:, :].rearrange("p (c t) -> p c t", c=KC), ACT.Copy)\
                            .then_inc(x2T_ok, 1)
                    if on["D"] and i == 15:
                        act.wait_ge(logit_ok, s - 2 + 1)
                        if rep >= 3:
                            act.wait_ge(sel_ok, s - 2)
                        act.activation(esig[:, :, :].rearrange("p t e -> p (t e)"), pF[1][:, 0:QT * E],
                                       ACT.Exp, scale=-1.0).then_inc(esig_ok, 1)

            act.wait_ge(bias_ok, 1)
            pipeline(act, step)

            def silu(t, par, rep):
                act.wait_ge(tg_ok, t + 1)
                if rep >= 2:
                    act.wait_ge(th_ok, t - 1)
                act.activation(sg_t[par], pT[par][:, 0:P], ACT.Silu).then_inc(ts_ok, 1)

            def weigh(t, j, g, rep):
                act.wait_ge(ty_ok, t + 1)
                act.wait_ge(tw_ok, t + 1)
                if rep >= RING:
                    act.wait_ge(acc_ok[j], g * 16)
                act.activation(y_t[j], pF[j % 2][:, 0:D], ACT.Copy, scale=wt_t[j][:, 0:1]).then_inc(te_ok, 1)

            def turn(g, steady, shared):
                for j in range(RING):
                    silu(g * RING + j, j % 2, RING if steady else j)
                    if j:
                        weigh(g * RING + j - 1, j - 1, g, RING if steady else j - 1)
                    elif steady:
                        weigh(g * RING - 1, RING - 1, g - 1, 2)
                    if shared and j == 3:
                        act.wait_ge(sh_gu, g + 1)
                        due(act, sh_h_ok, g)
                        act.activation(sh_g, pC[:, 0, 0:ISH], ACT.Silu).then_inc(sh_silu, 1)

            turns(act, turn)
            weigh(TILES - 1, RING - 1, TILES // RING - 1, RING)

        @block.vector
        def _(dve):
            setup = Chain(dve, set_v, 1 << 20)

            dve.wait_ge(ids_in, 16)
            setup.link(dve.tensor_copy(idf[:, :], ids_sb[:, :]))
            for i in range(3):
                setup.link(dve.tensor_scalar(ge[:, i, :], idf[:, :], float(TIERS[i]), None, ALU.is_ge))
            setup.link(dve.tensor_scalar(intier[:, 0, :], ge[:, 0, :], -1.0, 1.0, ALU.mult, ALU.add))
            setup.link(dve.tensor_tensor(intier[:, 1, :], ge[:, 0, :], ge[:, 1, :], ALU.subtract))
            setup.link(dve.tensor_tensor(intier[:, 2, :], ge[:, 1, :], ge[:, 2, :], ALU.subtract))
            setup.link(dve.tensor_copy(maxq[:, :], intier[:, 0, :]))
            for i, of in enumerate((intier[:, 1, :], intier[:, 2, :], ge[:, 2, :])):
                setup.link(dve.scalar_tensor_tensor(maxq[:, :], of, MAXQ[i], maxq[:, :], ALU.mult, ALU.add))
            setup.link(dve.tensor_scalar(nmaxq[:, :], maxq[:, :], -1.0, None, ALU.mult))
            dve.memset(cmax[:, :, :], 0.0).then_inc(scan_v, 1)

            scan_links = [1]

            def reduce_chunk(slot, count, parts, rows, tier, links):
                dve.wait_ge(ring_in[slot], count)
                dve.wait_ge(scan_v, links)
                dve.tensor_reduce(cnew[0:parts, :], ring[0:parts, slot, 0:rows, :].rearrange("p n d -> p d n"),
                                  AX_X, ALU.max, apply_absolute_value=True).then_inc(ring_used, 1)
                return cmax[0:parts, tier, :], cnew[0:parts, :]

            def scan_chunk(slot, count, parts, rows, tier, index, links):
                into, new = reduce_chunk(slot, count, parts, rows, tier, links)
                dve.wait_ge(ring_used, index + 1)
                dve.tensor_tensor(into, into, new, ALU.max).then_inc(scan_v, 1)

            rows2 = (TIERS[2] - TIERS[1]) // P // 2
            heads = ((P, rows2, 1), (P, rows2, 1), (T1P, 4, 0), (REST3, 1, 2))
            for k, (parts_, rows, tier) in enumerate(heads):
                scan_chunk(HEAD0 + k, 16, parts_, rows, tier, k, k + 1)

            def turn(i):
                for j in range(SCAN_RING):
                    index = i * SCAN_RING + j + len(heads)
                    scan_chunk(j, (i + (2 if j >= HEAD0 else 1)) * 16, P, SCAN_ROWS, 2, index, index + 1)

            turn(0)
            dve.wait_ge(consts_ok, 1)
            dve.wait_ge(slope_in_s, 16)
            setup.link(dve.tensor_copy(sparts[:, 0:1], slope_in[:, 0:1]))
            setup.link(dve.tensor_tensor(slope_in[:, 1:2], slope_in[:, 0:1], sparts[:, 0:1], ALU.subtract))
            setup.link(dve.tensor_copy(sparts[:, 1:2], slope_in[:, 1:2]))
            setup.link(dve.tensor_tensor(slope_in[:, 2:3], slope_in[:, 1:2], sparts[:, 1:2], ALU.subtract))
            setup.link(dve.tensor_copy(sparts[:, 2:3], slope_in[:, 2:3]))
            for i in range(3):
                last = dve.tensor_scalar(slope_p[:, i, :], onesrow[:, :], sparts[:, i:i + 1], None, ALU.mult)
            last.then_inc(rows_ok, 1)
            dve.tensor_scalar(pos_p[:, 0, :], pos_f[:, :], -1.0, None, ALU.mult)
            dve.tensor_copy(pos_p[:, 1, :], pos_f[:, :])
            dve.tensor_copy(pos_p[:, 2, :], onesrow[:, :]).then_inc(rows_ok, 1)
            dve.wait_ge(w_in_sb, NLOADS * 16)
            dve.tensor_scalar(bqk_sb[:, 0:2], bqk_sb[:, 0:2], 0.25, None, ALU.mult).then_inc(bias_ok, 1)
            with dve.Fori(1, CHUNKS // SCAN_RING) as i:
                turn(i)

            dve.wait_ge(scan_v, CHUNKS + len(heads) + 1)
            setup.link(dve.tensor_tensor(cmax[:, :, :], cmax[:, :, :], tsb[:, 1:4, :], ALU.mult))
            dve.tensor_reduce(pmax[:, 0:3], cmax[:, :, :], AX_X, ALU.max, apply_absolute_value=True)\
               .then_inc(pmax_ok, 1)
            dve.wait_ge(amax_ok, 1)
            setup.link(dve.tensor_scalar(sc3[:, 0:3], amax[:, 0:3], 1e-8, None, ALU.max))
            for i in range(3):
                setup.link(dve.tensor_scalar(sc3[:, i:i + 1], sc3[:, i:i + 1], float(np.float32(1) / np.float32(MAXQ[i])),
                                             None, ALU.mult))
            src = intier[:, 0, :]
            for i, of in enumerate((intier[:, 1, :], intier[:, 2, :], ge[:, 2, :])):
                setup.link(dve.scalar_tensor_tensor(scale[:, :], of, sc3[:, i:i + 1], src, ALU.mult, ALU.add))
                src = scale[:, :]
            setup.link(dve.reciprocal(inv[:, :], scale[:, :]))
            dve.wait_ge(emb_ok, 1)

            ca, cd, cr = (Chain(dve, s_, per) for s_, per in
                          ((chain_a, LINKS_A), (chain_d, LINKS_D), (chain_r, LINKS_R)))

            def token(t, b):
                return bass.ds(b * QT + t, 1)

            def quantise(b, part):
                for t in range(QT):
                    k = token(t, b)
                    if part == 0:
                        ins = dve.tensor_scalar(xq[:, t, :], emb[:, k, :].rearrange("p o d -> p (o d)"), inv[:, k],
                                                ROUND, ALU.mult, ALU.add)
                    elif part == 1:
                        ins = dve.tensor_scalar(xq[:, t, :], xq[:, t, :], -ROUND, maxq[:, k], ALU.add, ALU.min)
                    else:
                        ins = dve.tensor_scalar(xq[:, t, :], xq[:, t, :], nmaxq[:, k], scale[:, k], ALU.max, ALU.mult)
                ca.link(ins)

            def straight_through(b):
                ca.link(dve.tensor_tensor(xq[:, :, :], xq[:, :, :], emb[:, bass.ds(b * QT, QT), :], ALU.subtract))
                for t in range(QT):
                    e1 = emb[:, token(t, b), :].rearrange("p o d -> p (o d)")
                    ins = dve.scalar_tensor_tensor(e1, xq[:, t, :], ge[:, 0, token(t, b)], e1, ALU.mult, ALU.add)
                ca.link(ins)

            def norm_stats(c, b, src, st, m, eps, signal, used):
                apart(dve)
                for t in range(QT):
                    ins = dve.bn_stats(st[:, t, :], src(t))
                c.link(ins)
                apart(dve)
                for t in range(QT):
                    ins = dve.bn_aggr(m[:, t, :], st[:, t, :])
                c.link(ins)
                due(dve, used, 2 * b)
                dve.tensor_scalar(eps[:, 1, :], m[:, :, 0], -1.0, None, ALU.mult)
                dve.tensor_scalar(eps[:, 0, :], m[:, :, 1], EPS, None, ALU.add).then_inc(signal, 1)

            def step(s, rep):
                on = stages(rep)
                par = rep % 2
                for i in range(H):
                    if on["B"]:
                        n = (s - 1) * H + i
                        dve.wait_ge(s_ok, n + 1)
                        if i % MG == 0 and rep >= 2:
                            dve.wait_ge(mT_ok, (s - 2) * NM + i // MG + 1)
                        dve.tensor_reduce(nmax[:, i, :], pS[i % 2][:, :].rearrange("p (t k) -> p t k", t=QT),
                                          AX_X, ALU.max, negate=True).then_inc(max_ok, 1)
                    if on["A"] and i == 0:
                        ca.start(s)
                        quantise(s, 0)
                        quantise(s, 1)
                    if on["A"] and i == 1:
                        quantise(s, 2)
                    if on["A"] and i == 2:
                        straight_through(s)
                    if on["A"] and i == 3:
                        norm_stats(ca, s, lambda t: emb[:, token(t, s), :].rearrange("p o d -> p (o d)"),
                                   stats, mv, mv_eps, var_ok, rstd_ok)
                    if on["D"] and i in (3, 9):
                        d, half_no = s - 2, int(i == 9)
                        if i == 3:
                            cd.start(d)
                        dve.wait_ge(half_ok, 2 * d + half_no + 1)
                        c4 = pF[0][:, :].rearrange("p (t h d) -> p t h d", t=QT, h=H // 2)
                        sums = rsum[:, :, half_no * (H // 2):(half_no + 1) * (H // 2)]
                        cd.link(dve.reciprocal(sums, c4[:, :, :, HD]))
                        if rep - 2 >= 1:
                            dve.wait_ge(cnT_ok, d)
                        dve.tensor_tensor(cn[:, :, half_no * P:(half_no + 1) * P].rearrange("p t (h d) -> p t h d", d=HD),
                                          c4[:, :, :, 0:HD], sums.unsqueeze(3).broadcast_to([P, QT, H // 2, HD]),
                                          ALU.mult).then_inc(cn_ok, 1)
                    if on["R"] and i in (5, 6, 7):
                        (scores, groups, sixth)[i - 5](s - 3)
                    if on["R"] and i == 9:
                        chosen(s - 3)
                    if on["R"] and i == 11:
                        places(s - 3)
                    if on["D"] and i == 11:
                        d = s - 2
                        pair = bass.ds(d * QT, QT)
                        dve.wait_ge(wo_ok, d + 1)
                        dve.wait_ge(embo_ok, d + 1)
                        apart(dve)
                        dve.tensor_tensor(emb[:, pair, :], pF[1][:, :].rearrange("p (t d) -> p t d", t=QT), xo[:, :, :],
                                          ALU.add).then_inc(res_ok, 1)
                        dve.wait_ge(res_ok, d + 1)
                        norm_stats(cd, d, lambda t: emb[:, token(t, d), :].rearrange("p o d -> p (o d)"),
                                   stats2, mv2, mv2_eps, var2_ok, rstd2_ok)
                    if on["R"] and i == 13:
                        slots(s - 3, rep - 3)
                    if on["R"] and i == 14:
                        weights(s - 3, rep - 3)

            def scores(r):
                cr.start(r)
                dve.wait_ge(esig_ok, r + 1)
                cr.link(dve.tensor_scalar(score[:, :, :], esig[:, :, :], 1.0, None, ALU.add))
                cr.link(dve.reciprocal(score[:, :, :], score[:, :, :]))
                cr.link(dve.tensor_tensor(score[:, :, :], score[:, :, :],
                                          gbias_sb[:, :].unsqueeze(1).broadcast_to([P, QT, E]), ALU.add))
                by_group = score[:, :, :].rearrange("p t (g e) -> p (t g) e", g=G)
                cr.link(dve.tensor_reduce(gs[:, :, :].rearrange("p t g -> p (t g)"), by_group, AX_X, ALU.max))

            def groups(r):
                other = gs[:, :, :].unsqueeze(2).broadcast_to([P, QT, G, G])
                own = gs[:, :, :].unsqueeze(3).broadcast_to([P, QT, G, G])
                dve.tensor_tensor(cmp_a[:, :, :, :], other, own, ALU.is_gt)
                cr.link(dve.tensor_tensor(cmp_b[:, :, :, :], other, own, ALU.is_equal))
                cr.link(dve.tensor_tensor(cmp_b[:, :, :, :], cmp_b[:, :, :, :],
                                          lower[:, :, :].unsqueeze(1).broadcast_to([P, QT, G, G]), ALU.mult))
                cr.link(dve.tensor_tensor(cmp_a[:, :, :, :], cmp_a[:, :, :, :], cmp_b[:, :, :, :], ALU.add))
                cr.link(dve.tensor_reduce(gmask[:, :, :], cmp_a[:, :, :, :], AX_X, ALU.add))
                cr.link(dve.tensor_scalar(gmask[:, :, :], gmask[:, :, :], float(TG), None, ALU.is_lt))
                cr.link(dve.tensor_tensor(ms[:, :, :].rearrange("p t (g e) -> p t g e", g=G),
                                          score[:, :, :].rearrange("p t (g e) -> p t g e", g=G),
                                          gmask[:, :, :].unsqueeze(3).broadcast_to([P, QT, G, E // G]), ALU.mult))
                cr.link(dve.tensor_scalar(ms[:, :, :], ms[:, :, :], 0.0, None, ALU.add))

            def sixth(r):
                apart(dve)
                for t in range(QT):
                    ins = dve.max(top[:, t, :], ms[:, t, :])
                cr.link(ins)
                apart(dve)
                for t in range(QT):
                    ins = dve.max_index(topi[:, t, :], top[:, t, :], ms[:, t, :])
                cr.link(ins)
                dve.tensor_reduce(wsum[:, :], top[:, :, 0:TOPK], AX_X, ALU.add)
                cr.link(dve.tensor_copy(lastf[:, :], topi[:, :, TOPK - 1]))
                cr.link(dve.tensor_scalar(wsum[:, :], wsum[:, :], 1e-8, None, ALU.add))
                cr.link(dve.reciprocal(wsum[:, :], wsum[:, :]))

            def chosen(r):
                due(dve, prefix_ok, r)
                for t in range(QT):
                    ins = dve.tensor_scalar(tie[:, t, :], eidx[:, :], lastf[:, t:t + 1], None, ALU.is_le)
                cr.link(ins)
                for t in range(QT):
                    ins = dve.scalar_tensor_tensor(tie[:, t, :], ms[:, t, :], top[:, t, TOPK - 1:TOPK], tie[:, t, :],
                                                   ALU.is_equal, ALU.mult)
                cr.link(ins)
                for t in range(QT):
                    ins = dve.scalar_tensor_tensor(M[:, t, :], ms[:, t, :], top[:, t, TOPK - 1:TOPK], tie[:, t, :],
                                                   ALU.is_gt, ALU.add)
                ins.then_inc(sel_ok, 1)
                dve.wait_ge(sel_ok, r + 1)
                for t in range(QT):
                    ins = dve.scalar_tensor_tensor(wn[:, t, :], ms[:, t, :], wsum[:, t:t + 1], M[:, t, :],
                                                   ALU.mult, ALU.mult)
                cr.link(ins)

            def places(r):
                dve.wait_ge(prefix_ok, r + 1)
                pre = pF[0][:, 0:3 * E].rearrange("p (x e) -> p x e", x=3)
                cr.link(dve.tensor_tensor(key[:, :, :], pre[:, 0:QT, :], run[:, :].unsqueeze(1)
                                          .broadcast_to([P, QT, E]), ALU.add))
                dve.tensor_tensor(run[:, :], run[:, :], pre[:, QT, :], ALU.add).then_inc(prefix_used, 1)

            def slots(r, rep):
                cr.link(dve.tensor_tensor(key[:, :, :], key[:, :, :], ebase[:, :].unsqueeze(1)
                                          .broadcast_to([P, QT, E]), ALU.add))
                cr.link(dve.tensor_tensor(key[:, :, :], key[:, :, :], M[:, :, :], ALU.mult))
                apart(dve)
                for t in range(QT):
                    ins = dve.max(topk[:, t, :], key[:, t, :])
                cr.link(ins)

            def weights(r, rep):
                par = rep % 2
                due(dve, scat_ok[par], (r - par) * (QT * TOPK * 16 // 2))
                for t in range(QT):
                    for k in range(TOPK):
                        dve.scalar_tensor_tensor(eq[:, t, k, :], key[:, t, :], topk[:, t, k:k + 1], wn[:, t, :],
                                                 ALU.is_equal, ALU.mult, accum_out=x2[par][:, t, WCOL + k:WCOL + k + 1])
                dve.tensor_copy(x2[par][:, :, SLOTCOL:SLOTCOL + TOPK], topk[:, :, 0:TOPK])
                dve.tensor_copy(x2[par][:, :, TOKCOL:TOKCOL + 1].bitcast(I32),
                                tok_u[:, bass.ds(r * QT, QT)].unsqueeze(2))
                dve.tensor_scalar(slot_u[par][:, :, :], topk[:, :, 0:TOPK], -1.0, None, ALU.add).then_inc(slots_ok, 1)

            pipeline(dve, step)

            tab = Chain(dve, chain_t, 1 << 20)
            dve.wait_ge(prefix_used, B)
            tab.link(dve.tensor_scalar(nt_e[:, :], run[:, :], 127.0, 1.0 / 128.0, ALU.add, ALU.mult))
            tab.link(dve.tensor_scalar(nt_e[:, :], nt_e[:, :], -127.0 / 256.0, ROUND, ALU.add, ALU.add))
            tab.link(dve.tensor_scalar(nt_e[:, :], nt_e[:, :], -ROUND, None, ALU.add))
            tab.link(dve.tensor_tensor_scan(end_e[:, :], one_e[:, :], nt_e[:, :], 0.0, ALU.mult, ALU.add))
            tab.link(dve.tensor_tensor(start_e[:, :], end_e[:, :], nt_e[:, :], ALU.subtract))
            tile_no = part_f[:, 0:2]

            def by_tile(x):
                return x.unsqueeze(1).broadcast_to([P, 2, E])

            of_tile = tile_no.unsqueeze(2).broadcast_to([P, 2, E])
            dve.tensor_tensor(own[:, :, :], by_tile(start_e[:, :]), of_tile, ALU.is_le)
            tab.link(dve.tensor_tensor(ended[:, :, :], by_tile(end_e[:, :]), of_tile, ALU.is_le))
            dve.tensor_reduce(tinfo[:, 0, :], ended[:, :, :], AX_X, ALU.add)
            tab.link(dve.tensor_tensor(own[:, :, :], own[:, :, :], ended[:, :, :], ALU.subtract))
            dve.tensor_tensor(ended[:, :, :], ended[:, :, :], by_tile(nt_e[:, :]), ALU.mult)
            tab.link(dve.tensor_tensor(own[:, :, :], own[:, :, :], by_tile(run[:, :]), ALU.mult))
            dve.tensor_reduce(tinfo[:, 1, :], ended[:, :, :], AX_X, ALU.add)
            tab.link(dve.tensor_reduce(tinfo[:, 2, :], own[:, :, :], AX_X, ALU.add))
            dve.tensor_scalar(tinfo[:, 3, :], tinfo[:, 0, :], float(E - 1), float(CAP), ALU.min, ALU.mult)
            tab.link(dve.tensor_tensor(tinfo[:, 4, :], tile_no, tinfo[:, 1, :], ALU.subtract))
            dve.tensor_scalar(tinfo[:, 5, :], tinfo[:, 2, :], float(-P), None, ALU.add)
            tab.link(dve.tensor_scalar(tinfo[:, 4, :], tinfo[:, 4, :], float(P), None, ALU.mult))
            tab.link(dve.tensor_tensor(tinfo[:, START, :], tinfo[:, 4, :], tinfo[:, 5, :], ALU.min))
            for k, of in ((START, START), (START + 1, 4)):
                ins = dve.scalar_tensor_tensor(tinfo[:, k, :], tinfo[:, of, :], float(P), tinfo[:, 3, :], ALU.add, ALU.add)
            ins.then_inc(tinfo_ok, 1)
            dve.wait_ge(tinfo_in, 48)
            dve.tensor_copy(treg[:, :], treg_f[:, :]).then_inc(treg_ok, 1)
            tab.link(dve.tensor_scalar(tslot[:, :], tslot[:, :], part_f[:, 2:3], None, ALU.add))
            tab.link(dve.tensor_tensor(tfirst[:, :], tslot[:, :], tfirst[:, :], ALU.is_gt))
            dve.tensor_tensor(tslot[:, :], tslot[:, :], tfirst[:, :], ALU.mult).then_inc(tslot_ok, 1)

            def copy_x(t, j, g, rep):
                dve.wait_ge(tT_ok, t + 1)
                if rep >= 2:
                    dve.wait_ge(tg_ok, t - 1)
                dve.tensor_copy(xT_t[j % 2], pS[j % 2][:, 0:KC * P]).then_inc(tx_ok, 1)
                if rep >= RING:
                    dve.wait_ge(te_ok, t - RING + 1)
                dve.scalar_tensor_tensor(eq_t[j][:, 0:TOPK], x_t[j][:, SLOTCOL:SLOTCOL + TOPK], tslot[:, bass.ds(t, 1)],
                                         x_t[j][:, WCOL:WCOL + TOPK], ALU.is_equal, ALU.mult,
                                         accum_out=wt_t[j][:, 0:1]).then_inc(tw_ok, 1)

            def gate_up(t, j, rep):
                dve.wait_ge(ts_ok, t + 1)
                if rep >= 2:
                    dve.wait_ge(ty_ok, t - 1)
                dve.tensor_tensor(h_t[j % 2], sg_t[j % 2], pT[j % 2][:, P:2 * P], ALU.mult).then_inc(th_ok, 1)

            dve.wait_ge(tslot_ok, 1)

            def turn(g, steady, shared):
                for j in range(RING):
                    copy_x(g * RING + j, j, g, RING if steady else j)
                    if j or steady:
                        gate_up(g * RING + j - 1, (j - 1) % RING, RING if steady else j - 1)
                    if shared and j == 4:
                        dve.wait_ge(sh_silu, g + 1)
                        due(dve, sh_y, g)
                        dve.tensor_tensor(sh_h[:, :, :].rearrange("p m t -> p (m t)"), sh_g, pC[:, 0, ISH:2 * ISH],
                                          ALU.mult).then_inc(sh_h_ok, 1)
                    if shared and j == 7:
                        dve.wait_ge(sh_y, g + 1)
                        own_rows = emb[:, bass.ds(g, 1), :].rearrange("p o d -> p (o d)")
                        dve.tensor_tensor(own_rows, pC[:, 1, 0:D], own_rows, ALU.add).then_inc(sh_done, 1)

            turns(dve, turn)
            gate_up(TILES - 1, RING - 1, RING)
            dve.wait_ge(sh_done, NT)

            for n in range(NT // FG):
                dve.wait_ge(fin_in[n % FBUF], (n // FBUF + 1) * NACC * 16)
                tiles = emb[:, n * FG:(n + 1) * FG, :]
                for a in range(NACC):
                    ins = dve.tensor_tensor(tiles, tiles, fin[n % FBUF][:, a], ALU.add)
                    if a < NACC - 1:
                        ins.then_inc(fin_v, 1)
                        dve.wait_ge(fin_v, n * (NACC - 1) + a + 1)
                    else:
                        ins.then_inc(fin_ok, 1)

        @block.tensor
        def _(pe):
            def transpose2(src, dst, rows):
                for t in range(QT):
                    for c in range(KC):
                        ins = pe.transpose(dst[:, c * S + t * P:c * S + (t + 1) * P], src(t)[:, c * P:(c + 1) * P],
                                           ident[:, :])
                return ins

            def step(s, rep):
                on = stages(rep)
                par = rep % 2
                for i in range(H):
                    if on["B"]:
                        b = s - 1
                        bpar = (rep - 1) % 2
                        if i == 0:
                            pe.wait_ge(qk_in, (b + 1) * 192)
                            if rep == 1:
                                pe.wait_ge(rows_in, 18 * 16)
                        n = b * H + i
                        if rep > 1 or i >= 2:
                            pe.wait_ge(max_ok, n - 1)
                        for t in range(QT):
                            ins = pe.matmul(pS[i % 2][:, t * S:(t + 1) * S], Qs[bpar][0:ROWS_B, i, t * P:(t + 1) * P],
                                            Ks[bpar][0:ROWS_B, i, :], start=True, stop=True)
                        ins.then_inc(s_ok, 1)
                    if mg := m_group(s, rep, i):
                        b, g = mg
                        n = b * NM + g
                        pe.wait_ge(max_ok, (n + 1) * MG)
                        if rep - (1 if i else 2) > 0 or g >= 1:
                            pe.wait_ge(mrows_ok, n)
                        if g == 0 and rep == 1:
                            pe.wait_ge(v_done, 1)
                        if g == 1:
                            if on["A"]:
                                pe.wait_ge(qk32_ok, s * 4 + 4)
                            else:
                                pe.wait_ge(cn_ok, (s - 2) * 2 + 1)
                        if g == 2:
                            if on["R"]:
                                pe.wait_ge(prefix_used, s - 2)
                            elif on["D"]:
                                pe.wait_ge(cT_ok, s - 1)
                        if g == 3:
                            if rep >= 3:
                                pe.wait_ge(esig_ok, s - 2)
                            else:
                                pe.wait_ge(v_done, 2)
                        pe.transpose(pF[MBANK[g]][0:MG * QT, 0:P],
                                     nmax[:, g * MG:(g + 1) * MG, :].rearrange("p h t -> p (h t)"), ident[:, :])\
                          .then_inc(mT_ok, 1)
                    if head := c_head(s, rep, i):
                        b, h = head
                        crep = rep - (1 if i >= LAG else 2)
                        cpar = crep % 2
                        n = b * H + h
                        if h % MG == 0:
                            pe.wait_ge(max_in[h // MG], (b + 1) * 16)
                        if crep > 0 or h >= 2:
                            pe.wait_ge(exp_ok, n - 1)
                        for kt in range(QT):
                            ins = pe.matmul(pT[h % 2][:, kt * S:(kt + 1) * S], Ks[cpar][0:ROWS_C, h, kt * P:(kt + 1) * P],
                                            Qs[cpar][0:ROWS_C, h, :], start=True, stop=True)
                        ins.then_inc(sT_ok, 1)
                    back = c_head(s, rep, i - 1) if i else None
                    if i == 0 and rep >= 1:
                        back = c_head(s - 1, rep - 1, H - 1)
                    if back:
                        b, h = back
                        brep = rep - (1 if i - 1 >= LAG else 2) if i else rep - 1 - 1
                        vpar = brep % 2
                        n = b * H + h
                        pe.wait_ge(exp_ok, n + 1)
                        if h == 0:
                            pe.wait_ge(v_done, b + 1)
                        if h % (H // 2) == 0 and brep > 0:
                            pe.wait_ge(ctx_ok, 2 * b - (1 if h == 0 else 0))
                        rows = slice(h % 4 * VW, (h % 4 + 1) * VW)
                        cols = slice(h // 4 % 2 * S, (h // 4 % 2 + 1) * S)
                        for kt in range(QT):
                            ins = pe.matmul(pC[rows, h // 8, cols], V[vpar][:, kt, h, :], PT[h % 2][:, kt, :],
                                            start=(kt == 0), stop=(kt == QT - 1))
                        ins.then_inc(pv_ok, 1)
                    if on["D"] and i in (2, 9):
                        d = s - 2
                        pe.wait_ge(ctx_ok, 2 * d + (1 if i == 2 else 2))
                        if i == 2 and rep > 2:
                            pe.wait_ge(x2T_ok, (s - 2) * 2)
                        elif i == 2:
                            pe.wait_ge(mrows_ok, 3)
                        elif on["B"]:
                            pe.wait_ge(mrows_ok, (s - 1) * NM + 2)
                        else:
                            pe.wait_ge(cn_ok, 2 * d + 1)
                        for t in range(QT):
                            for c in range(2):
                                ins = pe.transpose(pF[0][:, (2 * t + c) * P:(2 * t + c + 1) * P],
                                                   ctx_sb[:, c * S + t * P:c * S + (t + 1) * P], ident[:, :])
                        ins.then_inc(half_ok, 1)
                    if on["A"] and i == 5:
                        pe.wait_ge(xn_ok, s + 1)
                        if on["D"]:
                            pe.wait_ge(cn_ok, (s - 2) * 2 + 1)
                        elif rep == 1:
                            pe.wait_ge(qk32_ok, 4)
                        if rep == 0:
                            pe.wait_ge(consts_ok, 1)
                        transpose2(lambda t: xn[:, t, :], pF[0], P).then_inc(xnT_ok, 1)
                    if on["A"] and i == 6:
                        if rep == 0:
                            pe.wait_ge(w_in_sb, NLOADS * 16)
                        pe.wait_ge(xT_ok, s + 1)
                        if rep >= 1:
                            pe.wait_ge(mrows_ok, (s - 1) * NM + 1)
                        for w in range(2):
                            for m in range(2):
                                for c in range(KC):
                                    ins = pe.matmul(pF[1 - w][:, m * S:(m + 1) * S],
                                                    wqk_sb[:, c, w * D + m * P:w * D + (m + 1) * P], xT[:, c, :],
                                                    start=(c == 0), stop=(c == KC - 1))
                            ins.then_inc(qk_ok, 1)
                    if on["A"] and i == 8:
                        pe.wait_ge(qk32_ok, s * 4 + 2)
                        for t in range(QT):
                            for c in range(KC):
                                ins = pe.matmul(pF[1][:, t * D:(t + 1) * D], xT[:, c, t * P:(t + 1) * P],
                                                wv_sb[:, c, :], start=(c == 0), stop=(c == KC - 1))
                        ins.then_inc(v_ok, 1)
                    if on["D"] and i == 10:
                        pe.wait_ge(cn_ok, (s - 2) * 2 + 2)
                        transpose2(lambda t: cn[:, t, :], pF[0], P).then_inc(cnT_ok, 1)
                    if on["D"] and i == 11:
                        d = s - 2
                        pe.wait_ge(cT_ok, d + 1)
                        if on["A"]:
                            pe.wait_ge(v_done, s + 1)
                        elif on["B"]:
                            pe.wait_ge(mrows_ok, (s - 1) * NM + 1)
                        else:
                            pe.wait_ge(mrows_ok, B * NM)
                        for t in range(QT):
                            for c in range(KC):
                                ins = pe.matmul(pF[1][:, t * D:(t + 1) * D], cT[:, c, t * P:(t + 1) * P],
                                                wo_sb[:, c, :], start=(c == 0), stop=(c == KC - 1))
                        ins.then_inc(wo_ok, 1)
                    if on["R"] and i == 11:
                        r = s - 3
                        pe.wait_ge(sel_ok, r + 1)
                        if on["D"]:
                            pe.wait_ge(cT_ok, s - 1)
                        else:
                            pe.wait_ge(x2T_ok, (s - 2) * 2)
                        pre = pF[0][:, 0:3 * E]
                        pe.matmul(pre[:, 0:E], before[:, :], M[:, 0, :], start=True, stop=True)
                        pe.matmul(pre[:, E:2 * E], before[:, :], M[:, 1, :], start=True, stop=False)
                        pe.matmul(pre[:, E:2 * E], ones[:, :], M[:, 0, :], start=False, stop=True)
                        pe.matmul(pre[:, 2 * E:3 * E], ones[:, :], M[:, 0, :], start=True, stop=False)
                        pe.matmul(pre[:, 2 * E:3 * E], ones[:, :], M[:, 1, :], start=False, stop=True)\
                          .then_inc(prefix_ok, 1)
                    if on["D"] and i == 14:
                        pe.wait_ge(x2_ok, s - 2 + 1)
                        if on["B"]:
                            pe.wait_ge(mrows_ok, (s - 1) * NM + 3)
                        else:
                            pe.wait_ge(prefix_used, s - 2)
                        transpose2(lambda t: x2[par][:, t, :], pF[0], P).then_inc(x2T_ps, 1)
                    if on["D"] and i == 15:
                        pe.wait_ge(x2T_ok, (s - 2) * 2 + 1)
                        for t in range(QT):
                            for c in range(KC):
                                ins = pe.matmul(pF[1][:, t * E:(t + 1) * E], x2T[:, c, t * P:(t + 1) * P],
                                                gate_sb[:, c, :], start=(c == 0), stop=(c == KC - 1))
                        ins.then_inc(logit_ok, 1)

            pipeline(pe, step)
            def rows_t(t, j, g, rep):
                pe.wait_ge(x_in[j], (g + 1) * 16)
                if rep >= 2:
                    pe.wait_ge(tx_ok, t - 1)
                for c in range(KC):
                    ins = pe.transpose(pS[j % 2][:, c * P:(c + 1) * P], x_t[j][:, c * P:(c + 1) * P], ident[:, :])
                ins.then_inc(tT_ok, 1)

            def gate_up(t, j, g, rep):
                pe.wait_ge(w_in[j], (g + 1) * 16)
                pe.wait_ge(tx_ok, t + 1)
                if rep >= 2:
                    pe.wait_ge(th_ok, t - 1)
                for w in range(2):
                    for c in range(KC):
                        ins = pe.matmul(pT[j % 2][:, w * P:(w + 1) * P], w_t[j][:, c * 2 * P + w * P:c * 2 * P + (w + 1) * P],
                                        xT_t[j % 2][:, c * P:(c + 1) * P], start=(c == 0), stop=(c == KC - 1))
                ins.then_inc(tg_ok, 1)

            def down(t, j, rep):
                pe.wait_ge(th_ok, t + 1)
                if rep >= 2:
                    pe.wait_ge(te_ok, t - 1)
                pe.matmul(pF[j % 2][:, 0:D], h_t[j % 2], w_t[j][:, 2 * D:3 * D], start=True, stop=True)\
                  .then_inc(ty_ok, 1)

            def shared_gate_up(n):
                due(pe, sh_h_ok, n)
                for k in range(2 * ISH // P):
                    for c in range(KC):
                        ins = pe.matmul(pC[:, 0, k * P:(k + 1) * P], sgu_sb[:, c, k * P:(k + 1) * P],
                                        xT_all[:, c, bass.ds(n * P, P)], start=(c == 0), stop=(c == KC - 1))
                ins.then_inc(sh_gu, 1)

            def shared_down(n):
                pe.wait_ge(sh_h_ok, n + 1)
                due(pe, sh_done, n)
                for m in range(ISH // P):
                    ins = pe.matmul(pC[:, 1, 0:D], sh_h[:, m, :], sdown_sb[:, m, :],
                                    start=(m == 0), stop=(m == ISH // P - 1))
                ins.then_inc(sh_y, 1)

            def turn(g, steady, shared):
                for j in range(RING):
                    rows_t(g * RING + j, j, g, RING if steady else j)
                    if steady or j >= 1:
                        gate_up(g * RING + j - 1, (j - 1) % RING, g if j else g - 1, RING if steady else j - 1)
                    if steady or j >= 2:
                        down(g * RING + j - 2, (j - 2) % RING, RING if steady else j - 2)
                    if shared and j == 2:
                        shared_gate_up(g)
                    if shared and j == 5:
                        shared_down(g)

            pe.wait_ge(x2T_ok, B * 2)
            pe.wait_ge(esig_ok, B)
            pe.wait_ge(exp_ok, B * H)
            pe.wait_ge(prefix_used, B)
            pe.wait_ge(sh_w_in, 32)
            turns(pe, turn)
            gate_up(TILES - 1, RING - 1, TILES // RING - 1, RING)
            down(TILES - 2, RING - 2, RING)
            down(TILES - 1, RING - 1, RING)


def kernel(**inputs):
    import concourse.bacc as _bacc
    from concourse.bass_utils import run_bass_kernel_spmd as _run

    a = {n: np.asarray(v) for n, v in inputs.items()}

    def chunks(m):
        return np.ascontiguousarray(m.reshape(-1, P, m.shape[1]).transpose(1, 0, 2))

    f = "L0_ffn_"
    t = "L0_attn_"
    experts = np.empty((E, P, 3 * D), np.float32)
    for c in range(KC):
        experts[:, :, c * D:c * D + P] = a[f + "eg_w"][:, :, c * P:(c + 1) * P].transpose(0, 2, 1)
        experts[:, :, c * D + P:(c + 1) * D] = a[f + "eu_w"][:, :, c * P:(c + 1) * P].transpose(0, 2, 1)
    experts[:, :, 2 * D:] = a[f + "ed_w"].transpose(0, 2, 1)
    arrays = {
        "ids": np.ascontiguousarray(a["x"].reshape(NT, P).T),
        "table": np.concatenate([a[f"L0_tok_tw{i}"] for i in range(4)]),
        "ts": np.concatenate([a[f"L0_tok_ts{i}"] for i in range(4)]),
        "wqk": chunks(np.concatenate([a[t + "Wq"].T, a[t + "Wk"].T], axis=1)),
        "wv": chunks(a[t + "Wv"].T),
        "wo": chunks(a[t + "Wo"].T),
        "bqk": np.ascontiguousarray(np.concatenate([a[t + "bq"], a[t + "bk"]]).reshape(4, P).T),
        "bv": np.ascontiguousarray(a[t + "bv"].reshape(KC, P).T),
        "bo": a[t + "bo"].reshape(1, D),
        "slopes": a[t + "slopes"].reshape(H, 1),
        "gate": chunks(a[f + "gate_w"].T),
        "gbias": a[f + "gate_bias"].reshape(1, E),
        "experts": experts.reshape(E * P, 3 * D),
        "sgu": chunks(np.concatenate([a[f + "sg_w"].T, a[f + "su_w"].T], axis=1)),
        "sdown": chunks(a[f + "sd_w"].T),
    }
    nc = _bacc.Bacc("TRN2", target_bir_lowering=False, num_devices=1)
    args = [nc.dram_tensor(f"in_{n}", v.shape, mybir.dt.from_np(v.dtype), kind="ExternalInput").ap()
            for n, v in arrays.items()]
    out = nc.dram_tensor("out_dram", (T, D), F32, kind="ExternalOutput").ap()
    tower(nc, *args, out)
    r = _run(nc, [{f"in_{n}": v for n, v in arrays.items()}], core_ids=[0])
    return r.results[0]["out_dram"].reshape(B, S, D)
```
